# Optimizing a Trainium2 kernel written in Bass

```python
import numpy as np
import jax
import jax.numpy as jnp

def _softmax(x, axis=-1):
    return jax.nn.softmax(x, axis=axis)

def _gelu(x):
    return jax.nn.gelu(x, approximate=True)

def _silu(x):
    return jax.nn.silu(x)

def _sigmoid(x):
    return jax.nn.sigmoid(x)

def _layernorm(x, axis=-1, eps=1e-05):
    m = jnp.mean(x, axis=axis, keepdims=True)
    v = jnp.var(x, axis=axis, keepdims=True)
    return (x - m) / jnp.sqrt(v + eps)

def _scatter_add(tgt, idx, src, axis=0):
    return tgt.at[idx].add(src)

def _segment_sum(src, seg, n):
    return jax.ops.segment_sum(src, seg, n)
kernel_name = 'mk_decoder_postln_d2_seqx_r8_6d6498'

def setup_inputs(seed: int=0):
    np.random.seed(seed)
    _w = jnp.asarray

    def _rec_inputs():
        import jax
        import jax.numpy as jnp
        _rk = jax.random.key(seed)
        x = -0.0002928 + 1 * jax.random.normal(jax.random.fold_in(_rk, 1), (8, 256, 256), jnp.float32)
        _lenS = 256 - jax.random.randint(jax.random.fold_in(_rk, 7), (8,), 0, max(1, 256 // 4) + 1, jnp.int32)
        _lenS2 = 1601 - jax.random.randint(jax.random.fold_in(_rk, 8), (8,), 0, max(1, 1601 // 4) + 1, jnp.int32)
        _ctx_2048P = jax.random.normal(jax.random.fold_in(_rk, 11), (8, 16, 256), jnp.float32)
        _ctx_2048c = jax.random.dirichlet(jax.random.fold_in(_rk, 511), 0.3 * jnp.ones((16,), jnp.float32), (8, 1601))
        _ctx_2048t = jnp.einsum('bsk,bkd->bsd', _ctx_2048c, _ctx_2048P)
        _ctx_2048t = _ctx_2048t * jax.lax.rsqrt(jnp.mean(jnp.square(_ctx_2048t)) + 1e-12) * 0.953939
        ctx_2048 = 4.13588e-05 + 0.999923 * (_ctx_2048t + 0.3 * jax.random.normal(jax.random.fold_in(_rk, 611), (8, 1601, 256), jnp.float32))
        _validS = jnp.arange(256)[None, :] < _lenS[:, None]
        _validS2 = jnp.arange(1601)[None, :] < _lenS2[:, None]
        _causal = jnp.tril(jnp.ones((256, 256), dtype=bool))
        mask_1xSxS2_ff0 = jnp.where(jnp.ones((1, 256, 1601), dtype=bool), 0.0, -1000000000.0).astype(jnp.float32)
        mask_BxS2_bk0 = jnp.logical_not(jnp.broadcast_to(_validS2[:, :], (8, 1601)))
        return (x, ctx_2048, mask_1xSxS2_ff0, mask_BxS2_bk0)
    x, ctx_2048, mask_1xSxS2_ff0, mask_BxS2_bk0 = _rec_inputs()

    def _L0_attn_setup():
        import jax, jax.numpy as jnp
        import numpy as np
        from jax import lax
        B, N, D = (4, 512, 256)
        E = 128
        H = D // E
        CHUNK = 64
        EPS = 1e-06

        def rmsnorm(x, w):
            var = jnp.mean(jnp.square(x), axis=-1, keepdims=True)
            return x * lax.rsqrt(var + EPS) * w

        def chunked_gla(q, v, log_f):
            b, n, h, e = q.shape
            nc = n // CHUNK
            k = 1.0 - jnp.exp(log_f)

            def to_chunks(t):
                return t.reshape(b, nc, CHUNK, h, e).transpose(1, 0, 2, 3, 4)
            qs, ks_, vs, lfs = map(to_chunks, (q, k, v, log_f))
            A = jnp.cumsum(lfs, axis=2)
            mask = jnp.tril(jnp.ones((CHUNK, CHUNK), dtype=bool))

            def step(S, xs):
                qc, kc, vc, Ac = xs
                q_dec = qc * jnp.exp(Ac)
                k_dec = kc * jnp.exp(-Ac)
                scores = jnp.einsum('bthe,bshe->bhts', q_dec, k_dec)
                scores = jnp.where(mask[None, None], scores, 0.0)
                o_intra = jnp.einsum('bhts,bshe->bthe', scores, vc)
                o_inter = jnp.einsum('bthe,bhef->bthf', q_dec, S)
                A_last = Ac[:, -1]
                k_rem = kc * jnp.exp(A_last[:, None] - Ac)
                S_new = jnp.exp(A_last)[..., None] * S + jnp.einsum('bthe,bthf->bhef', k_rem, vc)
                return (S_new, o_intra + o_inter)
            S0 = jnp.zeros((b, h, e, e), dtype=q.dtype)
            _, o = lax.scan(step, S0, (qs, ks_, vs, A))
            return o.transpose(1, 0, 2, 3, 4).reshape(b, n, h, e)
        key = jax.random.key(seed)
        ks = jax.random.split(key, 6)
        std = 0.02
        x = jax.random.normal(ks[0], (B, N, D), dtype=jnp.float32)
        Wq = jax.random.normal(ks[1], (D, D), dtype=jnp.float32) * std
        Wk = jax.random.normal(ks[2], (D, D), dtype=jnp.float32) * std
        Wv = jax.random.normal(ks[3], (D, D), dtype=jnp.float32) * std
        Wo = jax.random.normal(ks[4], (D, D), dtype=jnp.float32) * std
        norm_w = jnp.ones((D,), dtype=jnp.float32)
        return {'x': x, 'Wq': Wq, 'Wk': Wk, 'Wv': Wv, 'Wo': Wo, 'norm_w': norm_w}
    _L0_attn_all = _L0_attn_setup()
    _L0_attn_in = {k: v for k, v in _L0_attn_all.items() if k in ('Wq', 'Wk', 'Wv', 'Wo', 'norm_w')}
    del _L0_attn_all

    def _L0_xattn_setup():
        import jax, jax.numpy as jnp
        import numpy as np
        H = 256
        NH = 16
        NKV = 4
        HD = 128
        GROUPS = NH // NKV
        EPS = 1e-06
        B, S, SE = (1, 256, 512)

        def _rmsnorm(x, w, eps=EPS):
            xf = x.astype(jnp.float32)
            var = jnp.mean(xf * xf, axis=-1, keepdims=True)
            return (xf * jax.lax.rsqrt(var + eps)).astype(x.dtype) * w
        key = jax.random.key(seed)
        ks = jax.random.split(key, 12)
        sc = 0.02
        return {'hidden_states': jax.random.normal(ks[0], (B, S, H), jnp.float32), 'encoder_hidden_states': jax.random.normal(ks[1], (B, SE, H), jnp.float32), 'attention_mask': jnp.zeros((B, S, SE), jnp.float32), 'Wq': jax.random.normal(ks[2], (H, NH * HD), jnp.float32) * sc, 'bq': jax.random.normal(ks[3], (NH * HD,), jnp.float32) * sc, 'Wk': jax.random.normal(ks[4], (H, NKV * HD), jnp.float32) * sc, 'bk': jax.random.normal(ks[5], (NKV * HD,), jnp.float32) * sc, 'Wv': jax.random.normal(ks[6], (H, NKV * HD), jnp.float32) * sc, 'bv': jax.random.normal(ks[7], (NKV * HD,), jnp.float32) * sc, 'Wo': jax.random.normal(ks[8], (NH * HD, H), jnp.float32) * sc, 'qn_w': jnp.ones((HD,), jnp.float32), 'kn_w': jnp.ones((HD,), jnp.float32)}
    _L0_xattn_all = _L0_xattn_setup()
    _L0_xattn_in = {k: v for k, v in _L0_xattn_all.items() if k in ('Wq', 'bq', 'Wk', 'bk', 'Wv', 'bv', 'Wo', 'qn_w', 'kn_w')}
    del _L0_xattn_all

    def _L0_ffn_setup():
        import jax, jax.numpy as jnp
        import numpy as np
        TOP_K = 8
        NUM_GROUPS = 8
        key = jax.random.key(seed)
        ks = jax.random.split(key, 6)
        T_B, T_S, H, I, E, G = (1, 256, 256, 96, 32, NUM_GROUPS)
        hidden_states = jax.random.normal(ks[0], (T_B, T_S, H), dtype=jnp.float32)
        gate_weight = jax.random.normal(ks[1], (E, H), dtype=jnp.float32) * 0.02
        gate_up_proj = jax.random.normal(ks[2], (E, 2 * I, H), dtype=jnp.float32) * 0.02
        down_proj = jax.random.normal(ks[3], (E, H, I), dtype=jnp.float32) * 0.02
        merge_groups = jax.random.randint(ks[4], (E,), 0, G, dtype=jnp.int64)
        merge_groups = merge_groups.at[:G].set(jnp.arange(G, dtype=jnp.int64))
        dominant_experts = jax.random.randint(ks[5], (G,), 0, E, dtype=jnp.int64)
        return {'hidden_states': hidden_states, 'gate_weight': gate_weight, 'gate_up_proj': gate_up_proj, 'down_proj': down_proj, 'merge_groups': merge_groups, 'dominant_experts': dominant_experts}
    _L0_ffn_all = _L0_ffn_setup()
    _L0_ffn_in = {k: v for k, v in _L0_ffn_all.items() if k in ('gate_weight', 'gate_up_proj', 'down_proj', 'merge_groups', 'dominant_experts')}
    del _L0_ffn_all

    def _L1_attn_setup():
        import jax, jax.numpy as jnp
        import numpy as np
        HIDDEN = 256
        NUM_HEADS = 32
        HEAD_DIM = 64
        NUM_KV = 8
        GROUP = NUM_HEADS // NUM_KV
        SCALE = HEAD_DIM ** (-0.5)
        ROPE_BASE = 10000.0

        def apply_rope(t):
            S, D = (t.shape[-2], t.shape[-1])
            inv_freq = 1.0 / ROPE_BASE ** (jnp.arange(0, D, 2, dtype=jnp.float32) / D)
            ang = jnp.arange(S, dtype=jnp.float32)[:, None] * inv_freq[None, :]
            cos, sin = (jnp.cos(ang), jnp.sin(ang))
            x1, x2 = (t[..., :D // 2], t[..., D // 2:])
            return jnp.concatenate([x1 * cos - x2 * sin, x2 * cos + x1 * sin], axis=-1)
        key = jax.random.key(seed)
        ks = jax.random.split(key, 10)
        B, S = (2, 256)
        s_in = HIDDEN ** (-0.5)
        s_o = (NUM_HEADS * HEAD_DIM) ** (-0.5)
        return {'x': jax.random.normal(ks[0], (B, S, HIDDEN), jnp.float32), 'Wq': jax.random.normal(ks[1], (NUM_HEADS * HEAD_DIM, HIDDEN), jnp.float32) * s_in, 'bq': jnp.zeros((NUM_HEADS * HEAD_DIM,), jnp.float32), 'Wk': jax.random.normal(ks[2], (NUM_KV * HEAD_DIM, HIDDEN), jnp.float32) * s_in, 'bk': jnp.zeros((NUM_KV * HEAD_DIM,), jnp.float32), 'Wv': jax.random.normal(ks[3], (NUM_KV * HEAD_DIM, HIDDEN), jnp.float32) * s_in, 'bv': jnp.zeros((NUM_KV * HEAD_DIM,), jnp.float32), 'Wo': jax.random.normal(ks[4], (HIDDEN, NUM_HEADS * HEAD_DIM), jnp.float32) * s_o, 'bo': jnp.zeros((HIDDEN,), jnp.float32), 'key_weights': jax.random.normal(ks[5], (NUM_HEADS,), jnp.float32)}
    _L1_attn_all = _L1_attn_setup()
    _L1_attn_in = {k: v for k, v in _L1_attn_all.items() if k in ('Wq', 'bq', 'Wk', 'bk', 'Wv', 'bv', 'Wo', 'bo', 'key_weights')}
    del _L1_attn_all

    def _L1_xattn_setup():
        import jax, jax.numpy as jnp
        import numpy as np
        key = jax.random.key(seed)
        k1, k2, k3 = jax.random.split(key, 3)
        B, S, D, M = (8, 256, 256, 128)
        hidden_states = jax.random.normal(k1, (B, S, D), dtype=jnp.float32)
        memory_tokens = jax.random.normal(k2, (B, M, D), dtype=jnp.float32)
        memory_mask = jax.random.randint(k3, (B, M), 0, 2).astype(jnp.bool_)
        return {'hidden_states': hidden_states, 'memory_tokens': memory_tokens, 'memory_mask': memory_mask}
    _L1_xattn_all = _L1_xattn_setup()
    _L1_xattn_in = {k: v for k, v in _L1_xattn_all.items() if k in ()}
    del _L1_xattn_all

    def _L1_ffn_setup():
        import jax, jax.numpy as jnp
        import numpy as np
        E = 8
        K = 2
        CAP = 64
        H = 256
        F = 1024
        key = jax.random.key(seed)
        ks = jax.random.split(key, 6)
        inp = {'hidden_states': jax.random.normal(ks[0], (2, 128, H), jnp.float32), 'router_w': jax.random.normal(ks[1], (E, H), jnp.float32) * (0.01 / np.sqrt(H)), 'w1': jax.random.normal(ks[2], (F, H), jnp.float32) * (1.0 / np.sqrt(H)), 'b1': jax.random.normal(ks[3], (F,), jnp.float32) * 0.01, 'w2': jax.random.normal(ks[4], (H, F), jnp.float32) * (1.0 / np.sqrt(F)), 'b2': jax.random.normal(ks[5], (H,), jnp.float32) * 0.01}
        return inp
    _L1_ffn_all = _L1_ffn_setup()
    _L1_ffn_in = {k: v for k, v in _L1_ffn_all.items() if k in ('router_w', 'w1', 'b1', 'w2', 'b2')}
    del _L1_ffn_all
    return {'x': x, 'ctx_2048': ctx_2048, 'mask_1xSxS2_ff0': mask_1xSxS2_ff0, 'mask_BxS2_bk0': mask_BxS2_bk0, 'L0_attn_Wq': _L0_attn_in['Wq'], 'L0_attn_Wk': _L0_attn_in['Wk'], 'L0_attn_Wv': _L0_attn_in['Wv'], 'L0_attn_Wo': _L0_attn_in['Wo'], 'L0_attn_norm_w': _L0_attn_in['norm_w'], 'L0_xattn_Wq': _L0_xattn_in['Wq'], 'L0_xattn_bq': _L0_xattn_in['bq'], 'L0_xattn_Wk': _L0_xattn_in['Wk'], 'L0_xattn_bk': _L0_xattn_in['bk'], 'L0_xattn_Wv': _L0_xattn_in['Wv'], 'L0_xattn_bv': _L0_xattn_in['bv'], 'L0_xattn_Wo': _L0_xattn_in['Wo'], 'L0_xattn_qn_w': _L0_xattn_in['qn_w'], 'L0_xattn_kn_w': _L0_xattn_in['kn_w'], 'L0_ffn_gate_weight': _L0_ffn_in['gate_weight'], 'L0_ffn_gate_up_proj': _L0_ffn_in['gate_up_proj'], 'L0_ffn_down_proj': _L0_ffn_in['down_proj'], 'L0_ffn_merge_groups': _L0_ffn_in['merge_groups'], 'L0_ffn_dominant_experts': _L0_ffn_in['dominant_experts'], 'L1_attn_Wq': _L1_attn_in['Wq'], 'L1_attn_bq': _L1_attn_in['bq'], 'L1_attn_Wk': _L1_attn_in['Wk'], 'L1_attn_bk': _L1_attn_in['bk'], 'L1_attn_Wv': _L1_attn_in['Wv'], 'L1_attn_bv': _L1_attn_in['bv'], 'L1_attn_Wo': _L1_attn_in['Wo'], 'L1_attn_bo': _L1_attn_in['bo'], 'L1_attn_key_weights': _L1_attn_in['key_weights'], 'L1_ffn_router_w': _L1_ffn_in['router_w'], 'L1_ffn_w1': _L1_ffn_in['w1'], 'L1_ffn_b1': _L1_ffn_in['b1'], 'L1_ffn_w2': _L1_ffn_in['w2'], 'L1_ffn_b2': _L1_ffn_in['b2']}

def reference(x, ctx_2048, mask_1xSxS2_ff0, mask_BxS2_bk0, L0_attn_Wq, L0_attn_Wk, L0_attn_Wv, L0_attn_Wo, L0_attn_norm_w, L0_xattn_Wq, L0_xattn_bq, L0_xattn_Wk, L0_xattn_bk, L0_xattn_Wv, L0_xattn_bv, L0_xattn_Wo, L0_xattn_qn_w, L0_xattn_kn_w, L0_ffn_gate_weight, L0_ffn_gate_up_proj, L0_ffn_down_proj, L0_ffn_merge_groups, L0_ffn_dominant_experts, L1_attn_Wq, L1_attn_bq, L1_attn_Wk, L1_attn_bk, L1_attn_Wv, L1_attn_bv, L1_attn_Wo, L1_attn_bo, L1_attn_key_weights, L1_ffn_router_w, L1_ffn_w1, L1_ffn_b1, L1_ffn_w2, L1_ffn_b2):
    import jax
    import jax.numpy as jnp

    def _L0_attn_ref(x, Wq, Wk, Wv, Wo, norm_w):
        import jax, jax.numpy as jnp
        import numpy as np
        from jax import lax
        B, N, D = (4, 512, 256)
        E = 128
        H = D // E
        CHUNK = 64
        EPS = 1e-06

        def rmsnorm(x, w):
            var = jnp.mean(jnp.square(x), axis=-1, keepdims=True)
            return x * lax.rsqrt(var + EPS) * w

        def chunked_gla(q, v, log_f):
            b, n, h, e = q.shape
            nc = n // CHUNK
            k = 1.0 - jnp.exp(log_f)

            def to_chunks(t):
                return t.reshape(b, nc, CHUNK, h, e).transpose(1, 0, 2, 3, 4)
            qs, ks_, vs, lfs = map(to_chunks, (q, k, v, log_f))
            A = jnp.cumsum(lfs, axis=2)
            mask = jnp.tril(jnp.ones((CHUNK, CHUNK), dtype=bool))

            def step(S, xs):
                qc, kc, vc, Ac = xs
                q_dec = qc * jnp.exp(Ac)
                k_dec = kc * jnp.exp(-Ac)
                scores = jnp.einsum('bthe,bshe->bhts', q_dec, k_dec)
                scores = jnp.where(mask[None, None], scores, 0.0)
                o_intra = jnp.einsum('bhts,bshe->bthe', scores, vc)
                o_inter = jnp.einsum('bthe,bhef->bthf', q_dec, S)
                A_last = Ac[:, -1]
                k_rem = kc * jnp.exp(A_last[:, None] - Ac)
                S_new = jnp.exp(A_last)[..., None] * S + jnp.einsum('bthe,bthf->bhef', k_rem, vc)
                return (S_new, o_intra + o_inter)
            S0 = jnp.zeros((b, h, e, e), dtype=q.dtype)
            _, o = lax.scan(step, S0, (qs, ks_, vs, A))
            return o.transpose(1, 0, 2, 3, 4).reshape(b, n, h, e)
        b, n, d = x.shape
        q = jax.nn.silu(x @ Wq.T)
        f = jax.nn.sigmoid(x @ Wk.T)
        log_f = jax.nn.log_sigmoid(f)
        v = x @ Wv.T
        q, v, log_f = (t.reshape(b, n, H, E) for t in (q, v, log_f))
        o = chunked_gla(q, v, log_f)
        o = o.reshape(b, n, d)
        o = rmsnorm(o, norm_w)
        return o @ Wo.T

    def _L0_xattn_ref(hidden_states, encoder_hidden_states, attention_mask, Wq, bq, Wk, bk, Wv, bv, Wo, qn_w, kn_w):
        import jax, jax.numpy as jnp
        import numpy as np
        H = 256
        NH = 16
        NKV = 4
        HD = 128
        GROUPS = NH // NKV
        EPS = 1e-06
        B, S, SE = (1, 256, 512)

        def _rmsnorm(x, w, eps=EPS):
            xf = x.astype(jnp.float32)
            var = jnp.mean(xf * xf, axis=-1, keepdims=True)
            return (xf * jax.lax.rsqrt(var + eps)).astype(x.dtype) * w
        b, s, _ = hidden_states.shape
        se = encoder_hidden_states.shape[1]
        q = (hidden_states @ Wq + bq).reshape(b, s, NH, HD).transpose(0, 2, 1, 3)
        k = (encoder_hidden_states @ Wk + bk).reshape(b, se, NKV, HD).transpose(0, 2, 1, 3)
        v = (encoder_hidden_states @ Wv + bv).reshape(b, se, NKV, HD).transpose(0, 2, 1, 3)
        k = jnp.repeat(k, GROUPS, axis=1)
        v = jnp.repeat(v, GROUPS, axis=1)
        q = _rmsnorm(q, qn_w)
        k = _rmsnorm(k, kn_w)
        scale = 1.0 / np.sqrt(HD).astype(np.float32)
        scores = jnp.einsum('bhsd,bhed->bhse', q, k) * scale
        scores = scores + attention_mask[:, None, :, :]
        probs = jax.nn.softmax(scores.astype(jnp.float32), axis=-1).astype(q.dtype)
        out = jnp.einsum('bhse,bhed->bhsd', probs, v)
        out = out.transpose(0, 2, 1, 3).reshape(b, s, NH * HD)
        return out @ Wo

    def _L0_ffn_ref(hidden_states, gate_weight, gate_up_proj, down_proj, merge_groups, dominant_experts):
        import jax, jax.numpy as jnp
        import numpy as np
        TOP_K = 8
        NUM_GROUPS = 8
        B, S, H = hidden_states.shape
        G = dominant_experts.shape[0]
        x = hidden_states.reshape(-1, H)
        logits = jnp.einsum('th,eh->te', x, gate_weight)
        probs = jax.nn.softmax(logits.astype(jnp.float32), axis=-1).astype(logits.dtype)
        top_val, top_idx = jax.lax.top_k(probs, TOP_K)
        top_val = top_val / jnp.sum(top_val, axis=-1, keepdims=True)
        sel_group = merge_groups[top_idx]
        onehot = jax.nn.one_hot(sel_group, G, dtype=top_val.dtype)
        w_tg = jnp.einsum('tk,tkg->tg', top_val, onehot)
        gu = gate_up_proj[dominant_experts]
        dn = down_proj[dominant_experts]
        h = jnp.einsum('th,goh->tgo', x, gu)
        gate, up = jnp.split(h, 2, axis=-1)
        act = jax.nn.silu(gate) * up
        y = jnp.einsum('tgi,ghi->tgh', act, dn)
        out = jnp.einsum('tg,tgh->th', w_tg, y)
        return out.reshape(B, S, H)

    def _L1_attn_ref(x, Wq, bq, Wk, bk, Wv, bv, Wo, bo, key_weights):
        import jax, jax.numpy as jnp
        import numpy as np
        HIDDEN = 256
        NUM_HEADS = 32
        HEAD_DIM = 64
        NUM_KV = 8
        GROUP = NUM_HEADS // NUM_KV
        SCALE = HEAD_DIM ** (-0.5)
        ROPE_BASE = 10000.0

        def apply_rope(t):
            S, D = (t.shape[-2], t.shape[-1])
            inv_freq = 1.0 / ROPE_BASE ** (jnp.arange(0, D, 2, dtype=jnp.float32) / D)
            ang = jnp.arange(S, dtype=jnp.float32)[:, None] * inv_freq[None, :]
            cos, sin = (jnp.cos(ang), jnp.sin(ang))
            x1, x2 = (t[..., :D // 2], t[..., D // 2:])
            return jnp.concatenate([x1 * cos - x2 * sin, x2 * cos + x1 * sin], axis=-1)
        B, S, _ = x.shape
        q = (x @ Wq.T + bq).reshape(B, S, NUM_HEADS, HEAD_DIM).transpose(0, 2, 1, 3)
        k = (x @ Wk.T + bk).reshape(B, S, NUM_KV, HEAD_DIM).transpose(0, 2, 1, 3)
        v = (x @ Wv.T + bv).reshape(B, S, NUM_KV, HEAD_DIM).transpose(0, 2, 1, 3)
        q = apply_rope(q)
        k = apply_rope(k)
        qg = q.reshape(B, NUM_KV, GROUP, S, HEAD_DIM)
        scores = jnp.einsum('bkgsd,bktd->bkgst', qg, k) * SCALE
        scores = scores * key_weights.reshape(1, NUM_KV, GROUP, 1, 1)
        causal = jnp.tril(jnp.ones((S, S), bool))
        scores = jnp.where(causal, scores, -jnp.inf)
        a = jax.nn.softmax(scores, axis=-1)
        o = jnp.einsum('bkgst,bktd->bkgsd', a, v)
        o = o.reshape(B, NUM_HEADS, S, HEAD_DIM).transpose(0, 2, 1, 3).reshape(B, S, NUM_HEADS * HEAD_DIM)
        return o @ Wo.T + bo

    def _L1_xattn_ref(hidden_states, memory_tokens, memory_mask):
        import jax, jax.numpy as jnp
        import numpy as np
        B, S, D = hidden_states.shape
        scale = 1.0 / jnp.sqrt(jnp.asarray(D, hidden_states.dtype))
        scores = jnp.einsum('bsd,bmd->bsm', hidden_states, memory_tokens) * scale
        neg_inf = jnp.asarray(-1e+30, scores.dtype)
        scores = jnp.where(memory_mask[:, None, :], scores, neg_inf)
        attn = jax.nn.softmax(scores, axis=-1)
        readout = jnp.einsum('bsm,bmd->bsd', attn, memory_tokens)
        valid_b = jnp.any(memory_mask, axis=-1)
        out = jnp.where(valid_b[:, None, None], readout, jnp.zeros_like(readout))
        return out

    def _L1_ffn_ref(hidden_states, router_w, w1, b1, w2, b2):
        import jax, jax.numpy as jnp
        import numpy as np
        E = 8
        K = 2
        CAP = 64
        H = 256
        F = 1024
        orig_shape = hidden_states.shape
        x = hidden_states.reshape(-1, H)
        N = x.shape[0]
        logits = x @ router_w.T
        probs = jax.nn.softmax(logits, axis=-1)
        top_p, top_i = jax.lax.top_k(probs, K)
        expert_flat = top_i.T.reshape(-1)
        probs_flat = top_p.T.reshape(-1)
        token_idx = jnp.tile(jnp.arange(N), K)
        onehot = (expert_flat[:, None] == jnp.arange(E)[None, :]).astype(jnp.int32)
        pos = jnp.take_along_axis(jnp.cumsum(onehot, axis=0), expert_flat[:, None], axis=1)[:, 0] - 1
        keep = pos < CAP
        dest = expert_flat * CAP + pos
        dest_m = jnp.where(keep, dest, E * CAP)
        buf = jnp.zeros((E * CAP, H), x.dtype).at[dest_m].set(x[token_idx], mode='drop')
        h = jax.nn.gelu(buf @ w1.T + b1, approximate=False) @ w2.T + b2
        gathered = jnp.where(keep[:, None], h[jnp.where(keep, dest, 0)], 0.0) * probs_flat[:, None]
        out = jnp.zeros_like(x).at[token_idx].add(gathered)
        return out.reshape(orig_shape)
    x = _layernorm(x + _L0_attn_ref(x, L0_attn_Wq, L0_attn_Wk, L0_attn_Wv, L0_attn_Wo, L0_attn_norm_w), axis=-1)
    x = _layernorm(x + _L0_xattn_ref(x, ctx_2048, mask_1xSxS2_ff0, L0_xattn_Wq, L0_xattn_bq, L0_xattn_Wk, L0_xattn_bk, L0_xattn_Wv, L0_xattn_bv, L0_xattn_Wo, L0_xattn_qn_w, L0_xattn_kn_w), axis=-1)
    x = _layernorm(x + _L0_ffn_ref(x, L0_ffn_gate_weight, L0_ffn_gate_up_proj, L0_ffn_down_proj, L0_ffn_merge_groups, L0_ffn_dominant_experts), axis=-1)
    x = _layernorm(x + _L1_attn_ref(x, L1_attn_Wq, L1_attn_bq, L1_attn_Wk, L1_attn_bk, L1_attn_Wv, L1_attn_bv, L1_attn_Wo, L1_attn_bo, L1_attn_key_weights), axis=-1)
    x = _layernorm(x + _L1_xattn_ref(x, ctx_2048, mask_BxS2_bk0), axis=-1)
    x = _layernorm(x + _L1_ffn_ref(x, L1_ffn_router_w, L1_ffn_w1, L1_ffn_b1, L1_ffn_w2, L1_ffn_b2), axis=-1)
    return x

_drawn_inputs = setup_inputs


def setup_inputs(seed=0):
    import zlib

    import numpy as np

    out = dict(_drawn_inputs(seed))
    spreads = {'L0_attn_norm_w': (1.0, 0.2),
     'L0_xattn_qn_w': (1.0, 0.6),
     'L0_xattn_kn_w': (1.0, 0.6),
     'L1_attn_bq': (0.0, 0.388),
     'L1_attn_bk': (0.0, 0.58),
     'L1_attn_bv': (0.0, 0.1),
     'L1_attn_bo': (0.0, 0.1)}
    factors = {'L0_attn_Wk': 4.944,
     'L0_xattn_bq': 8.0,
     'L0_xattn_bk': 8.0,
     'L0_ffn_gate_weight': 8.0,
     'L0_ffn_gate_up_proj': 8.0,
     'L0_ffn_down_proj': 8.0,
     'L1_ffn_b1': 64.0,
     'L1_ffn_b2': 64.0,
     'L1_ffn_router_w': 2.688}
    for name, (base, spread) in spreads.items():
        noise = np.random.default_rng([zlib.crc32(name.encode()), seed]).standard_normal(out[name].shape)
        drawn = base * np.exp(spread * noise) if base else spread * noise
        out[name] = jnp.asarray(drawn.astype(out[name].dtype))
    for name, factor in factors.items():
        out[name] = (out[name] * factor).astype(out[name].dtype)
    return out
```

```python
from contextlib import ExitStack

import numpy as np

import concourse.bass as bass
from concourse import mybir

F32 = mybir.dt.float32
I32 = mybir.dt.int32
U8 = mybir.dt.uint8
ALU = mybir.AluOpType
ACT = mybir.ActivationFunctionType
AX_X = mybir.AxisListType.X

P = 128
B = 8
S = 256
D = 256
ST = S // P
DC = D // P
BANK = 512
LN_EPS = 1e-5
RMS_EPS = 1e-6


def at(i, per_iteration, k):
    return i * per_iteration + k


def one(ap, i):
    return ap[bass.ds(i, 1)].squeeze(0)


class Chain:

    def __init__(self, eng, sem, per=0, i=None):
        self.eng, self.sem, self.per, self.i, self.k = eng, sem, per, i, 0

    def __call__(self, ins):
        self.k += 1
        ins.then_inc(self.sem, 1)
        self.eng.wait_ge(self.sem, self.k if self.i is None else at(self.i, self.per, self.k))

    def end(self):
        assert self.i is None or self.k == self.per, self.k


class Stage:

    def __init__(self, k, name, x_in, x_out):
        self.k, self.nc, self.name = k, k.nc, name
        self.ctx, self.sems = ExitStack(), []
        self.x_in = x_in.rearrange("(b s p) d -> b p s d", s=ST, p=P)
        self.x_out = x_out.rearrange("(b s p) d -> b p s d", s=ST, p=P)
        self.xb = self.sb("xb", [P, ST, D])
        self.xT = self.sb("xT", [P, DC, S])
        self.z = self.sb("z", [P, ST, D])
        self.xo = self.sb("xo", [P, ST, D])
        self.bn = self.sb("bn", [P, ST, 6])
        self.mv = self.sb("mv", [P, ST, 2])
        self.ve = self.sb("ve", [P, ST])
        self.rstd = self.sb("rstd", [P, ST])
        self.x_loaded = self.sem("x_loaded")
        self.x_free = self.sem("x_free")
        self.xT_ps = self.sem("xT_ps")
        self.xT_ready = self.sem("xT_ready")
        self.var_ready = self.sem("var_ready")
        self.rstd_ready = self.sem("rstd_ready")
        self.xo_ready = self.sem("xo_ready")
        self.xo_stored = self.sem("xo_stored")
        self.pool_own = self.sem("pool_own")
        self.ln_own = self.sem("ln_own")
        self.fence = self.sem("fence")
        self.own2 = self.sem("own2")

    def sb(self, name, shape, dt=F32):
        return self.ctx.enter_context(self.nc.sbuf_tensor(f"{self.name}_{name}_sb", shape, dt))

    def sem(self, name):
        self.sems.append(self.nc.alloc_semaphore(name=f"{self.name}_{name}"))
        return self.sems[-1]

    def close(self):
        self.nc.clear_and_free_semaphores(self.sems)
        self.nc.all_engine_barrier()
        self.ctx.close()

    def carry(self, dve):
        dve.sem_inc(self.fence, 1)

    def load_x(self, sp, i):
        sp.wait_ge(self.x_free, at(i, 1, 1))
        sp.dma_start(self.xb[:], one(self.x_in, i)).then_inc(self.x_loaded, 16)

    def store_x(self, sp, i):
        sp.wait_ge(self.xo_ready, at(i, 1, 1))
        sp.dma_start(one(self.x_out, i), self.xo[:]).then_inc(self.xo_stored, 16)

    def rows_dma(self, sp, more=None):
        if more:
            more(0)
        self.load_x(sp, 0)
        with sp.Fori(0, B - 1) as i:
            if more:
                more(i + 1)
            self.load_x(sp, i + 1)
            self.store_x(sp, i)
        self.store_x(sp, B - 1)
        sp.wait_ge(self.xo_stored, 16 * (B + 1))

    def transpose_x(self, pe, i, ps):
        pe.wait_ge(self.x_loaded, at(i, 16, 16))
        for dc in range(DC):
            for st in range(ST):
                last = pe.transpose(ps[:, dc * S + st * P:dc * S + (st + 1) * P],
                                    self.xb[:, st, dc * P:(dc + 1) * P], self.k.ident[:])
        last.then_inc(self.xT_ps, 1)

    def copy_xT(self, act, i, ps):
        act.wait_ge(self.xT_ps, at(i, 1, 1))
        act.copy(self.xT[:].rearrange("p c s -> p (c s)"), ps).then_inc(self.xT_ready, 1)

    def credits(self, dve):
        dve.sem_inc(self.x_free, 1)
        dve.sem_inc(self.xo_stored, 16)

    def norm_dve(self, dve, i, wait=True):
        if wait:
            dve.wait_ge(self.x_free, at(i, 1, 2))
        own = Chain(dve, self.ln_own, 3, i)
        for st in range(ST - 1):
            dve.bn_stats(self.bn[:, st, :], self.z[:, st, :])
        own(dve.bn_stats(self.bn[:, ST - 1, :], self.z[:, ST - 1, :]))
        self.carry(dve)
        for st in range(ST - 1):
            dve.bn_aggr(self.mv[:, st, :], self.bn[:, st, :])
        own(dve.bn_aggr(self.mv[:, ST - 1, :], self.bn[:, ST - 1, :]))
        dve.tensor_scalar(self.ve[:], self.mv[:, :, 1], LN_EPS, None, ALU.add).then_inc(self.var_ready, 1)
        dve.wait_ge(self.rstd_ready, at(i, 1, 1))
        dve.wait_ge(self.xo_stored, at(i, 16, 16))
        for st in range(ST):
            last = dve.tensor_scalar(self.xo[:, st, :], self.z[:, st, :], self.mv[:, st, 0:1],
                                     self.rstd[:, st:st + 1], ALU.subtract, ALU.mult)
        own(last)
        own.end()
        dve.nop().then_inc(self.xo_ready, 1)

    def norm_pool(self, pool, i):
        pool.wait_ge(self.var_ready, at(i, 1, 1))
        pool.tensor_tensor(self.rstd[:], self.ve[:], self.k.neg_half[:, 0:ST], ALU.pow).then_inc(self.rstd_ready, 1)


def gla_stage(k, x_in, x_out, wq, wk, wv, wo, norm_w):
    nc, ps, ident = k.nc, k.ps, k.ident
    H, CH = 2, 64
    NCH = S // CH
    s = Stage(k, "gla", x_in, x_out)
    W = {n: s.sb(n, [P, DC, D]) for n in ("wq", "wk", "wv", "wo")}
    nw = s.sb("nw", [P, H])
    keep = s.sb("keep", [P, P])
    reset = s.sb("reset", [P, H * S])
    ones = s.sb("ones", [P, 1])
    t = {n: s.sb(n, [P, H * S]) for n in ("eq", "ef", "qs", "f", "e2", "lf", "c", "kk", "dec", "grow", "qd", "kd",
                                          "kr", "ow", "sq")}
    v = s.sb("v", [P, ST, D])
    krn = s.sb("krn", [P, H * ST, P])
    scm = s.sb("scm", [P, H * ST, P])
    state = s.sb("state", [P, H, NCH - 1, P])
    ss = s.sb("ss", [P, ST])
    r = s.sb("r", [P, ST])
    w_loaded, const_ready = s.sem("w_loaded"), s.sem("const_ready")
    proj_ps, exps, silu, gates, cums, decays, decayed = (s.sem(n) for n in (
        "proj_ps", "exps", "silu", "gates", "cums", "decays", "decayed"))
    v_ready, sc_ps, sc_ready, kr_ps, kr_ready, st_ps, st_ready = (s.sem(n) for n in (
        "v_ready", "sc_ps", "sc_ready", "kr_ps", "kr_ready", "st_ps", "st_ready"))
    o_ps, o_ready, sq_ready, ss_ps, ss_ready, r_ready, y_ps, dve_own, act_own = (s.sem(n) for n in (
        "o_ps", "o_ready", "sq_ready", "ss_ps", "ss_ready", "r_ready", "y_ps", "dve_own", "act_own"))
    qps, fps, vps, scps, krps, ops, stps0, stps1 = (ps[:, n, :] for n in range(8))
    update = lambda h, c: (stps0, stps1)[c % 2][:, (c // 2 * H + h) * P:(c // 2 * H + h + 1) * P]
    xps, yps, ssps = vps, qps, fps

    with nc.Block() as block:
        @block.sync
        def _(sp):
            for n, w in (("wq", wq), ("wk", wk), ("wv", wv), ("wo", wo)):
                sp.dma_start(W[n][:], w.rearrange("(c p) n -> p c n", p=P)).then_inc(w_loaded, 16)
            sp.dma_start(nw[:], norm_w).then_inc(w_loaded, 16)
            s.rows_dma(sp)

        @block.gpsimd
        def _(pool):
            own = Chain(pool, s.pool_own)
            own(pool.memset(keep[:], 1.0))
            own(pool.affine_select(out=keep[:], in_=keep[:], compare_op=ALU.is_ge, fill=0.0, base=0,
                                   pattern=[[1, P]], channel_multiplier=-1))
            own(pool.memset(keep[0:CH, CH:P], 0.0))
            pool.memset(ones[:], 1.0)
            own(pool.memset(reset[:], 1.0))
            pool.memset(reset[:].rearrange("p (c n) -> p c n", n=CH)[:, :, 0:1], 0.0).then_inc(const_ready, 1)
            with pool.Fori(0, B) as i:
                pool.wait_ge(ss_ready, at(i, 1, 1))
                pool.tensor_tensor(r[:], ss[:], k.neg_half[:, 0:ST], ALU.pow).then_inc(r_ready, 1)
                s.norm_pool(pool, i)

        @block.tensor
        def _(pe):
            pe.wait_ge(w_loaded, 16 * 5)
            pe.wait_ge(const_ready, 1)
            with pe.Fori(0, B) as i:
                s.transpose_x(pe, i, xps)
                pe.wait_ge(s.xT_ready, at(i, 1, 1))
                for out, w in ((qps, "wq"), (fps, "wk")):
                    for h in range(H):
                        for dc in range(DC):
                            last = pe.matmul(out[:, h * S:(h + 1) * S], W[w][:, dc, h * P:(h + 1) * P],
                                             s.xT[:, dc, :], start=dc == 0, stop=dc == DC - 1)
                    last.then_inc(proj_ps, 1)
                for st in range(ST):
                    for dc in range(DC):
                        last = pe.matmul(vps[:, st * D:(st + 1) * D], s.xT[:, dc, st * P:(st + 1) * P],
                                         W["wv"][:, dc, :], start=dc == 0, stop=dc == DC - 1)
                last.then_inc(proj_ps, 1)
                pe.wait_ge(decayed, at(i, 2, 1))
                for h in range(H):
                    for st in range(ST):
                        a = h * S + st * P
                        last = pe.matmul(scps[:, (h * ST + st) * P:(h * ST + st + 1) * P], t["kd"][:, a:a + P],
                                         t["qd"][:, a:a + P], start=True, stop=True)
                last.then_inc(sc_ps, 1)
                pe.wait_ge(decayed, at(i, 2, 2))
                for n in range(H * ST):
                    last = pe.transpose(krps[:, n * P:(n + 1) * P], t["kr"][:, n * P:(n + 1) * P], ident[:])
                last.then_inc(kr_ps, 1)
                pe.wait_ge(kr_ready, at(i, 1, 1))
                pe.wait_ge(v_ready, at(i, 1, 1))
                for c in range(NCH - 1):
                    for h in range(H):
                        a = (c % 2) * CH
                        last = pe.matmul(update(h, c), krn[a:a + CH, h * ST + c // 2, :],
                                         v[a:a + CH, c // 2, h * P:(h + 1) * P], start=True, stop=True)
                last.then_inc(st_ps, 1)
                pe.wait_ge(sc_ready, at(i, 1, 1))
                for h in range(H):
                    for st in range(ST):
                        n = h * ST + st
                        pe.matmul(ops[:, n * P:(n + 1) * P], v[:, st, h * P:(h + 1) * P], scm[:, n, :],
                                  start=n == 0, stop=False, skip_group_check=True)
                for c in range(1, NCH):
                    pe.wait_ge(st_ready, at(i, NCH - 1, c))
                    for h in range(H):
                        a = h * S + c * CH
                        last = pe.matmul(ops[:, a:a + CH], state[:, h, c - 1, :], t["qd"][:, a:a + CH],
                                         start=False, stop=True, skip_group_check=True)
                last.then_inc(o_ps, 1)
                pe.wait_ge(sq_ready, at(i, 1, 1))
                for st in range(ST):
                    for h in range(H):
                        last = pe.matmul(ssps[:, st:st + 1], t["sq"][:, h * S + st * P:h * S + (st + 1) * P],
                                         ones[:], start=h == 0, stop=h == H - 1)
                last.then_inc(ss_ps, 1)
                pe.wait_ge(o_ready, at(i, 1, 1))
                for st in range(ST):
                    for h in range(H):
                        last = pe.matmul(yps[:, st * D:(st + 1) * D], t["ow"][:, h * S + st * P:h * S + (st + 1) * P],
                                         W["wo"][:, h, :], start=h == 0, stop=h == H - 1)
                last.then_inc(y_ps, 1)

        @block.scalar
        def _(act):
            with act.Fori(0, B) as i:
                own = Chain(act, act_own, 2, i)
                s.copy_xT(act, i, xps)
                act.wait_ge(proj_ps, at(i, 3, 1))
                act.activation(t["eq"][:], qps, ACT.Exp, scale=-1.0).then_inc(exps, 1)
                act.wait_ge(proj_ps, at(i, 3, 2))
                act.activation(t["ef"][:], fps, ACT.Exp, scale=-1.0).then_inc(exps, 1)
                act.wait_ge(proj_ps, at(i, 3, 3))
                act.copy(v[:].rearrange("p s d -> p (s d)"), vps).then_inc(v_ready, 1)
                act.wait_ge(gates, at(i, 1, 1))
                own(act.activation(t["e2"][:], t["f"][:], ACT.Exp, scale=-1.0))
                act.activation(t["lf"][:], t["e2"][:], ACT.Ln, bias=1.0).then_inc(exps, 1)
                act.wait_ge(cums, at(i, 1, 1))
                act.activation(t["dec"][:], t["c"][:], ACT.Exp, scale=-1.0).then_inc(decays, 1)
                act.activation(t["grow"][:], t["c"][:], ACT.Exp).then_inc(decays, 1)
                act.wait_ge(kr_ps, at(i, 1, 1))
                act.copy(krn[:].rearrange("p n q -> p (n q)"), krps).then_inc(kr_ready, 1)
                act.wait_ge(o_ps, at(i, 1, 1))
                own(act.activation(t["sq"][:], ops, ACT.Square))
                act.nop().then_inc(sq_ready, 1)
                own.end()

        @block.vector
        def _(dve):
            s.credits(dve)
            dve.wait_ge(w_loaded, 16 * 5)
            dve.wait_ge(const_ready, 1)
            with dve.Fori(0, B) as i:
                own = Chain(dve, dve_own, 9, i)
                dve.wait_ge(exps, at(i, 3, 1))
                own(dve.tensor_scalar(t["eq"][:], t["eq"][:], 1.0, None, ALU.add))
                own(dve.reciprocal(t["eq"][:], t["eq"][:]))
                dve.tensor_tensor(t["qs"][:], qps, t["eq"][:], ALU.mult)
                dve.wait_ge(exps, at(i, 3, 2))
                own(dve.tensor_scalar(t["ef"][:], t["ef"][:], 1.0, None, ALU.add))
                dve.reciprocal(t["f"][:], t["ef"][:]).then_inc(gates, 1)
                dve.wait_ge(exps, at(i, 3, 3))
                dve.tensor_tensor_scan(t["c"][:], reset[:], t["lf"][:], 0.0, ALU.mult, ALU.add).then_inc(cums, 1)
                own(dve.tensor_scalar(t["kk"][:], t["e2"][:], 1.0, None, ALU.add))
                own(dve.reciprocal(t["kk"][:], t["kk"][:]))
                own(dve.tensor_tensor(t["kk"][:], t["kk"][:], t["e2"][:], ALU.mult))
                dve.wait_ge(decays, at(i, 2, 1))
                dve.tensor_tensor(t["qd"][:], t["qs"][:], t["dec"][:], ALU.mult)
                dve.wait_ge(decays, at(i, 2, 2))
                own(dve.tensor_tensor(t["kd"][:], t["kk"][:], t["grow"][:], ALU.mult))
                dve.nop().then_inc(decayed, 1)
                to_end = t["dec"][:].rearrange("p (c n) -> p c n", n=CH)[:, :, CH - 1:CH]
                dve.tensor_tensor(t["kr"][:].rearrange("p (c n) -> p c n", n=CH),
                                  t["kd"][:].rearrange("p (c n) -> p c n", n=CH),
                                  to_end.to_broadcast([P, H * NCH, CH]), ALU.mult).then_inc(decayed, 1)
                dve.wait_ge(sc_ps, at(i, 1, 1))
                dve.tensor_tensor(scm[:], scps.rearrange("p (n q) -> p n q", q=P),
                                  keep[:].unsqueeze(1).to_broadcast([P, H * ST, P]), ALU.mult).then_inc(sc_ready, 1)
                dve.wait_ge(st_ps, at(i, 1, 1))
                for c in range(NCH - 1):
                    for h in range(H):
                        new, u = state[:, h, c, :], update(h, c)
                        e = h * S + (c + 1) * CH - 1
                        if c == 0:
                            last = dve.tensor_copy(new, u)
                        else:
                            last = dve.scalar_tensor_tensor(new, state[:, h, c - 1, :], t["dec"][:, e:e + 1], u,
                                                            ALU.mult, ALU.add)
                    last.then_inc(st_ready, 1)
                    dve.wait_ge(st_ready, at(i, NCH - 1, c + 1))
                dve.wait_ge(sq_ready, at(i, 1, 1))
                for h in range(H):
                    last = dve.tensor_scalar(t["ow"][:, h * S:(h + 1) * S], ops[:, h * S:(h + 1) * S],
                                             nw[:, h:h + 1], None, ALU.mult)
                own(last)
                dve.nop().then_inc(o_ready, 1)
                dve.wait_ge(ss_ps, at(i, 1, 1))
                dve.tensor_scalar(ss[:], ssps[:, 0:ST], 1.0 / D, RMS_EPS, ALU.mult, ALU.add).then_inc(ss_ready, 1)
                dve.wait_ge(y_ps, at(i, 1, 1))
                dve.wait_ge(r_ready, at(i, 1, 1))
                for st in range(ST):
                    last = dve.scalar_tensor_tensor(s.z[:, st, :], yps[:, st * D:(st + 1) * D], r[:, st:st + 1],
                                                    s.xb[:, st, :], ALU.mult, ALU.add)
                own(last)
                own.end()
                dve.nop().then_inc(s.x_free, 1)
                s.norm_dve(dve, i)
    s.close()


def cross_stage(k, x_in, x_out, ctxT_in, mask_in, wq, bq, wk, bk, wv, bv, wo, qn, kn):
    nc, ps, ident = k.nc, k.ps, k.ident
    NH, NKV, HD = 16, 4, 128
    G = NH // NKV
    E = ctxT_in.shape[2]
    ET = (E + P - 1) // P
    rows = [min(P, E - e * P) for e in range(ET)]
    chunks = [(c, min(BANK, E - c)) for c in range(0, E, BANK)]
    NC = len(chunks)
    UNITS = ST * NKV
    HEADS = UNITS * G
    NORMED = ET + UNITS
    LAG = 3
    s = Stage(k, "cross", x_in, x_out)
    wq_s, wk_s, wv_s = s.sb("wq", [P, DC, NH * HD]), s.sb("wk", [P, DC, NKV * HD]), s.sb("wv", [P, DC, NKV * HD])
    wo_s = s.sb("wo", [P, NH, D])
    bq_s, bk_s, bv_s = s.sb("bq", [P, NH * HD]), s.sb("bk", [P, NKV * HD]), s.sb("bv", [P, NKV * HD])
    nw = s.sb("nw", [P, 2])
    qk_w = s.sb("qk_w", [P, 1])
    mask = s.sb("mask", [P, ST, E])
    ctxT = s.sb("ctxT", [P, DC, E])
    kT = s.sb("kT", [P, NKV, E])
    v = s.sb("v", [P, ET, NKV * HD])
    qT = s.sb("qT", [P, UNITS, G * P])
    sc = [s.sb(f"sc{n}", [P, E]) for n in range(2)]
    pT = s.sb("pT", [P, ET, G, P])
    raw = [s.sb(f"raw{n}", [P, NKV * HD]) for n in range(3)]
    sq = s.sb("sq", [P, NKV * HD])
    nrm = [s.sb(f"nrm{n}", [P, NKV * HD]) for n in range(2)]
    msq, rr = s.sb("msq", [P, 2, NKV]), s.sb("rr", [P, 3, NKV])
    mx, nmx, sums, rsum = s.sb("mx", [P, 2, NC]), s.sb("nmx", [P, 2]), s.sb("sums", [P, HEADS]), s.sb("rsum", [P, G])
    ones = s.sb("ones", [P, P])
    diag, rbc, oT = raw
    (w_loaded, const_ready, ctx_loaded, kq_ps, v_ps, raw_ready, sq_ready, v_ready, ms_ready, rr_ready,
     nrm_ready, turn_ps, turned) = (s.sem(n) for n in (
        "w_loaded", "const_ready", "ctx_loaded", "kq_ps", "v_ps", "raw_ready", "sq_ready", "v_ready",
        "ms_ready", "rr_ready", "nrm_ready", "turn_ps", "turned"))
    (sc_ps, sc_read, nmx_ready, exp_done, t_ps, t_act, t_dve, pv_ps, diag_ready, oT_ready, y_ps, dve_own) = (
        s.sem(n) for n in ("sc_ps", "sc_read", "nmx_ready", "exp_done", "t_ps", "t_act", "t_dve", "pv_ps",
                           "diag_ready", "oT_ready", "y_ps", "dve_own"))
    bank = lambda n: ps[:, n, :]
    KQ, VB, TB, OB, YB = (0, 1), (2, 3), (4, 5), 6, 7
    SLOTS = (ET + G - 1) // G
    ON_ACT = 2
    T_PS = SLOTS * HEADS + UNITS
    A_EV, D_EV = ON_ACT * HEADS + UNITS, (SLOTS - ON_ACT) * HEADS
    t_count = lambda n, j: SLOTS * n + n // G + j + 1
    a_count = lambda n, j: ON_ACT * n + n // G + j + 1
    d_count = lambda n, j: (SLOTS - ON_ACT) * n + j - ON_ACT + 1

    with nc.Block() as block:
        @block.sync
        def _(sp):
            for t_, a in ((wk_s, wk), (wv_s, wv), (wq_s, wq)):
                sp.dma_start(t_[:], a.rearrange("(c p) n -> p c n", p=P)).then_inc(w_loaded, 16)
            for t_, a in ((bk_s, bk), (bv_s, bv), (bq_s, bq)):
                sp.dma_start(t_[:], a.partition_broadcast(P)).then_inc(w_loaded, 16)
            sp.dma_start(nw[:, 0:1], qn).then_inc(w_loaded, 16)
            sp.dma_start(nw[:, 1:2], kn).then_inc(w_loaded, 16)
            sp.dma_start(wo_s[:], wo.rearrange("(h p) n -> p h n", p=P)).then_inc(w_loaded, 16)
            sp.dma_start(mask[:], mask_in.rearrange("(s p) e -> p s e", p=P)).then_inc(w_loaded, 16)

            def context(i):
                if not isinstance(i, int):
                    sp.wait_ge(v_ps, at(i, ET, 0))
                sp.dma_start(ctxT[:], one(ctxT_in, i).rearrange("(c p) e -> p c e", p=P)).then_inc(ctx_loaded, 16)

            s.rows_dma(sp, context)

        @block.gpsimd
        def _(pool):
            pool.memset(ones[:], 1.0).then_inc(const_ready, 1)
            with pool.Fori(0, B) as i:
                for j in range(NORMED):
                    pool.wait_ge(ms_ready, at(i, NORMED, j + 1))
                    pool.tensor_tensor(rr[:, j % 3, :], msq[:, j % 2, :], k.neg_half[:, 0:NKV], ALU.pow)\
                        .then_inc(rr_ready, 1)
                s.norm_pool(pool, i)

        @block.tensor
        def _(pe):
            pe.wait_ge(w_loaded, 16 * 10)
            pe.wait_ge(const_ready, 1)
            with pe.Fori(0, B) as i:
                def project(j):
                    key = j < ET
                    m = rows[j] if key else P
                    if j >= 2:
                        pe.wait_ge(raw_ready, at(i, NORMED, j - 1))
                    for dc in range(DC):
                        if key:
                            lhs, rhs = ctxT[:, dc, j * P:j * P + m], wk_s[:, dc, :]
                        else:
                            st, g = divmod(j - ET, NKV)
                            lhs, rhs = s.xT[:, dc, st * P:(st + 1) * P], wq_s[:, dc, g * G * HD:(g + 1) * G * HD]
                        last = pe.matmul(bank(KQ[j % 2])[0:m, :], lhs, rhs, start=dc == 0, stop=dc == DC - 1)
                    last.then_inc(kq_ps, 1)
                    if key:
                        if j >= 2:
                            pe.wait_ge(v_ready, at(i, ET, j - 1))
                        for dc in range(DC):
                            last = pe.matmul(bank(VB[j % 2])[0:m, :], ctxT[:, dc, j * P:j * P + m], wv_s[:, dc, :],
                                             start=dc == 0, stop=dc == DC - 1)
                        last.then_inc(v_ps, 1)

                def turn(j):
                    m = rows[j] if j < ET else P
                    pe.wait_ge(nrm_ready, at(i, NORMED, j + 1))
                    if j >= 2:
                        pe.wait_ge(turned, at(i, NORMED, j - 1))
                    for g in range(NKV):
                        last = pe.transpose(bank(TB[j % 2])[:, g * P:g * P + m], nrm[j % 2][0:m, g * P:(g + 1) * P],
                                            ident[0:m, 0:m])
                    last.then_inc(turn_ps, 1)

                def scores(n):
                    u = n // G
                    st, g = divmod(u, NKV)
                    for c, (e0, w) in enumerate(chunks):
                        if n >= 1:
                            pe.wait_ge(sc_read, at(i, NC * HEADS, NC * (n - 1) + c + 1))
                        pe.matmul(bank(c)[:, 0:w], qT[:, u, (n % G) * P:(n % G + 1) * P], kT[:, g, e0:e0 + w],
                                  start=True, stop=True).then_inc(sc_ps, 1)

                def turn_probs(n):
                    pe.wait_ge(exp_done, at(i, HEADS, n + 1))
                    for j in range(SLOTS):
                        if j >= 2:
                            pe.wait_ge(t_act, at(i, A_EV, a_count(n, j - 2)))
                        elif n >= 1:
                            pe.wait_ge(t_dve, at(i, D_EV, d_count(n - 1, j + 2)))
                            if j == 0 and n % G == 0:
                                pe.wait_ge(t_act, at(i, A_EV, a_count(n, 0) - 1))
                        for e in range(G * j, min(G * j + G, ET)):
                            last = pe.transpose(bank(TB[j % 2])[0:rows[e], (e % G) * P:(e % G + 1) * P],
                                                sc[n % 2][:, e * P:e * P + rows[e]], ident[:])
                        last.then_inc(t_ps, 1)

                def mix(u):
                    n = G * u + G - 1
                    pe.wait_ge(t_act, at(i, A_EV, a_count(n, ON_ACT - 1)))
                    pe.wait_ge(t_dve, at(i, D_EV, d_count(n, SLOTS - 1)))
                    if u >= 1:
                        pe.wait_ge(oT_ready, at(i, UNITS, u))
                    g = u % NKV
                    for e in range(ET):
                        last = pe.matmul(bank(OB), v[0:rows[e], e, g * HD:(g + 1) * HD],
                                         pT[0:rows[e], e, :, :].rearrange("p g s -> p (g s)"),
                                         start=e == 0, stop=e == ET - 1)
                    last.then_inc(pv_ps, 1)
                    pe.wait_ge(diag_ready, at(i, UNITS, u + 1))
                    pe.matmul(bank(TB[0]), ones[:], diag[:], start=True, stop=True).then_inc(t_ps, 1)

                def output(u):
                    st, g = divmod(u, NKV)
                    pe.wait_ge(oT_ready, at(i, UNITS, u + 1))
                    for h in range(G):
                        last = pe.matmul(bank(YB)[:, st * D:(st + 1) * D], oT[:, h * P:(h + 1) * P],
                                         wo_s[:, g * G + h, :], start=g == 0 and h == 0,
                                         stop=g == NKV - 1 and h == G - 1)
                    last.then_inc(y_ps, 1)

                s.transpose_x(pe, i, bank(YB))
                pe.wait_ge(ctx_loaded, at(i, 16, 16))
                for j in range(NORMED + LAG):
                    if j == ET:
                        pe.wait_ge(s.xT_ready, at(i, 1, 1))
                    if j < NORMED:
                        project(j)
                    if j >= LAG:
                        turn(j - LAG)
                pe.wait_ge(turned, at(i, NORMED, NORMED))
                pe.wait_ge(v_ready, at(i, ET, ET))
                scores(0)
                for n in range(HEADS):
                    if n + 1 < HEADS:
                        scores(n + 1)
                    turn_probs(n)
                    if n % G == G - 1:
                        mix(n // G)
                    if n % G == 0 and n:
                        output(n // G - 1)
                output(UNITS - 1)

        @block.scalar
        def _(act):
            act.wait_ge(const_ready, 2)
            with act.Fori(0, B) as i:
                s.copy_xT(act, i, bank(YB))
                for j in range(NORMED + LAG):
                    if j < NORMED:
                        m = rows[j] if j < ET else P
                        act.wait_ge(raw_ready, at(i, NORMED, j + 1))
                        if j >= 1:
                            act.wait_ge(ms_ready, at(i, NORMED, j))
                        act.activation(sq[0:m, :], raw[j % 3][0:m, :], ACT.Square).then_inc(sq_ready, 1)
                    if j >= LAG:
                        n = j - LAG
                        act.wait_ge(turn_ps, at(i, NORMED, n + 1))
                        src = bank(TB[n % 2])
                        if n < ET:
                            act.copy(kT[:, :, n * P:n * P + rows[n]],
                                     src.rearrange("p (g e) -> p g e", g=NKV)[:, :, 0:rows[n]]).then_inc(turned, 1)
                        else:
                            act.activation(qT[:, n - ET, :], src, ACT.Copy, scale=qk_w[:]).then_inc(turned, 1)

                def exp(n):
                    act.wait_ge(nmx_ready, at(i, HEADS, n + 1))
                    act.activation(sc[n % 2][:], sc[n % 2][:], ACT.Exp, bias=nmx[:, n % 2:n % 2 + 1],
                                   accum_out=sums[:, n:n + 1]).then_inc(exp_done, 1)

                exp(0)
                for n in range(HEADS):
                    if n >= G and n % G == 0:
                        act.wait_ge(pv_ps, at(i, UNITS, n // G))
                    for j in range(ON_ACT):
                        act.wait_ge(t_ps, at(i, T_PS, t_count(n, j)))
                        act.copy(pT[:, G * j:G * j + G, n % G, :],
                                 bank(TB[j % 2]).rearrange("p (e s) -> p e s", e=G)).then_inc(t_act, 1)
                    if n + 1 < HEADS:
                        exp(n + 1)
                    if n % G == G - 1:
                        if n // G >= 1:
                            act.wait_ge(oT_ready, at(i, UNITS, n // G))
                        act.wait_ge(t_ps, at(i, T_PS, t_count(n, SLOTS - 1) + 1))
                        act.copy(rbc[:], bank(TB[0])).then_inc(t_act, 1)

        @block.vector
        def _(dve):
            s.credits(dve)
            dve.wait_ge(w_loaded, 16 * 10)
            dve.wait_ge(const_ready, 1)
            dve.scalar_tensor_tensor(qk_w[:], nw[:, 0:1], float(HD) ** -0.5, nw[:, 1:2], ALU.mult, ALU.mult)\
               .then_inc(const_ready, 1)
            with dve.Fori(0, B) as i:
                own = Chain(dve, dve_own, NORMED + UNITS, i)
                for j in range(NORMED + 2):
                    if j < NORMED:
                        key = j < ET
                        m = rows[j] if key else P
                        bias = bk_s[:] if key else bq_s[:, (j - ET) % NKV * 512:((j - ET) % NKV + 1) * 512]
                        dve.wait_ge(kq_ps, at(i, NORMED, j + 1))
                        if j >= 3:
                            dve.wait_ge(sq_ready, at(i, NORMED, j - 2))
                            dve.wait_ge(nrm_ready, at(i, NORMED, j - 2))
                        dve.tensor_tensor(raw[j % 3][0:m, :], bank(KQ[j % 2])[0:m, :], bias[0:m, :], ALU.add)\
                           .then_inc(raw_ready, 1)
                        if key:
                            dve.wait_ge(v_ps, at(i, ET, j + 1))
                            dve.tensor_tensor(v[0:m, j, :], bank(VB[j % 2])[0:m, :], bv_s[0:m, :], ALU.add)\
                               .then_inc(v_ready, 1)
                    if 1 <= j <= NORMED:
                        n = j - 1
                        m = rows[n] if n < ET else P
                        dve.wait_ge(sq_ready, at(i, NORMED, n + 1))
                        if n >= 2:
                            dve.wait_ge(rr_ready, at(i, NORMED, n - 1))
                        own(dve.tensor_reduce(msq[0:m, n % 2, :], sq[0:m, :].rearrange("p (g d) -> p g d", g=NKV),
                                              AX_X, ALU.add))
                        dve.tensor_scalar(msq[0:m, n % 2, :], msq[0:m, n % 2, :], 1.0 / HD, RMS_EPS,
                                          ALU.mult, ALU.add).then_inc(ms_ready, 1)
                    if j >= 2:
                        n = j - 2
                        m = rows[n] if n < ET else P
                        dve.wait_ge(rr_ready, at(i, NORMED, n + 1))
                        if n >= 2:
                            dve.wait_ge(turn_ps, at(i, NORMED, n - 1))
                        dve.tensor_tensor(nrm[n % 2][0:m, :].rearrange("p (g d) -> p g d", g=NKV),
                                          raw[n % 3][0:m, :].rearrange("p (g d) -> p g d", g=NKV),
                                          rr[0:m, n % 3, :].unsqueeze(2).to_broadcast([m, NKV, HD]),
                                          ALU.mult).then_inc(nrm_ready, 1)

                def maxima(n):
                    st = n // G // NKV
                    if n >= 2:
                        dve.wait_ge(t_ps, at(i, T_PS, t_count(n - 2, SLOTS - 1)))
                    for c, (e0, w) in enumerate(chunks):
                        dve.wait_ge(sc_ps, at(i, NC * HEADS, NC * n + c + 1))
                        s.carry(dve)
                        dve.tensor_tensor_reduce(sc[n % 2][:, e0:e0 + w], bank(c)[:, 0:w], mask[:, st, e0:e0 + w],
                                                 1.0, -3.0e38, ALU.add, ALU.max, mx[:, n % 2, c:c + 1])\
                           .then_inc(sc_read, 1)
                    dve.wait_ge(sc_read, at(i, NC * HEADS, NC * n + NC))
                    dve.tensor_reduce(nmx[:, n % 2:n % 2 + 1], mx[:, n % 2, :], AX_X, ALU.max, negate=True)\
                       .then_inc(nmx_ready, 1)

                def empty(n):
                    if n >= G and n % G == 0:
                        dve.wait_ge(pv_ps, at(i, UNITS, n // G))
                    for j in range(ON_ACT, SLOTS):
                        dve.wait_ge(t_ps, at(i, T_PS, t_count(n, j)))
                        ne = min(G, ET - G * j)
                        m = P if ne == G else rows[-1]
                        dve.tensor_copy(pT[0:m, G * j:G * j + ne, n % G, :],
                                        bank(TB[j % 2])[0:m, 0:ne * P].rearrange("p (e s) -> p e s", e=ne))\
                           .then_inc(t_dve, 1)

                def reciprocals(u):
                    dve.wait_ge(exp_done, at(i, HEADS, G * u + G))
                    own(dve.reciprocal(rsum[:], sums[:, G * u:G * u + G]))
                    dve.tensor_tensor(diag[:].rearrange("p (h s) -> p h s", h=G),
                                      ident[:].unsqueeze(1).to_broadcast([P, G, P]),
                                      rsum[:].unsqueeze(2).to_broadcast([P, G, P]), ALU.mult)\
                       .then_inc(diag_ready, 1)

                def divide(u):
                    dve.wait_ge(t_act, at(i, A_EV, a_count(G * u + G - 1, ON_ACT - 1) + 1))
                    dve.wait_ge(pv_ps, at(i, UNITS, u + 1))
                    if u >= 1:
                        dve.wait_ge(y_ps, at(i, UNITS, u))
                    dve.tensor_tensor(oT[:], bank(OB), rbc[:], ALU.mult).then_inc(oT_ready, 1)

                maxima(0)
                for n in range(HEADS):
                    if n + 1 < HEADS:
                        maxima(n + 1)
                    empty(n)
                    if n % G == G - 1:
                        reciprocals(n // G)
                        divide(n // G)
                dve.wait_ge(y_ps, at(i, UNITS, UNITS))
                dve.tensor_tensor(s.z[:].rearrange("p s d -> p (s d)"), bank(YB),
                                  s.xb[:].rearrange("p s d -> p (s d)"), ALU.add).then_inc(s.x_free, 1)
                s.norm_dve(dve, i)
    s.close()


def experts_stage(k, x_in, x_out, gate_w, gate_up, down, merge, dominant):
    nc, ps, ident = k.nc, k.ps, k.ident
    E, I = down.shape[0], down.shape[1]
    GR = dominant.shape[1]
    s = Stage(k, "experts", x_in, x_out)
    gw = s.sb("gw", [P, DC, E])
    gu = s.sb("gu", [P, DC, GR * 2 * I])
    dn = s.sb("dn", [I, GR, D])
    dom = s.sb("dom", [1, GR], I32)
    mg, mgf = s.sb("mg", [E, 1], I32), s.sb("mgf", [E, 1])
    gi, gf = s.sb("gi", [E, GR], I32), s.sb("gf", [E, GR])
    group = s.sb("group", [E, GR])
    nmx, e, top, left, sel = (s.sb("nmx", [P, ST]), s.sb("e", [P, ST, E]), s.sb("top", [P, ST, 8]),
                              s.sb("left", [P, ST, E]), s.sb("sel", [P, ST, E]))
    tsum, rts, selT, wt = s.sb("tsum", [P, ST]), s.sb("rts", [P, ST]), s.sb("selT", [E, S]), s.sb("wt", [P, ST, GR])
    g = [s.sb(f"g{n}", [P, GR, I]) for n in range(ST)]
    a = [s.sb(f"a{n}", [P, GR, I]) for n in range(ST)]
    aT = [s.sb(f"aT{n}", [I, GR, P]) for n in range(ST)]
    (w_loaded, dom_loaded, const_ready, lg_ps, nmx_ready, e_ready, sel_ready, selT_ps, selT_ready, w_ps, wt_ready,
     h_ps, silu_ready, a_half, a_ready, t_ps, t_ev, y_ps, dve_own) = (s.sem(n) for n in (
        "w_loaded", "dom_loaded", "const_ready", "lg_ps", "nmx_ready", "e_ready", "sel_ready", "selT_ps",
        "selT_ready", "w_ps", "wt_ready", "h_ps", "silu_ready", "a_half", "a_ready", "t_ps", "t_ev", "y_ps",
        "dve_own"))
    HB = range(0, 4)
    TB, YB, MB = (4, 5), 6, 7
    W2 = 2 * 2 * I
    hid = ps[:, 0:4, 0:W2].rearrange("p b (g o) -> p b g o", g=2)
    v4 = lambda t_: t_[:].rearrange("p (b g) i -> p b g i", g=2)
    misc = ps[:, MB, :]
    LG, WP, TP = misc[:, 0:ST * E], misc[:, 64:64 + ST * GR], misc[0:E, 128:128 + S]

    with nc.Block() as block:
        @block.sync
        def _(sp):
            sp.dma_start(dom[:], dominant).then_inc(dom_loaded, 16)
            sp.dma_start(gw[:], gate_w.rearrange("(c p) n -> p c n", p=P)).then_inc(w_loaded, 16)
            sp.dma_start(mg[:], merge).then_inc(w_loaded, 16)
            sp.wait_ge(dom_loaded, 16)
            for n in range(GR):
                x = sp.value_load(dom[0:1, n:n + 1], min_val=0, max_val=E - 1)
                sp.dma_start(gu[:, :, n * 2 * I:(n + 1) * 2 * I],
                             one(gate_up, x).rearrange("(c p) o -> p c o", p=P)).then_inc(w_loaded, 16)
                sp.dma_start(dn[:, n, :], one(down, x)).then_inc(w_loaded, 16)
            s.rows_dma(sp)

        @block.gpsimd
        def _(pool):
            pool.iota(gi[:], [[1, GR]], base=0, channel_multiplier=0).then_inc(const_ready, 1)
            with pool.Fori(0, B) as i:
                s.norm_pool(pool, i)

        @block.tensor
        def _(pe):
            pe.wait_ge(w_loaded, 16 * (2 + 2 * GR))
            pe.wait_ge(const_ready, 2)
            with pe.Fori(0, B) as i:
                def hidden(st):
                    if st >= 1:
                        pe.wait_ge(a_half, at(i, ST, st))
                    for q in HB:
                        for dc in range(DC):
                            last = pe.matmul(ps[:, q, 0:W2], s.xT[:, dc, st * P:(st + 1) * P],
                                             gu[:, dc, q * W2:(q + 1) * W2], start=dc == 0, stop=dc == DC - 1)
                    last.then_inc(h_ps, 1)

                def down_product(st):
                    pe.wait_ge(a_ready, at(i, ST, st + 1))
                    if st >= 1:
                        pe.wait_ge(t_ev, at(i, 2 * ST, 2 * st))
                    for n in range(GR):
                        last = pe.transpose(ps[0:I, TB[n // 4], (n % 4) * P:(n % 4 + 1) * P], a[st][:, n, :], ident[:])
                        if n % 4 == 3:
                            last.then_inc(t_ps, 1)
                    pe.wait_ge(t_ev, at(i, 2 * ST, 2 * st + 2))
                    for n in range(GR):
                        last = pe.matmul(ps[:, YB, st * D:(st + 1) * D], aT[st][:, n, :], dn[:, n, :],
                                         start=n == 0, stop=n == GR - 1)
                    last.then_inc(y_ps, 1)

                s.transpose_x(pe, i, ps[:, YB, :])
                pe.wait_ge(s.xT_ready, at(i, 1, 1))
                for st in range(ST):
                    for dc in range(DC):
                        last = pe.matmul(LG[:, st * E:(st + 1) * E], s.xT[:, dc, st * P:(st + 1) * P], gw[:, dc, :],
                                         start=dc == 0, stop=dc == DC - 1)
                last.then_inc(lg_ps, 1)
                hidden(0)
                pe.wait_ge(sel_ready, at(i, 1, 1))
                for st in range(ST):
                    last = pe.transpose(TP[:, st * P:(st + 1) * P], sel[:, st, :], ident[:])
                last.then_inc(selT_ps, 1)
                pe.wait_ge(selT_ready, at(i, 1, 1))
                for st in range(ST):
                    last = pe.matmul(WP[:, st * GR:(st + 1) * GR], selT[:, st * P:(st + 1) * P], group[:],
                                     start=True, stop=True)
                last.then_inc(w_ps, 1)
                hidden(1)
                down_product(0)
                down_product(1)

        @block.scalar
        def _(act):
            with act.Fori(0, B) as i:
                s.copy_xT(act, i, ps[:, YB, :])
                act.wait_ge(nmx_ready, at(i, 1, 1))
                for st in range(ST):
                    last = act.activation(e[:, st, :], LG[:, st * E:(st + 1) * E], ACT.Exp, bias=nmx[:, st:st + 1])
                last.then_inc(e_ready, 1)
                for st in range(ST):
                    act.wait_ge(h_ps, at(i, ST, st + 1))
                    act.activation(v4(g[st]), hid[:, :, :, 0:I], ACT.Silu).then_inc(silu_ready, 1)
                for st in range(ST):
                    for q in range(2):
                        act.wait_ge(t_ps, at(i, 2 * ST, 2 * st + q + 1))
                        act.copy(aT[st][:, 4 * q:4 * q + 4, :].rearrange("p g s -> p (g s)"),
                                 ps[0:I, TB[q], :]).then_inc(t_ev, 1)

        @block.vector
        def _(dve):
            s.credits(dve)
            dve.wait_ge(w_loaded, 16 * (2 + 2 * GR))
            dve.wait_ge(const_ready, 1)
            first = Chain(dve, dve_own)
            dve.tensor_copy(mgf[:], mg[:])
            first(dve.tensor_copy(gf[:], gi[:]))
            dve.tensor_scalar(group[:], gf[:], mgf[:], None, ALU.is_equal).then_inc(const_ready, 1)
            with dve.Fori(0, B) as i:
                own = Chain(dve, a_half, ST, i)
                fence = Chain(dve, s.own2, 3, i)
                dve.wait_ge(lg_ps, at(i, 1, 1))
                dve.tensor_reduce(nmx[:], LG.rearrange("p (s e) -> p s e", s=ST), AX_X, ALU.max, negate=True)\
                   .then_inc(nmx_ready, 1)
                dve.wait_ge(e_ready, at(i, 1, 1))
                s.carry(dve)
                for st in range(ST):
                    last = dve.max(top[:, st, :], e[:, st, :])
                fence(last)
                s.carry(dve)
                for st in range(ST):
                    last = dve.match_replace(left[:, st, :], top[:, st, :], e[:, st, :], -1.0)
                fence(last)
                for st in range(ST):
                    last = dve.scalar_tensor_tensor(sel[:, st, :], left[:, st, :], 0.0, e[:, st, :], ALU.is_lt,
                                                    ALU.mult, accum_out=tsum[:, st:st + 1])
                fence(last)
                dve.sem_inc(sel_ready, 1)
                dve.reciprocal(rts[:], tsum[:])
                dve.wait_ge(selT_ps, at(i, 1, 1))
                dve.tensor_copy(selT[:], TP).then_inc(selT_ready, 1)
                dve.wait_ge(w_ps, at(i, 1, 1))
                dve.tensor_tensor(wt[:], WP.rearrange("p (s g) -> p s g", s=ST),
                                  rts[:].unsqueeze(2).to_broadcast([P, ST, GR]), ALU.mult).then_inc(wt_ready, 1)
                for st in range(ST):
                    dve.wait_ge(silu_ready, at(i, ST, st + 1))
                    own(dve.tensor_tensor(v4(a[st]), hid[:, :, :, I:2 * I], v4(g[st]), ALU.mult))
                    if st == 0:
                        dve.wait_ge(wt_ready, at(i, 1, 1))
                    dve.tensor_tensor(a[st][:], a[st][:], wt[:, st, :].unsqueeze(2).to_broadcast([P, GR, I]),
                                      ALU.mult).then_inc(a_ready, 1)
                own.end()
                dve.wait_ge(y_ps, at(i, ST, ST))
                dve.tensor_tensor(s.z[:].rearrange("p s d -> p (s d)"), ps[:, YB, :],
                                  s.xb[:].rearrange("p s d -> p (s d)"), ALU.add).then_inc(s.x_free, 1)
                s.norm_dve(dve, i)
    s.close()


def memory_stage(k, x_in, x_out, ctxT_in, ctx_in, mask_in):
    nc, ps, ident = k.nc, k.ps, k.ident
    E = ctxT_in.shape[2]
    ET = (E + P - 1) // P
    FULL = E // P
    rows = [min(P, E - e * P) for e in range(ET)]
    chunks = [(c, min(BANK, E - c)) for c in range(0, E, BANK)]
    NC = len(chunks)
    SCALE = float(D) ** -0.5
    G = BANK // P
    SLOTS = (ET + G - 1) // G
    NT = ST * SLOTS
    s = Stage(k, "memory", x_in, x_out)
    ctxT, ctx = s.sb("ctxT", [P, DC, E]), s.sb("ctx", [P, ET, D])
    m8 = s.sb("m8", [P, E], U8)
    am = s.sb("am", [P, E])
    any_ = s.sb("any", [P, 1])
    sc = [s.sb(f"sc{n}", [P, E]) for n in range(ST)]
    pT = [s.sb(f"pT{n}", [P, ET, P]) for n in range(ST)]
    mx, nmx, sums, rs = s.sb("mx", [P, ST, NC]), s.sb("nmx", [P, ST]), s.sb("sums", [P, ST]), s.sb("rs", [P, ST])
    (ctxT_loaded, ctx_loaded, m_loaded, am_ready, sc_ps, sc_read, nmx_ready, exp_done, t_ps, t_ev, o_ps, dve_own) = (
        s.sem(n) for n in ("ctxT_loaded", "ctx_loaded", "m_loaded", "am_ready", "sc_ps", "sc_read", "nmx_ready",
                           "exp_done", "t_ps", "t_ev", "o_ps", "dve_own"))
    TB, OB, XB = (4, 5), 6, 7

    with nc.Block() as block:
        @block.sync
        def _(sp):
            def context(i):
                later = not isinstance(i, int)
                if later:
                    sp.wait_ge(am_ready, at(i, 2, 0))
                    s.carry(sp)
                sp.dma_start(m8[:], one(mask_in, i).partition_broadcast(P)).then_inc(m_loaded, 16)
                if later:
                    sp.wait_ge(sc_ps, at(i, NC * ST, 0))
                    s.carry(sp)
                sp.dma_start(ctxT[:], one(ctxT_in, i).rearrange("(c p) e -> p c e", p=P)).then_inc(ctxT_loaded, 16)
                if later:
                    sp.wait_ge(o_ps, at(i, ST, 0))
                    s.carry(sp)
                c = one(ctx_in, i)
                sp.dma_start(ctx[:, 0:FULL, :], c[0:FULL * P, :].rearrange("(e p) d -> p e d", p=P))\
                  .then_inc(ctx_loaded, 16)
                sp.dma_start(ctx[0:rows[-1], FULL, :], c[FULL * P:E, :]).then_inc(ctx_loaded, 16)

            s.rows_dma(sp, context)

        @block.gpsimd
        def _(pool):
            with pool.Fori(0, B) as i:
                s.norm_pool(pool, i)

        @block.tensor
        def _(pe):
            with pe.Fori(0, B) as i:
                def scores(st):
                    for c, (e0, w) in enumerate(chunks):
                        if st >= 1:
                            pe.wait_ge(sc_read, at(i, NC * ST, NC * (st - 1) + c + 1))
                        for dc in range(DC):
                            last = pe.matmul(ps[:, c, 0:w], s.xT[:, dc, st * P:(st + 1) * P], ctxT[:, dc, e0:e0 + w],
                                             start=dc == 0, stop=dc == DC - 1)
                        last.then_inc(sc_ps, 1)

                def turn_probs(st):
                    pe.wait_ge(exp_done, at(i, ST, st + 1))
                    for j in range(SLOTS):
                        n = SLOTS * st + j
                        if n >= 2:
                            pe.wait_ge(t_ev, at(i, NT, n - 1))
                        for e in range(G * j, min(G * j + G, ET)):
                            last = pe.transpose(ps[0:rows[e], TB[n % 2], (e % G) * P:(e % G + 1) * P],
                                                sc[st][:, e * P:e * P + rows[e]], ident[:])
                        last.then_inc(t_ps, 1)

                def mix(st):
                    pe.wait_ge(t_ev, at(i, NT, SLOTS * (st + 1)))
                    for e in range(ET):
                        last = pe.matmul(ps[:, OB, st * D:(st + 1) * D], pT[st][0:rows[e], e, :], ctx[0:rows[e], e, :],
                                         start=e == 0, stop=e == ET - 1)
                    last.then_inc(o_ps, 1)

                s.transpose_x(pe, i, ps[:, XB, :])
                pe.wait_ge(s.xT_ready, at(i, 1, 1))
                pe.wait_ge(ctxT_loaded, at(i, 16, 16))
                scores(0)
                scores(1)
                turn_probs(0)
                pe.wait_ge(ctx_loaded, at(i, 32, 32))
                mix(0)
                turn_probs(1)
                mix(1)

        @block.scalar
        def _(act):
            with act.Fori(0, B) as i:
                s.copy_xT(act, i, ps[:, XB, :])
                for st in range(ST):
                    act.wait_ge(nmx_ready, at(i, ST, st + 1))
                    act.activation(sc[st][:], sc[st][:], ACT.Exp, bias=nmx[:, st:st + 1], scale=SCALE,
                                   accum_out=sums[:, st:st + 1]).then_inc(exp_done, 1)
                    for j in range(SLOTS):
                        n = SLOTS * st + j
                        act.wait_ge(t_ps, at(i, NT, n + 1))
                        ne = min(G, ET - G * j)
                        m = P if ne == G else rows[-1]
                        act.copy(pT[st][0:m, G * j:G * j + ne, :].rearrange("p e s -> p (e s)"),
                                 ps[0:m, TB[n % 2], 0:ne * P]).then_inc(t_ev, 1)

        @block.vector
        def _(dve):
            s.credits(dve)
            with dve.Fori(0, B) as i:
                own = Chain(dve, dve_own, ST + 2, i)
                dve.wait_ge(m_loaded, at(i, 16, 16))
                dve.tensor_reduce(any_[:], m8[:], AX_X, ALU.max).then_inc(am_ready, 1)
                dve.tensor_scalar(am[:], m8[:], 1.0, 1e30 / SCALE, ALU.subtract, ALU.mult).then_inc(am_ready, 1)
                dve.wait_ge(am_ready, at(i, 2, 2))
                for st in range(ST):
                    for c, (e0, w) in enumerate(chunks):
                        dve.wait_ge(sc_ps, at(i, NC * ST, NC * st + c + 1))
                        s.carry(dve)
                        dve.tensor_tensor_reduce(sc[st][:, e0:e0 + w], ps[:, c, 0:w], am[:, e0:e0 + w], 1.0, -3.0e38,
                                                 ALU.add, ALU.max, mx[:, st, c:c + 1]).then_inc(sc_read, 1)
                    dve.wait_ge(sc_read, at(i, NC * ST, NC * st + NC))
                    own(dve.tensor_reduce(nmx[:, st:st + 1], mx[:, st, :], AX_X, ALU.max, negate=True))
                    dve.tensor_scalar(nmx[:, st:st + 1], nmx[:, st:st + 1], SCALE, None, ALU.mult)\
                       .then_inc(nmx_ready, 1)
                dve.wait_ge(exp_done, at(i, ST, ST))
                own(dve.reciprocal(rs[:], sums[:]))
                own(dve.tensor_scalar(rs[:], rs[:], any_[:], None, ALU.mult))
                own.end()
                dve.wait_ge(o_ps, at(i, ST, ST))
                for st in range(ST):
                    last = dve.scalar_tensor_tensor(s.z[:, st, :], ps[:, OB, st * D:(st + 1) * D], rs[:, st:st + 1],
                                                    s.xb[:, st, :], ALU.mult, ALU.add)
                last.then_inc(s.x_free, 1)
                s.norm_dve(dve, i)
    s.close()


def rotary_stage(k, x_in, x_out, wq, bq, wk, bk, wv, bv, wo, bo, key_w, cos_in, sin_in):
    nc, ps, ident = k.nc, k.ps, k.ident
    NH, NKV, HD = 32, 8, 64
    HALF = HD // 2
    NA = NKV // 2
    G = NH // NKV
    PAIRS = NH // 2
    OW = NH * HD
    W3 = 3 * P
    s = Stage(k, "rotary", x_in, x_out)
    wq_s, wk_s, wv_s = s.sb("wq", [P, DC, OW]), s.sb("wk", [P, DC, NKV * HD]), s.sb("wv", [P, DC, NKV * HD])
    wo_s = s.sb("wo", [P, PAIRS, D])
    bq_s, bk_s, bv_s, bo_s = s.sb("bq", [P, OW]), s.sb("bk", [P, 512]), s.sb("bv", [P, 512]), s.sb("bo", [P, D])
    kw = s.sb("kw", [P, PAIRS])
    cos, sin = s.sb("cos", [P, ST, HALF]), s.sb("sin", [P, ST, HALF])
    nsin = s.sb("nsin", [P, ST, HALF])
    cm = s.sb("cm", [P, W3])
    raw = [s.sb(f"raw{n}", [P, 512]) for n in range(2)]
    byc = [s.sb(f"byc{n}", [P, 512]) for n in range(2)]
    rot = [s.sb(f"rot{n}", [P, 512]) for n in range(2)]
    bys = s.sb("bys", [P, 512])
    kT, v = s.sb("kT", [P, NA, S]), s.sb("v", [P, ST, NKV * HD])
    qT = s.sb("qT", [P, ST, PAIRS, P])
    sc = [s.sb(f"sc{n}", [P, W3]) for n in range(4)]
    pT = [s.sb(f"pT{n}", [P, W3]) for n in range(2)]
    mx, nmx, sums, rs = (s.sb("mx", [P, 4, ST]), s.sb("nmx", [P, 4, ST]), s.sb("sums", [P, NH, ST]),
                         s.sb("rs", [P, G * ST]))
    o = s.sb("o", [P, ST, OW])
    oT = s.sb("oT", [P, ST, PAIRS, P])
    zb = s.sb("zb", [P, ST, D])
    (w_loaded, const_ready, pr_ps, raw_ready, byc_ready, bys_ready, rot_ready, turn_ps, turned, v_ps, v_ready, sc_ps,
     sc_read, nmx_ready, exp_done, t_ps, t_act, t_dve, o_ps, o_ready, oT_ps, oT_ready, y_ps, dve_own, zb_ready) = (
        s.sem(n) for n in (
            "w_loaded", "const_ready", "pr_ps", "raw_ready", "byc_ready", "bys_ready", "rot_ready", "turn_ps",
            "turned", "v_ps", "v_ready", "sc_ps", "sc_read", "nmx_ready", "exp_done", "t_ps", "t_act", "t_dve",
            "o_ps", "o_ready", "oT_ps", "oT_ready", "y_ps", "dve_own", "zb_ready"))
    tiles = [("k", st, 0) for st in range(ST)] + [("q", st, a) for st in range(ST) for a in range(NA)]
    NT = len(tiles)
    LAG = 2
    TB, OB, XB = (4, 5), (6, 7), 7
    GROUPS = NH // G
    nh = lambda n: (n // 2 // G, n // 2 % G, n % 2)

    with nc.Block() as block:
        @block.sync
        def _(sp):
            def w(t_, a):
                sp.dma_start(t_, a).then_inc(w_loaded, 16)

            w(wk_s[:], wk.rearrange("(c p) n -> p c n", p=P))
            w(wv_s[:], wv.rearrange("(c p) n -> p c n", p=P))
            w(wq_s[:], wq.rearrange("(c p) n -> p c n", p=P))
            for t_, a in ((bk_s, bk), (bv_s, bv), (bq_s, bq), (bo_s, bo)):
                w(t_[:], a.partition_broadcast(P))
            w(cos[:], cos_in.rearrange("(s p) e -> p s e", p=P))
            w(sin[:], sin_in.rearrange("(s p) e -> p s e", p=P))
            for j in range(2):
                w(kw[j * HD:(j + 1) * HD, :], key_w[j].partition_broadcast(HD))
            w(wo_s[:], wo.rearrange("(q p) n -> p q n", p=P))
            s.rows_dma(sp)

        W_ALL = 16 * (3 + 4 + 2 + 2 + 1)

        @block.gpsimd
        def _(pool):
            own = Chain(pool, s.pool_own)
            own(pool.memset(cm[:], 0.0))
            for a in (0, 2 * P):
                last = pool.affine_select(out=cm[:, a:a + P], in_=cm[:, a:a + P], compare_op=ALU.is_ge, fill=-1e30,
                                          base=0, pattern=[[-1, P]], channel_multiplier=1)
            last.then_inc(const_ready, 1)
            pool.wait_ge(w_loaded, W_ALL)
            with pool.Fori(0, B) as i:
                for j, (kind, st, a) in enumerate(tiles):
                    pool.wait_ge(raw_ready, at(i, NT, j + 1))
                    if j >= 2:
                        pool.wait_ge(rot_ready, at(i, NT, j - 1))
                    pool.tensor_tensor(byc[j % 2][:].rearrange("p (h e) -> p h e", e=HALF),
                                       raw[j % 2][:].rearrange("p (h e) -> p h e", e=HALF),
                                       cos[:, st, :].unsqueeze(1).to_broadcast([P, 16, HALF]), ALU.mult)\
                        .then_inc(byc_ready, 1)
                s.norm_pool(pool, i)

        @block.tensor
        def _(pe):
            pe.wait_ge(w_loaded, W_ALL)
            with pe.Fori(0, B) as i:
                def project(j):
                    kind, st, a = tiles[j]
                    if j >= 2:
                        pe.wait_ge(raw_ready, at(i, NT, j - 1))
                    for dc in range(DC):
                        rhs = wk_s[:, dc, :] if kind == "k" else wq_s[:, dc, a * 512:(a + 1) * 512]
                        last = pe.matmul(ps[:, j % 2, :], s.xT[:, dc, st * P:(st + 1) * P], rhs,
                                         start=dc == 0, stop=dc == DC - 1)
                    last.then_inc(pr_ps, 1)
                    if kind == "k":
                        for dc in range(DC):
                            last = pe.matmul(ps[:, 2 + st, :], s.xT[:, dc, st * P:(st + 1) * P], wv_s[:, dc, :],
                                             start=dc == 0, stop=dc == DC - 1)
                        last.then_inc(v_ps, 1)

                def turn(j):
                    pe.wait_ge(rot_ready, at(i, NT, j + 1))
                    if j >= 2:
                        pe.wait_ge(turned, at(i, NT, j - 1))
                    for q in range(4):
                        last = pe.transpose(ps[:, TB[j % 2], q * P:(q + 1) * P], rot[j % 2][:, q * P:(q + 1) * P],
                                            ident[:])
                    last.then_inc(turn_ps, 1)

                def scores(n):
                    a, q, j = nh(n)
                    if n >= 4:
                        pe.wait_ge(sc_read, at(i, NH * ST, ST * (n - 3)))
                    for st in range(ST):
                        last = pe.matmul(ps[:, n % 4, st * P:st * P + (st + 1) * P],
                                         qT[j * HD:(j + 1) * HD, st, G * a + q, :],
                                         kT[j * HD:(j + 1) * HD, a, 0:(st + 1) * P], start=True, stop=True)
                    last.then_inc(sc_ps, 1)

                def turn_probs(n):
                    pe.wait_ge(exp_done, at(i, NH, n + 1))
                    if n >= 2:
                        pe.wait_ge((t_act, t_dve)[n % 2], at(i, NH // 2, n // 2))
                    for q in range(3):
                        last = pe.transpose(ps[:, TB[n % 2], q * P:(q + 1) * P], sc[n % 4][:, q * P:(q + 1) * P],
                                            ident[:])
                    last.then_inc(t_ps, 1)

                def mix(n):
                    a, q, j = nh(n)
                    kv = 2 * a + j
                    out = lambda st: ps[:, OB[n // G % 2], (n % G * ST + st) * HD:(n % G * ST + st + 1) * HD]
                    pe.wait_ge((t_act, t_dve)[n % 2], at(i, NH // 2, n // 2 + 1))
                    if n % G == 0 and n >= 2 * G:
                        pe.wait_ge(o_ready, at(i, GROUPS, n // G - 1))
                    pe.matmul(out(0), pT[n % 2][:, 0:P], v[:, 0, kv * HD:(kv + 1) * HD], start=True, stop=True)
                    pe.matmul(out(1), pT[n % 2][:, P:2 * P], v[:, 0, kv * HD:(kv + 1) * HD], start=True, stop=False)
                    pe.matmul(out(1), pT[n % 2][:, 2 * P:W3], v[:, 1, kv * HD:(kv + 1) * HD], start=False,
                              stop=True).then_inc(o_ps, 1)

                s.transpose_x(pe, i, ps[:, XB, :])
                pe.wait_ge(s.xT_ready, at(i, 1, 1))
                for j in range(NT + LAG):
                    if j < NT:
                        project(j)
                    if j >= LAG:
                        turn(j - LAG)
                pe.wait_ge(turned, at(i, NT, NT))
                pe.wait_ge(v_ready, at(i, ST, ST))
                for n in range(-3, NH):
                    if n + 3 < NH:
                        scores(n + 3)
                    if n >= 0:
                        turn_probs(n)
                    if n >= 1:
                        mix(n - 1)
                mix(NH - 1)
                pe.wait_ge(o_ready, at(i, GROUPS, GROUPS))
                for t in range(ST * PAIRS // 4):
                    st, p0 = divmod(4 * t, PAIRS)
                    if t >= 2:
                        pe.wait_ge(oT_ready, at(i, ST * PAIRS // 4, t - 1))
                    for q in range(4):
                        last = pe.transpose(ps[:, TB[t % 2], q * P:(q + 1) * P],
                                            o[:, st, (p0 + q) * P:(p0 + q + 1) * P], ident[:])
                    last.then_inc(oT_ps, 1)
                for st in range(ST):
                    pe.wait_ge(oT_ready, at(i, ST * PAIRS // 4, (st + 1) * PAIRS // 4))
                    for p in range(PAIRS):
                        last = pe.matmul(ps[:, 0, st * D:(st + 1) * D], oT[:, st, p, :], wo_s[:, p, :],
                                         start=p == 0, stop=p == PAIRS - 1)
                last.then_inc(y_ps, 1)

        @block.scalar
        def _(act):
            act.wait_ge(const_ready, 2)
            with act.Fori(0, B) as i:
                s.copy_xT(act, i, ps[:, XB, :])
                for j, (kind, st, a) in enumerate(tiles):
                    act.wait_ge(turn_ps, at(i, NT, j + 1))
                    if kind == "k":
                        act.copy(kT[:, :, st * P:(st + 1) * P], ps[:, TB[j % 2], :].rearrange("p (a e) -> p a e", a=NA))\
                           .then_inc(turned, 1)
                    else:
                        for q in range(G):
                            last = act.activation(qT[:, st, G * a + q, :], ps[:, TB[j % 2], q * P:(q + 1) * P],
                                                  ACT.Copy, scale=kw[:, G * a + q:G * a + q + 1])
                        last.then_inc(turned, 1)

                def exp(n):
                    act.wait_ge(nmx_ready, at(i, NH, n + 1))
                    for st in range(ST):
                        part = sc[n % 4][:, st * P:st * P + (st + 1) * P]
                        last = act.activation(part, part, ACT.Exp, bias=nmx[:, n % 4, st:st + 1],
                                              accum_out=sums[:, n, st:st + 1])
                    last.then_inc(exp_done, 1)

                exp(0)
                for n in range(NH):
                    if n + 1 < NH:
                        exp(n + 1)
                    if n % 2 == 0:
                        if n >= 2:
                            act.wait_ge(o_ps, at(i, NH, n - 1))
                        act.wait_ge(t_ps, at(i, NH, n + 1))
                        act.copy(pT[0][:], ps[:, TB[0], 0:W3]).then_inc(t_act, 1)
                for t in range(ST * PAIRS // 4):
                    st, p0 = divmod(4 * t, PAIRS)
                    act.wait_ge(oT_ps, at(i, ST * PAIRS // 4, t + 1))
                    act.copy(oT[:, st, p0:p0 + 4, :].rearrange("p q s -> p (q s)"), ps[:, TB[t % 2], :])\
                       .then_inc(oT_ready, 1)

        @block.vector
        def _(dve):
            s.credits(dve)
            dve.wait_ge(w_loaded, W_ALL)
            dve.wait_ge(const_ready, 1)
            own0 = Chain(dve, s.own2)
            dve.tensor_scalar(nsin[:], sin[:], -1.0, None, ALU.mult)
            own0(dve.tensor_scalar(kw[:], kw[:], float(HD) ** -0.5, None, ALU.mult))
            dve.sem_inc(const_ready, 1)
            with dve.Fori(0, B) as i:
                own = Chain(dve, dve_own, NH // G, i)

                def biased(j):
                    kind, st, a = tiles[j]
                    dve.wait_ge(pr_ps, at(i, NT, j + 1))
                    if j >= 2:
                        dve.wait_ge(byc_ready, at(i, NT, j - 1))
                    dve.tensor_tensor(raw[j % 2][:], ps[:, j % 2, :],
                                      bk_s[:] if kind == "k" else bq_s[:, a * 512:(a + 1) * 512], ALU.add)\
                       .then_inc(raw_ready, 1)
                    if kind == "k":
                        dve.wait_ge(v_ps, at(i, ST, st + 1))
                        dve.tensor_tensor(v[:, st, :], ps[:, 2 + st, :], bv_s[:], ALU.add).then_inc(v_ready, 1)

                def rotate(j):
                    kind, st, a = tiles[j]
                    x = raw[j % 2][:].rearrange("p (h t e) -> p h t e", t=2, e=HALF)
                    y = bys[:].rearrange("p (h t e) -> p h t e", t=2, e=HALF)
                    dve.wait_ge(raw_ready, at(i, NT, j + 1))
                    if j >= 1:
                        dve.wait_ge(rot_ready, at(i, NT, j))
                    for half, table in ((0, nsin), (1, sin)):
                        last = dve.tensor_tensor(y[:, :, half, :], x[:, :, 1 - half, :],
                                                 table[:, st, :].unsqueeze(1).to_broadcast([P, 8, HALF]), ALU.mult)
                    last.then_inc(bys_ready, 1)
                    dve.wait_ge(bys_ready, at(i, NT, j + 1))
                    dve.wait_ge(byc_ready, at(i, NT, j + 1))
                    if j >= 2:
                        dve.wait_ge(turn_ps, at(i, NT, j - 1))
                    dve.tensor_tensor(rot[j % 2][:], byc[j % 2][:], bys[:], ALU.add).then_inc(rot_ready, 1)

                biased(0)
                for j in range(NT):
                    if j + 1 < NT:
                        biased(j + 1)
                    rotate(j)

                def maxima(n):
                    dve.wait_ge(sc_ps, at(i, NH, n + 1))
                    if n >= 4:
                        dve.wait_ge(t_ps, at(i, NH, n - 3))
                    for st in range(ST):
                        a, b = st * P, st * P + (st + 1) * P
                        s.carry(dve)
                        dve.tensor_tensor_reduce(sc[n % 4][:, a:b], ps[:, n % 4, a:b], cm[:, a:b], 1.0, -3.0e38,
                                                 ALU.add, ALU.max, mx[:, n % 4, st:st + 1]).then_inc(sc_read, 1)
                    dve.wait_ge(sc_read, at(i, NH * ST, ST * n + ST))
                    dve.tensor_scalar(nmx[:, n % 4, :], mx[:, n % 4, :], -1.0, None, ALU.mult).then_inc(nmx_ready, 1)

                def outputs(g):
                    dve.wait_ge(exp_done, at(i, NH, G * g + G))
                    if g >= 1:
                        dve.wait_ge(o_ready, at(i, GROUPS, g))
                    own(dve.reciprocal(rs[:], sums[:, G * g:G * g + G, :].rearrange("p n s -> p (n s)")))
                    dve.wait_ge(o_ps, at(i, NH, G * g + G))
                    dve.tensor_tensor(
                        o[:, :, G * g * HD:(G * g + G) * HD].rearrange("p s (n d) -> p n s d", n=G),
                        ps[:, OB[g % 2], :].rearrange("p (n s d) -> p n s d", n=G, s=ST),
                        rs[:].rearrange("p (n s) -> p n s", n=G).unsqueeze(3).to_broadcast([P, G, ST, HD]),
                        ALU.mult).then_inc(o_ready, 1)

                for n in range(-2, NH + 2):
                    if 0 <= n + 2 < NH:
                        maxima(n + 2)
                    if 0 <= n < NH and n % 2 == 1:
                        if n >= 2:
                            dve.wait_ge(o_ps, at(i, NH, n - 1))
                        dve.wait_ge(t_ps, at(i, NH, n + 1))
                        dve.tensor_copy(pT[1][:], ps[:, TB[1], 0:W3]).then_inc(t_dve, 1)
                    if n >= G and n % G == 1:
                        outputs(n // G - 1)
                dve.tensor_tensor(zb[:], s.xb[:], bo_s[:].unsqueeze(1).to_broadcast([P, ST, D]), ALU.add)\
                   .then_inc(zb_ready, 1)
                dve.wait_ge(zb_ready, at(i, 1, 1))
                dve.wait_ge(y_ps, at(i, 1, 1))
                dve.tensor_tensor(s.z[:].rearrange("p s d -> p (s d)"), ps[:, 0, :],
                                  zb[:].rearrange("p s d -> p (s d)"), ALU.add).then_inc(s.x_free, 1)
                s.norm_dve(dve, i)
    s.close()


def routed_stage(k, x_in, x_out, router, w1, b1, w2, b2):
    nc, ps, ident = k.nc, k.ps, k.ident
    E, CAP, K = router.shape[1], 64, 2
    F = w1.shape[1]
    FC = F // P
    NT = B * ST
    s = Stage(k, "route", x_in, x_out)
    rw, w1_s, w2_s = s.sb("rw", [P, DC, E]), s.sb("w1", [P, DC, F]), s.sb("w2", [P, FC, D])
    b1_s, b2_s = s.sb("b1", [P, FC]), s.sb("b2", [P, D])
    hT = s.sb("hT", [P, FC, S])
    y = s.sb("y", [P, ST, D])
    lg = s.sb("lg", [P, ST, E])
    lgs = s.sb("lgs", [P, NT, E])
    pref = s.sb("pref", [P, E])
    prefi = s.sb("prefi", [P, E], I32)
    upto, ones = s.sb("upto", [P, P]), s.sb("ones", [P, P])
    reset = s.sb("reset", [P, E, K * NT])
    pick = s.sb("pick", [P, K, NT, E])
    rank = s.sb("rank", [P, K * NT, E])
    total, before = s.sb("total", [P, E, K * NT]), s.sb("before", [P, E, K * NT])
    tmp, pw = s.sb("tmp", [P, NT, E]), s.sb("pw", [P, NT, E])
    m1, m2, den, w = s.sb("m1", [P, NT]), s.sb("m2", [P, NT]), s.sb("den", [P, NT]), s.sb("w", [P, NT])
    wb = s.sb("wb", [P, ST])
    (w_loaded, const_ready, h_ps, hT_ready, y_ps, y_ready, y_stored, lg_ps, lg_ready, lg_moved, ch, ex, rank_ps,
     w_ready, wb_loaded, y_loaded) = (s.sem(n) for n in (
        "w_loaded", "const_ready", "h_ps", "hT_ready", "y_ps", "y_ready", "y_stored", "lg_ps", "lg_ready",
        "lg_moved", "ch", "ex", "rank_ps", "w_ready", "wb_loaded", "y_loaded"))
    y_dram = nc.dram_tensor("mlp_rows", [B, P, ST * D], F32, kind="Internal").ap()
    XB, YB, LB = 5, 6, 7

    with nc.Block() as block:
        @block.sync
        def _(sp):
            sp.dma_start(rw[:], router.rearrange("(c p) n -> p c n", p=P)).then_inc(w_loaded, 16)
            sp.dma_start(w1_s[:], w1.rearrange("(c p) n -> p c n", p=P)).then_inc(w_loaded, 16)
            sp.dma_start(w2_s[:], w2.rearrange("(c p) n -> p c n", p=P)).then_inc(w_loaded, 16)
            sp.dma_start(b1_s[:], b1).then_inc(w_loaded, 16)
            sp.dma_start(b2_s[:], b2.partition_broadcast(P)).then_inc(w_loaded, 16)

            def keep(i):
                sp.wait_ge(lg_ready, at(i, 1, 1))
                s.carry(sp)
                sp.dma_start(lgs[:, bass.ds(i * ST, ST), :], lg[:]).then_inc(lg_moved, 16)
                sp.wait_ge(y_ready, at(i, 1, 1))
                sp.dma_start(one(y_dram, i), y[:].rearrange("p s d -> p (s d)")).then_inc(y_stored, 16)

            s.load_x(sp, 0)
            with sp.Fori(0, B - 1) as i:
                s.load_x(sp, i + 1)
                keep(i)
            keep(B - 1)
            sp.wait_ge(y_stored, 16 * (B + 1))

        @block.gpsimd
        def _(pool):
            own = Chain(pool, s.pool_own)
            pool.memset(ones[:], 1.0)
            pool.memset(upto[:], 1.0)
            pool.memset(reset[:], 1.0)
            own(pool.iota(prefi[:], [[-1, E]], base=E, channel_multiplier=0))
            pool.affine_select(out=upto[:], in_=upto[:], compare_op=ALU.is_ge, fill=0.0, base=0, pattern=[[1, P]],
                               channel_multiplier=-1)
            own(pool.memset(reset[:, :, 0:1], 0.0))
            pool.sem_inc(const_ready, 1)

        @block.tensor
        def _(pe):
            pe.wait_ge(w_loaded, 16 * 5)
            pe.wait_ge(const_ready, 1)
            with pe.Fori(0, B) as i:
                s.transpose_x(pe, i, ps[:, XB, :])
                pe.wait_ge(s.xT_ready, at(i, 1, 1))
                for st in range(ST):
                    for dc in range(DC):
                        last = pe.matmul(ps[:, LB, st * E:(st + 1) * E], s.xT[:, dc, st * P:(st + 1) * P],
                                         rw[:, dc, :], start=dc == 0, stop=dc == DC - 1)
                last.then_inc(lg_ps, 1)
                for f in range(FC):
                    if f >= 4:
                        pe.wait_ge(hT_ready, at(i, FC, f - 3))
                    for dc in range(DC):
                        last = pe.matmul(ps[:, f % 4, 0:S], w1_s[:, dc, f * P:(f + 1) * P], s.xT[:, dc, :],
                                         start=dc == 0, stop=dc == DC - 1)
                    last.then_inc(h_ps, 1)
                for st in range(ST):
                    for f in range(FC):
                        if st == 0:
                            pe.wait_ge(hT_ready, at(i, FC, f + 1))
                        last = pe.matmul(ps[:, YB, st * D:(st + 1) * D], hT[:, f, st * P:(st + 1) * P], w2_s[:, f, :],
                                         start=f == 0, stop=f == FC - 1)
                last.then_inc(y_ps, 1)

        @block.scalar
        def _(act):
            act.wait_ge(w_loaded, 16 * 5)
            with act.Fori(0, B) as i:
                s.copy_xT(act, i, ps[:, XB, :])
                for f in range(FC):
                    act.wait_ge(h_ps, at(i, FC, f + 1))
                    act.activation(hT[:, f, :], ps[:, f % 4, 0:S], ACT.Gelu, bias=b1_s[:, f:f + 1]).then_inc(hT_ready, 1)

        @block.vector
        def _(dve):
            dve.sem_inc(s.x_free, 1)
            dve.sem_inc(lg_moved, 16)
            dve.sem_inc(y_stored, 16)
            dve.wait_ge(w_loaded, 16 * 5)
            dve.wait_ge(const_ready, 1)
            dve.tensor_copy(pref[:], prefi[:])
            with dve.Fori(0, B) as i:
                dve.wait_ge(lg_ps, at(i, 1, 1))
                dve.wait_ge(lg_moved, at(i, 16, 16))
                dve.tensor_copy(lg[:].rearrange("p s e -> p (s e)"), ps[:, LB, 0:ST * E]).then_inc(lg_ready, 1)
                dve.wait_ge(y_ps, at(i, 1, 1))
                dve.wait_ge(y_stored, at(i, 16, 16))
                dve.tensor_tensor(y[:], ps[:, YB, :].rearrange("p (s d) -> p s d", s=ST),
                                  b2_s[:].unsqueeze(1).to_broadcast([P, ST, D]), ALU.add).then_inc(y_ready, 1)
                dve.wait_ge(y_ready, at(i, 1, 1))
                dve.sem_inc(s.x_free, 1)

    all_e = lambda t_: t_[:].unsqueeze(2).to_broadcast([P, NT, E])
    with nc.Block() as block:
        @block.tensor
        def _(pe):
            pe.wait_ge(w_ready, 1)
            picks = pick[:].rearrange("p k t e -> p (k t e)")
            pe.matmul(ps[:, 0, 0:K * NT * E], upto[:], picks, start=True, stop=True)
            pe.matmul(ps[:, 1, 0:K * NT * E], ones[:], picks, start=True, stop=True).then_inc(rank_ps, 1)

        @block.scalar
        def _(act):
            act.wait_ge(ex, 1)
            act.activation(lgs[:], lgs[:], ACT.Exp).then_inc(ex, 1)

        @block.vector
        def _(dve):
            own = Chain(dve, ch)
            own(dve.tensor_reduce(m1[:], lgs[:], AX_X, ALU.max))
            own(dve.tensor_tensor(lgs[:], lgs[:], all_e(m1), ALU.subtract))
            dve.sem_inc(ex, 1)
            dve.wait_ge(ex, 2)
            own(dve.tensor_reduce(den[:], lgs[:], AX_X, ALU.add))
            own(dve.reciprocal(den[:], den[:]))
            own(dve.tensor_tensor(lgs[:], lgs[:], all_e(den), ALU.mult))
            own(dve.tensor_copy(pw[:], lgs[:]))
            for c in range(K):
                own(dve.tensor_reduce(m1[:], pw[:], AX_X, ALU.max))
                own(dve.tensor_tensor(tmp[:], pw[:], all_e(m1), ALU.is_equal))
                own(dve.tensor_tensor(tmp[:], tmp[:], pref[:].unsqueeze(1).to_broadcast([P, NT, E]), ALU.mult))
                own(dve.tensor_reduce(m2[:], tmp[:], AX_X, ALU.max))
                own(dve.tensor_tensor(pick[:, c], tmp[:], all_e(m2), ALU.is_equal))
                own(dve.scalar_tensor_tensor(pw[:], pick[:, c], -4.0, pw[:], ALU.mult, ALU.add))
            dve.sem_inc(w_ready, 1)
            dve.wait_ge(rank_ps, 1)
            own(dve.tensor_copy(total[:], ps[:, 1, 0:K * NT * E].rearrange("p (t e) -> p e t", e=E)))
            own(dve.tensor_tensor_scan(before[:].rearrange("p e t -> p (e t)"), reset[:].rearrange("p e t -> p (e t)"),
                                       total[:].rearrange("p e t -> p (e t)"), 0.0, ALU.mult, ALU.add))
            own(dve.tensor_tensor(before[:], before[:], total[:], ALU.subtract))
            own(dve.tensor_tensor(rank[:], ps[:, 0, 0:K * NT * E].rearrange("p (t e) -> p t e", e=E),
                                  before[:].rearrange("p e t -> p t e"), ALU.add))
            own(dve.scalar_tensor_tensor(rank[:].rearrange("p t e -> p (t e)"), rank[:].rearrange("p t e -> p (t e)"),
                                         CAP + 0.5, pick[:].rearrange("p k t e -> p (k t e)"), ALU.is_lt, ALU.mult))
            kept = rank[:].rearrange("p (k t) e -> p k t e", k=K)
            own(dve.tensor_tensor(tmp[:], kept[:, 0], kept[:, 1], ALU.add))
            own(dve.tensor_tensor(tmp[:], tmp[:], lgs[:], ALU.mult))
            own(dve.tensor_reduce(w[:], tmp[:], AX_X, ALU.add))

    x2, y2 = s.sb("x2", [P, ST, D]), s.sb("y2", [P, ST, D])
    in2, free2 = s.sem("in2"), s.sem("free2")
    with nc.Block() as block:
        @block.sync
        def _(sp):
            def rows(i):
                sp.wait_ge(free2, at(i, 1, 1))
                s.carry(sp)
                sp.dma_start(x2[:], one(s.x_in, i)).then_inc(in2, 16)
                sp.dma_start(y2[:].rearrange("p s d -> p (s d)"), one(y_dram, i)).then_inc(in2, 16)
                sp.dma_start(wb[:], w[:, bass.ds(i * ST, ST)]).then_inc(in2, 16)

            rows(0)
            with sp.Fori(0, B - 1) as i:
                rows(i + 1)
                s.store_x(sp, i)
            s.store_x(sp, B - 1)
            sp.wait_ge(s.xo_stored, 16 * (B + 1))

        @block.gpsimd
        def _(pool):
            with pool.Fori(0, B) as i:
                s.norm_pool(pool, i)

        @block.vector
        def _(dve):
            dve.sem_inc(free2, 1)
            dve.sem_inc(s.xo_stored, 16)
            with dve.Fori(0, B) as i:
                own = Chain(dve, s.own2, 1, i)
                dve.wait_ge(in2, at(i, 48, 48))
                for st in range(ST):
                    last = dve.scalar_tensor_tensor(s.z[:, st, :], y2[:, st, :], wb[:, st:st + 1], x2[:, st, :],
                                                    ALU.mult, ALU.add)
                own(last)
                dve.sem_inc(free2, 1)
                s.norm_dve(dve, i, wait=False)
    s.close()


class Kernel:

    def __init__(self, nc, ctx):
        self.nc = nc
        self.ps = ctx.enter_context(nc.psum_tensor("ps", [P, 8, BANK], F32))
        self.ident = ctx.enter_context(nc.sbuf_tensor("ident", [P, P], F32))
        self.neg_half = ctx.enter_context(nc.sbuf_tensor("neg_half", [P, 64], F32))
        const = ctx.enter_context(nc.semaphore("common_consts"))
        with nc.Block() as block:
            @block.gpsimd
            def _(pool):
                own = Chain(pool, const)
                pool.memset(self.neg_half[:], -0.5)
                own(pool.memset(self.ident[:], 0.0))
                own(pool.affine_select(out=self.ident[:], in_=self.ident[:], compare_op=ALU.not_equal, fill=1.0,
                                       base=0, pattern=[[-1, P]], channel_multiplier=1))


STAGES = [
    (gla_stage, ["gla_wq", "gla_wk", "gla_wv", "gla_wo", "gla_nw"]),
    (cross_stage, ["ctxT", "mask", "x_wq", "x_bq", "x_wk", "x_bk", "x_wv", "x_bv", "x_wo", "x_qn", "x_kn"]),
    (experts_stage, ["e_gate", "e_gu", "e_dn", "e_merge", "e_dom"]),
    (rotary_stage, ["r_wq", "r_bq", "r_wk", "r_bk", "r_wv", "r_bv", "r_wo", "r_bo", "r_kw", "r_cos", "r_sin"]),
    (memory_stage, ["ctxT", "ctx", "kept"]),
    (routed_stage, ["m_router", "m_w1", "m_b1", "m_w2", "m_b2"]),
]


def layout(**a):
    c = np.ascontiguousarray
    T = lambda w: c(np.asarray(w).T)


    def pairs(w):
        w = np.asarray(w)
        return w.reshape(4, 2, 4, w.shape[0] // 32, -1).transpose(0, 2, 1, 3, 4).reshape(w.shape)

    inv = (1.0 / np.power(np.float32(10000.0), np.arange(0, 64, 2, dtype=np.float32) / np.float32(64))).astype(np.float32)
    angle = (np.arange(S, dtype=np.float32)[:, None] * inv[None, :]).astype(np.float32)
    return {
        "x": c(a["x"]).reshape(B * S, D),
        "gla_wq": T(a["L0_attn_Wq"]), "gla_wk": T(a["L0_attn_Wk"]), "gla_wv": T(a["L0_attn_Wv"]),
        "gla_wo": T(a["L0_attn_Wo"]), "gla_nw": c(np.asarray(a["L0_attn_norm_w"]).reshape(2, P).T),
        "ctx": c(a["ctx_2048"]), "ctxT": c(np.asarray(a["ctx_2048"]).transpose(0, 2, 1)),
        "mask": c(a["mask_1xSxS2_ff0"])[0],
        "x_wq": c(a["L0_xattn_Wq"]), "x_bq": c(a["L0_xattn_bq"]), "x_wk": c(a["L0_xattn_Wk"]),
        "x_bk": c(a["L0_xattn_bk"]), "x_wv": c(a["L0_xattn_Wv"]), "x_bv": c(a["L0_xattn_bv"]),
        "x_wo": c(a["L0_xattn_Wo"]), "x_qn": c(a["L0_xattn_qn_w"]).reshape(P, 1),
        "x_kn": c(a["L0_xattn_kn_w"]).reshape(P, 1),
        "e_gate": T(a["L0_ffn_gate_weight"]), "e_gu": c(np.asarray(a["L0_ffn_gate_up_proj"]).transpose(0, 2, 1)),
        "e_dn": c(np.asarray(a["L0_ffn_down_proj"]).transpose(0, 2, 1)),
        "e_merge": c(a["L0_ffn_merge_groups"]).reshape(-1, 1), "e_dom": c(a["L0_ffn_dominant_experts"]).reshape(1, -1),
        "r_wq": T(pairs(a["L1_attn_Wq"])), "r_bq": c(pairs(a["L1_attn_bq"])), "r_wk": T(a["L1_attn_Wk"]),
        "r_bk": c(a["L1_attn_bk"]), "r_wv": T(a["L1_attn_Wv"]), "r_bv": c(a["L1_attn_bv"]),
        "r_wo": c(pairs(np.asarray(a["L1_attn_Wo"]).T)), "r_bo": c(a["L1_attn_bo"]), "r_kw": c(pairs(a["L1_attn_key_weights"]).reshape(-1, 2).T),
        "r_cos": np.cos(angle), "r_sin": np.sin(angle),
        "m_router": T(a["L1_ffn_router_w"]), "m_w1": T(a["L1_ffn_w1"]),
        "m_b1": c(np.asarray(a["L1_ffn_b1"]).reshape(-1, P).T), "m_w2": T(a["L1_ffn_w2"]), "m_b2": c(a["L1_ffn_b2"]),
        "kept": c(a["mask_BxS2_bk0"]),
    }


_OUT = "out"


def build(nc, ap):
    with ExitStack() as ctx:
        k = Kernel(nc, ctx)
        rows = ap["x"]
        for n, (stage, names) in enumerate(STAGES):
            after = ap[_OUT] if n == len(STAGES) - 1 else \
                nc.dram_tensor(f"rows_{n + 1}", [B * S, D], F32, kind="Internal").ap()
            stage(k, rows, after, *[ap[name] for name in names])
            rows = after


def kernel(**inputs):
    import concourse.bacc as bacc
    from concourse.bass_utils import run_bass_kernel_spmd

    nc = bacc.Bacc("TRN2", target_bir_lowering=False, num_devices=1)
    arrays = layout(**inputs)
    ap = {name: nc.dram_tensor(name, a.shape, mybir.dt.from_np(a.dtype), kind="ExternalInput").ap()
          for name, a in arrays.items()}
    ap[_OUT] = nc.dram_tensor(_OUT, [B * S, D], F32, kind="ExternalOutput").ap()
    build(nc, ap)
    result = run_bass_kernel_spmd(nc, [arrays], core_ids=[0])
    return result.results[0][_OUT].reshape(B, S, D)
```

```python
from contextlib import ExitStack

import numpy as np

import concourse.bass as bass
from concourse import mybir

F32 = mybir.dt.float32
F16 = mybir.dt.float16
I32 = mybir.dt.int32
U8 = mybir.dt.uint8
ALU = mybir.AluOpType
ACT = mybir.ActivationFunctionType
AX_X = mybir.AxisListType.X

P = 128
B = 8
S = 256
D = 256
ST = S // P
DC = D // P
BANK = 512
LN_EPS = 1e-5
RMS_EPS = 1e-6


def at(i, per_iteration, k):
    return i * per_iteration + k


def one(ap, i):
    return ap[bass.ds(i, 1)].squeeze(0)


class Chain:

    def __init__(self, eng, sem, per=0, i=None):
        self.eng, self.sem, self.per, self.i, self.k = eng, sem, per, i, 0

    def __call__(self, ins):
        self.k += 1
        ins.then_inc(self.sem, 1)
        self.eng.wait_ge(self.sem, self.k if self.i is None else at(self.i, self.per, self.k))

    def end(self):
        assert self.i is None or self.k == self.per, self.k


class Stage:

    def __init__(self, k, name, x_in, x_out):
        self.k, self.nc, self.name = k, k.nc, name
        self.ctx, self.sems = ExitStack(), []
        self.x_in = x_in.rearrange("(b s p) d -> b p s d", s=ST, p=P)
        self.x_out = x_out.rearrange("(b s p) d -> b p s d", s=ST, p=P)
        self.xb = self.sb("xb", [P, ST, D])
        self.xr = self.sb("xr", [P, ST, D])
        self.xT = self.sb("xT", [P, DC, S])
        self.z = self.sb("z", [P, ST, D])
        self.xo = self.sb("xo", [P, ST, D])
        self.bn = self.sb("bn", [P, ST, 6])
        self.mv = self.sb("mv", [P, ST, 2])
        self.ve = self.sb("ve", [P, ST])
        self.rstd = self.sb("rstd", [P, ST])
        self.x_loaded = self.sem("x_loaded")
        self.x_kept = self.sem("x_kept")
        self.z_made = self.sem("z_made")
        self.xT_ps = self.sem("xT_ps")
        self.xT_ready = self.sem("xT_ready")
        self.var_ready = self.sem("var_ready")
        self.rstd_ready = self.sem("rstd_ready")
        self.xo_ready = self.sem("xo_ready")
        self.xo_stored = self.sem("xo_stored")
        self.pool_own = self.sem("pool_own")
        self.ln_own = self.sem("ln_own")
        self.fence = self.sem("fence")
        self.own2 = self.sem("own2")

    def sb(self, name, shape, dt=F32):
        return self.ctx.enter_context(self.nc.sbuf_tensor(f"{self.name}_{name}_sb", shape, dt))

    def sem(self, name):
        self.sems.append(self.nc.alloc_semaphore(name=f"{self.name}_{name}"))
        return self.sems[-1]

    def close(self):
        self.nc.clear_and_free_semaphores(self.sems)
        self.nc.all_engine_barrier()
        self.ctx.close()

    def carry(self, dve):
        dve.sem_inc(self.fence, 1)

    def load_x(self, sp, i, keeps=True):
        if not isinstance(i, int):
            sp.wait_ge(self.xT_ps, at(i, 1, 0))
            if keeps:
                sp.wait_ge(self.x_kept, at(i, 1, 0))
        sp.dma_start(self.xb[:], one(self.x_in, i)).then_inc(self.x_loaded, 16)

    def store_x(self, sp, i):
        sp.wait_ge(self.xo_ready, at(i, 1, 1))
        sp.dma_start(one(self.x_out, i), self.xo[:]).then_inc(self.xo_stored, 16)

    def rows_dma(self, sp, more=None):
        if more:
            more(0)
        self.load_x(sp, 0)
        with sp.Fori(0, B - 1) as i:
            self.load_x(sp, i + 1)
            if more:
                more(i + 1)
            self.store_x(sp, i)
        self.store_x(sp, B - 1)
        sp.wait_ge(self.xo_stored, 16 * (B + 1))

    def keep_x(self, pool, i, bias=None):
        pool.wait_ge(self.x_loaded, at(i, 16, 16))
        pool.wait_ge(self.z_made, at(i, 1, 1))
        if bias is None:
            self.carry(pool)
            pool.tensor_copy(self.xr[:], self.xb[:]).then_inc(self.x_kept, 1)
        else:
            pool.tensor_tensor(self.xr[:], self.xb[:], bias.unsqueeze(1).to_broadcast([P, ST, D]), ALU.add)\
                .then_inc(self.x_kept, 1)

    def transpose_x(self, pe, i, ps):
        pe.wait_ge(self.x_loaded, at(i, 16, 16))
        for dc in range(DC):
            for st in range(ST):
                last = pe.transpose(ps[:, dc * S + st * P:dc * S + (st + 1) * P],
                                    self.xb[:, st, dc * P:(dc + 1) * P], self.k.ident[:])
        last.then_inc(self.xT_ps, 1)

    def copy_xT(self, act, i, ps):
        act.wait_ge(self.xT_ps, at(i, 1, 1))
        act.copy(self.xT[:].rearrange("p c s -> p (c s)"), ps).then_inc(self.xT_ready, 1)

    def credits(self, dve):
        dve.sem_inc(self.z_made, 1)
        dve.sem_inc(self.xo_stored, 16)

    def each_sequence(self, dve, sequence):
        sequence(0, None)
        with dve.Fori(0, B - 1) as i:
            sequence(i + 1, i)
        self.norm_dve(dve, B - 1)

    def norm_before(self, dve, before):
        if before is not None:
            self.norm_dve(dve, before)

    def norm_dve(self, dve, i, wait=True):
        if wait:
            dve.wait_ge(self.z_made, at(i, 1, 2))
        own = Chain(dve, self.ln_own, 3, i)
        for st in range(ST - 1):
            dve.bn_stats(self.bn[:, st, :], self.z[:, st, :])
        own(dve.bn_stats(self.bn[:, ST - 1, :], self.z[:, ST - 1, :]))
        self.carry(dve)
        for st in range(ST - 1):
            dve.bn_aggr(self.mv[:, st, :], self.bn[:, st, :])
        own(dve.bn_aggr(self.mv[:, ST - 1, :], self.bn[:, ST - 1, :]))
        dve.tensor_scalar(self.ve[:], self.mv[:, :, 1], LN_EPS, None, ALU.add).then_inc(self.var_ready, 1)
        dve.wait_ge(self.rstd_ready, at(i, 1, 1))
        dve.wait_ge(self.xo_stored, at(i, 16, 16))
        for st in range(ST):
            last = dve.tensor_scalar(self.xo[:, st, :], self.z[:, st, :], self.mv[:, st, 0:1],
                                     self.rstd[:, st:st + 1], ALU.subtract, ALU.mult)
        own(last)
        own.end()
        dve.nop().then_inc(self.xo_ready, 1)

    def norm_pool(self, pool, i):
        pool.wait_ge(self.var_ready, at(i, 1, 1))
        pool.tensor_tensor(self.rstd[:], self.ve[:], self.k.neg_half[:, 0:ST], ALU.pow).then_inc(self.rstd_ready, 1)


def gla_stage(k, x_in, x_out, wq, wk, wv, wo, norm_w):
    nc, ps, ident = k.nc, k.ps, k.ident
    H, CH = 2, 64
    NCH = S // CH
    s = Stage(k, "gla", x_in, x_out)
    W = {n: s.sb(n, [P, DC, D]) for n in ("wq", "wk", "wv", "wo")}
    nw = s.sb("nw", [P, H])
    keep = s.sb("keep", [P, P])
    reset = s.sb("reset", [P, H * S])
    ones = s.sb("ones", [P, 1])
    t = {n: s.sb(n, [P, H * S]) for n in ("eq", "ef", "qs", "f", "e2", "lf", "c", "kk", "dec", "grow", "qd", "kd",
                                          "kr", "ow", "sq")}
    v = s.sb("v", [P, ST, D])
    krn = s.sb("krn", [P, H * ST, P])
    scm = s.sb("scm", [P, H * ST, P])
    state = s.sb("state", [P, H, NCH - 1, P])
    ss = s.sb("ss", [P, ST])
    r = s.sb("r", [P, ST])
    w_loaded, const_ready = s.sem("w_loaded"), s.sem("const_ready")
    proj_ps, exps, silu, gates, cums, decays, decayed = (s.sem(n) for n in (
        "proj_ps", "exps", "silu", "gates", "cums", "decays", "decayed"))
    v_ready, sc_ps, sc_ready, kr_ps, kr_ready, st_ps, st_ready = (s.sem(n) for n in (
        "v_ready", "sc_ps", "sc_ready", "kr_ps", "kr_ready", "st_ps", "st_ready"))
    o_ps, o_ready, sq_ready, ss_ps, ss_ready, r_ready, y_ps, dve_own, act_own = (s.sem(n) for n in (
        "o_ps", "o_ready", "sq_ready", "ss_ps", "ss_ready", "r_ready", "y_ps", "dve_own", "act_own"))
    qps, fps, vps, scps, krps, ops, stps0, stps1 = (ps[:, n, :] for n in range(8))
    update = lambda h, c: (stps0, stps1)[c % 2][:, (c // 2 * H + h) * P:(c // 2 * H + h + 1) * P]
    xps, yps, ssps = vps, qps, fps

    with nc.Block() as block:
        @block.sync
        def _(sp):
            for n, w in (("wq", wq), ("wk", wk), ("wv", wv), ("wo", wo)):
                sp.dma_start(W[n][:], w.rearrange("(c p) n -> p c n", p=P)).then_inc(w_loaded, 16)
            sp.dma_start(nw[:], norm_w).then_inc(w_loaded, 16)
            s.rows_dma(sp)

        @block.gpsimd
        def _(pool):
            own = Chain(pool, s.pool_own)
            own(pool.memset(keep[:], 1.0))
            own(pool.affine_select(out=keep[:], in_=keep[:], compare_op=ALU.is_ge, fill=0.0, base=0,
                                   pattern=[[1, P]], channel_multiplier=-1))
            own(pool.memset(keep[0:CH, CH:P], 0.0))
            pool.memset(ones[:], 1.0)
            own(pool.memset(reset[:], 1.0))
            pool.memset(reset[:].rearrange("p (c n) -> p c n", n=CH)[:, :, 0:1], 0.0).then_inc(const_ready, 1)
            with pool.Fori(0, B) as i:
                s.keep_x(pool, i)
                pool.wait_ge(ss_ready, at(i, 1, 1))
                pool.tensor_tensor(r[:], ss[:], k.neg_half[:, 0:ST], ALU.pow).then_inc(r_ready, 1)
                s.norm_pool(pool, i)

        @block.tensor
        def _(pe):
            pe.wait_ge(w_loaded, 16 * 5)
            pe.wait_ge(const_ready, 1)
            with pe.Fori(0, B) as i:
                s.transpose_x(pe, i, xps)
                pe.wait_ge(s.z_made, at(i, 1, 1))
                pe.wait_ge(s.xT_ready, at(i, 1, 1))
                for out, w in ((qps, "wq"), (fps, "wk")):
                    for h in range(H):
                        for dc in range(DC):
                            last = pe.matmul(out[:, h * S:(h + 1) * S], W[w][:, dc, h * P:(h + 1) * P],
                                             s.xT[:, dc, :], start=dc == 0, stop=dc == DC - 1)
                    last.then_inc(proj_ps, 1)
                for st in range(ST):
                    for dc in range(DC):
                        last = pe.matmul(vps[:, st * D:(st + 1) * D], s.xT[:, dc, st * P:(st + 1) * P],
                                         W["wv"][:, dc, :], start=dc == 0, stop=dc == DC - 1)
                last.then_inc(proj_ps, 1)
                pe.wait_ge(decayed, at(i, 2, 1))
                for h in range(H):
                    for st in range(ST):
                        a = h * S + st * P
                        last = pe.matmul(scps[:, (h * ST + st) * P:(h * ST + st + 1) * P], t["kd"][:, a:a + P],
                                         t["qd"][:, a:a + P], start=True, stop=True)
                last.then_inc(sc_ps, 1)
                pe.wait_ge(decayed, at(i, 2, 2))
                for n in range(H * ST):
                    last = pe.transpose(krps[:, n * P:(n + 1) * P], t["kr"][:, n * P:(n + 1) * P], ident[:])
                last.then_inc(kr_ps, 1)
                pe.wait_ge(kr_ready, at(i, 1, 1))
                pe.wait_ge(v_ready, at(i, 1, 1))
                for c in range(NCH - 1):
                    for h in range(H):
                        a = (c % 2) * CH
                        last = pe.matmul(update(h, c), krn[a:a + CH, h * ST + c // 2, :],
                                         v[a:a + CH, c // 2, h * P:(h + 1) * P], start=True, stop=True)
                last.then_inc(st_ps, 1)
                pe.wait_ge(sc_ready, at(i, 1, 1))
                for h in range(H):
                    for st in range(ST):
                        n = h * ST + st
                        pe.matmul(ops[:, n * P:(n + 1) * P], v[:, st, h * P:(h + 1) * P], scm[:, n, :],
                                  start=n == 0, stop=False, skip_group_check=True)
                for c in range(1, NCH):
                    pe.wait_ge(st_ready, at(i, NCH - 1, c))
                    for h in range(H):
                        a = h * S + c * CH
                        last = pe.matmul(ops[:, a:a + CH], state[:, h, c - 1, :], t["qd"][:, a:a + CH],
                                         start=False, stop=True, skip_group_check=True)
                last.then_inc(o_ps, 1)
                pe.wait_ge(sq_ready, at(i, 1, 1))
                for st in range(ST):
                    for h in range(H):
                        last = pe.matmul(ssps[:, st:st + 1], t["sq"][:, h * S + st * P:h * S + (st + 1) * P],
                                         ones[:], start=h == 0, stop=h == H - 1)
                last.then_inc(ss_ps, 1)
                pe.wait_ge(o_ready, at(i, 1, 1))
                for st in range(ST):
                    for h in range(H):
                        last = pe.matmul(yps[:, st * D:(st + 1) * D], t["ow"][:, h * S + st * P:h * S + (st + 1) * P],
                                         W["wo"][:, h, :], start=h == 0, stop=h == H - 1)
                last.then_inc(y_ps, 1)

        @block.scalar
        def _(act):
            with act.Fori(0, B) as i:
                own = Chain(act, act_own, 2, i)
                s.copy_xT(act, i, xps)
                act.wait_ge(proj_ps, at(i, 3, 1))
                act.activation(t["eq"][:], qps, ACT.Exp, scale=-1.0).then_inc(exps, 1)
                act.wait_ge(proj_ps, at(i, 3, 2))
                act.activation(t["ef"][:], fps, ACT.Exp, scale=-1.0).then_inc(exps, 1)
                act.wait_ge(proj_ps, at(i, 3, 3))
                act.copy(v[:].rearrange("p s d -> p (s d)"), vps).then_inc(v_ready, 1)
                act.wait_ge(gates, at(i, 1, 1))
                own(act.activation(t["e2"][:], t["f"][:], ACT.Exp, scale=-1.0))
                act.activation(t["lf"][:], t["e2"][:], ACT.Ln, bias=1.0).then_inc(exps, 1)
                act.wait_ge(cums, at(i, 1, 1))
                act.activation(t["dec"][:], t["c"][:], ACT.Exp, scale=-1.0).then_inc(decays, 1)
                act.activation(t["grow"][:], t["c"][:], ACT.Exp).then_inc(decays, 1)
                act.wait_ge(kr_ps, at(i, 1, 1))
                act.copy(krn[:].rearrange("p n q -> p (n q)"), krps).then_inc(kr_ready, 1)
                act.wait_ge(o_ps, at(i, 1, 1))
                own(act.activation(t["sq"][:], ops, ACT.Square))
                act.nop().then_inc(sq_ready, 1)
                own.end()

        @block.vector
        def _(dve):
            s.credits(dve)
            dve.wait_ge(w_loaded, 16 * 5)
            dve.wait_ge(const_ready, 1)

            def sequence(i, before):
                own = Chain(dve, dve_own, 9, i)
                dve.wait_ge(exps, at(i, 3, 1))
                own(dve.tensor_scalar(t["eq"][:], t["eq"][:], 1.0, None, ALU.add))
                own(dve.reciprocal(t["eq"][:], t["eq"][:]))
                dve.tensor_tensor(t["qs"][:], qps, t["eq"][:], ALU.mult)
                dve.wait_ge(exps, at(i, 3, 2))
                own(dve.tensor_scalar(t["ef"][:], t["ef"][:], 1.0, None, ALU.add))
                dve.reciprocal(t["f"][:], t["ef"][:]).then_inc(gates, 1)
                s.norm_before(dve, before)
                dve.wait_ge(exps, at(i, 3, 3))
                dve.tensor_tensor_scan(t["c"][:], reset[:], t["lf"][:], 0.0, ALU.mult, ALU.add).then_inc(cums, 1)
                own(dve.tensor_scalar(t["kk"][:], t["e2"][:], 1.0, None, ALU.add))
                own(dve.reciprocal(t["kk"][:], t["kk"][:]))
                own(dve.tensor_tensor(t["kk"][:], t["kk"][:], t["e2"][:], ALU.mult))
                dve.wait_ge(decays, at(i, 2, 1))
                dve.tensor_tensor(t["qd"][:], t["qs"][:], t["dec"][:], ALU.mult)
                dve.wait_ge(decays, at(i, 2, 2))
                own(dve.tensor_tensor(t["kd"][:], t["kk"][:], t["grow"][:], ALU.mult))
                dve.nop().then_inc(decayed, 1)
                to_end = t["dec"][:].rearrange("p (c n) -> p c n", n=CH)[:, :, CH - 1:CH]
                dve.tensor_tensor(t["kr"][:].rearrange("p (c n) -> p c n", n=CH),
                                  t["kd"][:].rearrange("p (c n) -> p c n", n=CH),
                                  to_end.to_broadcast([P, H * NCH, CH]), ALU.mult).then_inc(decayed, 1)
                dve.wait_ge(sc_ps, at(i, 1, 1))
                dve.tensor_tensor(scm[:], scps.rearrange("p (n q) -> p n q", q=P),
                                  keep[:].unsqueeze(1).to_broadcast([P, H * ST, P]), ALU.mult).then_inc(sc_ready, 1)
                dve.wait_ge(st_ps, at(i, 1, 1))
                for c in range(NCH - 1):
                    for h in range(H):
                        new, u = state[:, h, c, :], update(h, c)
                        e = h * S + (c + 1) * CH - 1
                        if c == 0:
                            last = dve.tensor_copy(new, u)
                        else:
                            last = dve.scalar_tensor_tensor(new, state[:, h, c - 1, :], t["dec"][:, e:e + 1], u,
                                                            ALU.mult, ALU.add)
                    last.then_inc(st_ready, 1)
                    dve.wait_ge(st_ready, at(i, NCH - 1, c + 1))
                dve.wait_ge(sq_ready, at(i, 1, 1))
                for h in range(H):
                    last = dve.tensor_scalar(t["ow"][:, h * S:(h + 1) * S], ops[:, h * S:(h + 1) * S],
                                             nw[:, h:h + 1], None, ALU.mult)
                own(last)
                dve.nop().then_inc(o_ready, 1)
                dve.wait_ge(ss_ps, at(i, 1, 1))
                dve.tensor_scalar(ss[:], ssps[:, 0:ST], 1.0 / D, RMS_EPS, ALU.mult, ALU.add).then_inc(ss_ready, 1)
                dve.wait_ge(y_ps, at(i, 1, 1))
                dve.wait_ge(r_ready, at(i, 1, 1))
                dve.wait_ge(s.x_kept, at(i, 1, 1))
                for st in range(ST):
                    last = dve.scalar_tensor_tensor(s.z[:, st, :], yps[:, st * D:(st + 1) * D], r[:, st:st + 1],
                                                    s.xr[:, st, :], ALU.mult, ALU.add)
                own(last)
                own.end()
                dve.nop().then_inc(s.z_made, 1)

            s.each_sequence(dve, sequence)
    s.close()


def cross_stage(k, x_in, x_out, ctxT_in, mask_in, wq, bq, wk, bk, wv, bv, wo, qn, kn):
    nc, ps, ident = k.nc, k.ps, k.ident
    NH, NKV, HD = 16, 4, 128
    G = NH // NKV
    E = ctxT_in.shape[2]
    ET = (E + P - 1) // P
    rows = [min(P, E - e * P) for e in range(ET)]
    chunks = [(c, min(BANK, E - c)) for c in range(0, E, BANK)]
    NC = len(chunks)
    UNITS = ST * NKV
    HEADS = UNITS * G
    NORMED = ET + UNITS
    LAG = 3
    XJ = ET - 4
    s = Stage(k, "cross", x_in, x_out)
    wq_p, wk_p, wv_p = ([s.sb(f"{name}_{part}", [P, DC, n], F16) for part in ("hi", "lo")]
                        for name, n in (("wq", NH * HD), ("wk", NKV * HD), ("wv", NKV * HD)))
    wo_s = s.sb("wo", [P, NH, D])
    bq_s, bk_s, bv_c = s.sb("bq", [P, NH * HD]), s.sb("bk", [P, NKV * HD]), s.sb("bv", [P, NKV])
    vbias = s.sb("vbias", [P, D])
    nw = s.sb("nw", [P, 2])
    qk_w = s.sb("qk_w", [P, 1])
    mask = s.sb("mask", [P, ST, E])
    ctxT = s.sb("ctxT", [P, DC, E])
    kT = [s.sb(f"kT_{part}", [P, NKV, E], F16) for part in ("hi", "lo")]
    v = [s.sb(f"v_{part}", [P, ET, NKV * HD], F16) for part in ("hi", "lo")]
    qT = [s.sb(f"qT_{part}", [P, UNITS, G * P], F16) for part in ("hi", "lo")]
    pT = [[s.sb(f"pT{n}_{part}", [P, ET, 2, P], F16) for part in ("hi", "lo")] for n in range(2)]
    sc = [s.sb(f"sc{n}", [P, E]) for n in range(3)]
    raw = [s.sb(f"raw{n}", [P, NKV * HD]) for n in range(3)]
    nrm, sq = [sc[2][:, 0:512], sc[2][:, 512:1024]], sc[2][:, 1024:1536]
    ctx_p = [t_[:].rearrange("p e g s -> p (e g s)")[:, 0:DC * E].rearrange("p (c e) -> p c e", c=DC)
             for t_ in pT[0]]
    xT_p = [s.xT[:].rearrange("p c s -> p (c s)").bitcast(F16)[:, n * DC * S:(n + 1) * DC * S]
            .rearrange("p (c s) -> p c s", c=DC) for n in range(2)]
    as_f32 = lambda t_: t_[:].rearrange("p g e -> p (g e)").bitcast(F32)
    w_in = [(wk_p, slice(0, DC), 0, wk, sc[0][:, 0:DC * NKV * HD]), (wv_p, slice(0, DC), 0, wv, sc[1][:, 0:DC * NKV * HD])] + \
           [(wq_p, slice(dc, dc + 1), dc, wq, as_f32(v[dc])[:, 0:NH * HD]) for dc in range(DC)]
    bv_b = raw[0][:].rearrange("p (g s) -> p g s", g=NKV)
    msq, rr = s.sb("msq", [P, 2, NKV]), s.sb("rr", [P, 3, NKV])
    mx, nmx, sums, rsum = s.sb("mx", [P, 3, NC]), s.sb("nmx", [P, 3]), s.sb("sums", [P, HEADS, 2]), s.sb("rsum", [P, 2])
    ones = s.sb("ones", [P, P])
    diag, rbc, oT = raw[0][:, 0:2 * P], [raw[1][:, 256 * n:256 * n + 256] for n in range(2)], \
        [raw[2][:, 256 * n:256 * n + 256] for n in range(2)]
    (w_loaded, const_ready, ctx_loaded, kq_ps, v_ps, raw_ready, sq_ready, v_ready, ms_ready, rr_ready,
     nrm_ready, turn_ps, turned, turned_hi, v_hi) = (s.sem(n) for n in (
        "w_loaded", "const_ready", "ctx_loaded", "kq_ps", "v_ps", "raw_ready", "sq_ready", "v_ready",
        "ms_ready", "rr_ready", "nrm_ready", "turn_ps", "turned", "turned_hi", "v_hi"))
    (w_hi, w_ready, bias_ps, ctx_hi, ctx_ready, xT_hi, mixed) = (s.sem(n) for n in (
        "w_hi", "w_ready", "bias_ps", "ctx_hi", "ctx_ready", "xT_hi", "mixed"))
    (sc_ps, sc_read, nmx_ready, exp_done, t_ps, t_act, t_dve, pv_ps, diag_ready, oT_ready, y_ps, dve_own) = (
        s.sem(n) for n in ("sc_ps", "sc_read", "nmx_ready", "exp_done", "t_ps", "t_act", "t_dve", "pv_ps",
                           "diag_ready", "oT_ready", "y_ps", "dve_own"))
    bank = lambda n: ps[:, n, :]
    KQ, VB, SB, TB, OB, YB = (0, 1), (2, 5), (0, 1, 2), (3, 4), (5, 6), 7
    SLOTS = (ET + G - 1) // G
    PAIRS = HEADS // 2
    slot_tiles = lambda j: min(G, ET - G * j)
    slot_rows = lambda j: P if slot_tiles(j) == G else rows[-1]
    order = []
    for n in range(HEADS):
        for j in range(SLOTS):
            order.append((n, j))
            if n % 2 == 0 and n and j == 2:
                order.append(("r", n // 2 - 1))
    order.append(("r", PAIRS - 1))
    T_PS = len(order)
    t_index = {what: x for x, what in enumerate(order)}
    t_count = lambda n, j: t_index[n, j] + 1
    r_count = lambda m: t_index["r", m] + 1
    d_count = lambda n, j: SLOTS * n + j + 1
    t_bank = lambda x: ps[:, TB[x % 2], :]
    PSCALE = 15 * float(np.log(2.0))
    WSCALE = 64.0
    PASSES = ((0, 0), (0, 1), (1, 0))
    CUT = 768
    parts = [range(ET * x // (2 * SLOTS), ET * (x + 1) // (2 * SLOTS)) for x in range(2 * SLOTS)]

    W_ALL = 16 * (len(w_in) + 2 + 1 + 2 + 2)

    with nc.Block() as block:
        @block.sync
        def _(sp):
            for _, cs, dc, a, t_ in w_in:
                sp.dma_start(t_.rearrange("p (c n) -> p c n", c=cs.stop - cs.start),
                             a.rearrange("(c p) n -> p c n", p=P)[:, cs, :]).then_inc(w_loaded, 16)
            for t_, a in ((bk_s, bk), (bq_s, bq)):
                sp.dma_start(t_[:], a.partition_broadcast(P)).then_inc(w_loaded, 16)
            sp.dma_start(bv_c[:], bv).then_inc(w_loaded, 16)
            sp.dma_start(nw[:, 0:1], qn).then_inc(w_loaded, 16)
            sp.dma_start(nw[:, 1:2], kn).then_inc(w_loaded, 16)
            sp.dma_start(wo_s[:], wo.rearrange("(h p) n -> p h n", p=P)).then_inc(w_loaded, 16)
            sp.dma_start(mask[:], mask_in.rearrange("(s p) e -> p s e", p=P)).then_inc(w_loaded, 16)

            def context(i):
                if not isinstance(i, int):
                    sp.wait_ge(ctx_ready, at(i, NC, 0))
                sp.dma_start(ctxT[:], one(ctxT_in, i).rearrange("(c p) e -> p c e", p=P)).then_inc(ctx_loaded, 16)

            s.rows_dma(sp, context)

        @block.gpsimd
        def _(pool):
            pool.memset(ones[:], 1.0).then_inc(const_ready, 1)
            pool.wait_ge(w_ready, len(w_in) + 1)
            with pool.Fori(0, B) as i:
                s.keep_x(pool, i, vbias[:])
                for j in range(NORMED):
                    m = rows[j] if j < ET else P
                    pool.wait_ge(ms_ready, at(i, NORMED, j + 1))
                    pool.tensor_tensor(rr[:, j % 3, :], msq[:, j % 2, :], k.neg_half[:, 0:NKV], ALU.pow)\
                        .then_inc(rr_ready, 1)
                    pool.wait_ge(rr_ready, at(i, NORMED, j + 1))
                    if j >= 2:
                        pool.wait_ge(turn_ps, at(i, NORMED, j - 1))
                    pool.tensor_tensor(nrm[j % 2][0:m, :].rearrange("p (g d) -> p g d", g=NKV),
                                       raw[j % 3][0:m, :].rearrange("p (g d) -> p g d", g=NKV),
                                       rr[0:m, j % 3, :].unsqueeze(2).to_broadcast([m, NKV, HD]), ALU.mult)\
                        .then_inc(nrm_ready, 1)
                s.norm_pool(pool, i)

        @block.tensor
        def _(pe):
            pe.wait_ge(w_loaded, W_ALL)
            pe.wait_ge(const_ready, 3)
            for h in range(NH):
                last = pe.matmul(bank(YB)[:, 0:D], bv_b[:, h // G, :], wo_s[:, h, :], start=h == 0, stop=h == NH - 1)
            last.then_inc(bias_ps, 1)
            pe.wait_ge(w_ready, len(w_in) + 1)
            with pe.Fori(0, B) as i:
                def project(j):
                    key = j < ET
                    m = rows[j] if key else P
                    if j >= 2:
                        pe.wait_ge(raw_ready, at(i, NORMED, j - 1))
                    def product(out, left, right, n0, n1, e0):
                        for dc in range(DC):
                            for lp, rp in PASSES:
                                last = pe.matmul(out[0:m, :], left[lp][:, dc, e0:e0 + m], right[rp][:, dc, n0:n1],
                                                 start=dc + lp + rp == 0, stop=dc == DC - 1 and lp == 1)
                        return last

                    if key:
                        last = product(bank(KQ[j % 2]), ctx_p, wk_p, 0, NKV * HD, j * P)
                    else:
                        st, g = divmod(j - ET, NKV)
                        last = product(bank(KQ[j % 2]), xT_p, wq_p, g * G * HD, (g + 1) * G * HD, st * P)
                    last.then_inc(kq_ps, 1)
                    if key:
                        if j >= 2:
                            pe.wait_ge(v_ready, at(i, ET, j - 1))
                        product(bank(VB[j % 2]), ctx_p, wv_p, 0, NKV * HD, j * P).then_inc(v_ps, 1)

                def turn(j):
                    m = rows[j] if j < ET else P
                    pe.wait_ge(nrm_ready, at(i, NORMED, j + 1))
                    if j >= 2:
                        pe.wait_ge(turned, at(i, NORMED, j - 1))
                    for g in range(NKV):
                        last = pe.transpose(bank(TB[j % 2])[:, g * P:g * P + m], nrm[j % 2][0:m, g * P:(g + 1) * P],
                                            ident[0:m, 0:m])
                    last.then_inc(turn_ps, 1)

                def scores(n, c):
                    u = n // G
                    g = u % NKV
                    e0, w = chunks[c]
                    x = NC * n + c
                    if x >= 3:
                        pe.wait_ge(sc_read, at(i, NC * HEADS, x - 2))
                    for q, kk in ((0, 0), (0, 1), (1, 0)):
                        last = pe.matmul(bank(SB[x % 3])[:, 0:w], qT[q][:, u, (n % G) * P:(n % G + 1) * P],
                                         kT[kk][:, g, e0:e0 + w], start=q + kk == 0, stop=q == 1)
                    last.then_inc(sc_ps, 1)

                def bank_read(x):
                    if x >= 2:
                        n, j = order[x - 2]
                        if n == "r":
                            pe.wait_ge(t_act, at(i, T_PS, r_count(j)))
                        else:
                            pe.wait_ge(t_dve, at(i, SLOTS * HEADS, d_count(n, j)))

                def turn_probs(n, j):
                    if j == 0:
                        pe.wait_ge(exp_done, at(i, HEADS, n + 1))
                    x = t_index[n, j]
                    bank_read(x)
                    for e in range(G * j, min(G * j + G, ET)):
                        last = pe.transpose(t_bank(x)[0:rows[e], (e % G) * P:(e % G + 1) * P],
                                            sc[n % 3][:, e * P:e * P + rows[e]], ident[:])
                    last.then_inc(t_ps, 1)

                def spread(m):
                    pe.wait_ge(diag_ready, at(i, PAIRS, m + 1))
                    x = t_index["r", m]
                    bank_read(x)
                    pe.matmul(t_bank(x)[:, 0:2 * P], ones[:], diag[:], start=True, stop=True).then_inc(t_ps, 1)

                def mix(m, part):
                    if part == 0:
                        pe.wait_ge(t_dve, at(i, SLOTS * HEADS, d_count(2 * m + 1, SLOTS - 1)))
                        if m >= 2:
                            pe.wait_ge(oT_ready, at(i, PAIRS, m - 1))
                    g = m // 2 % NKV
                    for e in parts[part]:
                        for vv, pp in ((0, 0), (0, 1), (1, 0)):
                            last = pe.matmul(bank(OB[m % 2])[:, 0:2 * P], v[vv][0:rows[e], e, g * HD:(g + 1) * HD],
                                             pT[m % 2][pp][0:rows[e], e, :, :].rearrange("p g s -> p (g s)"),
                                             start=e == 0 and vv + pp == 0, stop=e == ET - 1 and vv == 1)
                    if part == 2 * SLOTS - 1:
                        last.then_inc(pv_ps, 1)

                def output(m):
                    st, g = divmod(m // 2, NKV)
                    pe.wait_ge(oT_ready, at(i, PAIRS, m + 1))
                    for h in range(2):
                        last = pe.matmul(bank(YB)[:, st * D:(st + 1) * D], oT[m % 2][:, h * P:(h + 1) * P],
                                         wo_s[:, g * G + m % 2 * 2 + h, :], start=g == 0 and m % 2 == 0 and h == 0,
                                         stop=g == NKV - 1 and m % 2 == 1 and h == 1)
                    last.then_inc(y_ps, 1)

                for j in range(NORMED + LAG):
                    if j == XJ:
                        pe.wait_ge(s.z_made, at(i, 1, 1))
                        s.transpose_x(pe, i, bank(YB))
                    if j < ET and (j * P) % BANK == 0:
                        pe.wait_ge(ctx_ready, at(i, NC, j * P // BANK + 1))
                    if j == ET:
                        pe.wait_ge(s.xT_ready, at(i, 1, 1))
                    if j < NORMED:
                        project(j)
                    if j >= LAG:
                        turn(j - LAG)
                pe.wait_ge(turned, at(i, NORMED, NORMED))
                pe.wait_ge(v_ready, at(i, ET, ET))
                for n in range(2):
                    for c in range(NC):
                        scores(n, c)
                for n in range(HEADS):
                    m, odd = divmod(n, 2)
                    for j in range(SLOTS):
                        turn_probs(n, j)
                        if m >= 1:
                            mix(m - 1, SLOTS * odd + j)
                            if n % 2 == 0 and j == 2:
                                spread(m - 1)
                        if n + 2 < HEADS:
                            scores(n + 2, j)
                        if m >= 2 and odd == 0 and j == 2:
                            output(m - 2)
                for part in range(2 * SLOTS):
                    mix(PAIRS - 1, part)
                spread(PAIRS - 1)
                output(PAIRS - 2)
                output(PAIRS - 1)
                pe.wait_ge(pv_ps, at(i, PAIRS, PAIRS))
                pe.sem_inc(mixed, 1)

        @block.scalar
        def _(act):
            act.wait_ge(w_loaded, W_ALL)
            act.wait_ge(const_ready, 4)
            for n, (t_, cs, dc, a, w) in enumerate(w_in):
                act.activation(t_[0][:, cs, :], w.rearrange("p (c n) -> p c n", c=cs.stop - cs.start), ACT.Copy,
                               scale=WSCALE).then_inc(w_hi, 1)
            act.wait_ge(w_ready, len(w_in) + 1)
            with act.Fori(0, B) as i:
                def context_hi(c):
                    e0, w = chunks[c]
                    act.copy(ctx_p[0][:, :, e0:e0 + w], ctxT[:, :, e0:e0 + w]).then_inc(ctx_hi, 1)

                act.wait_ge(mixed, at(i, 1, 1))
                act.wait_ge(ctx_loaded, at(i, 16, 16))
                context_hi(0)
                for j in range(NORMED + LAG):
                    if j % G == 1 and j // G + 1 < NC:
                        context_hi(j // G + 1)
                    if j == XJ:
                        act.wait_ge(s.xT_ps, at(i, 1, 1))
                        act.copy(xT_p[0].rearrange("p c s -> p (c s)"), bank(YB)).then_inc(xT_hi, 1)
                    if j < NORMED:
                        m = rows[j] if j < ET else P
                        act.wait_ge(raw_ready, at(i, NORMED, j + 1))
                        if j >= 1:
                            act.wait_ge(sq_ready, at(i, NORMED, j))
                        if j >= 2:
                            act.wait_ge(rr_ready, at(i, NORMED, j - 1))
                        for g in range(NKV):
                            last = act.activation(sq[0:m, g * HD:(g + 1) * HD], raw[j % 3][0:m, g * HD:(g + 1) * HD],
                                                  ACT.Square, accum_out=msq[0:m, j % 2, g:g + 1])
                        last.then_inc(sq_ready, 1)
                        if j < ET:
                            act.wait_ge(v_ps, at(i, ET, j + 1))
                            act.activation(v[0][0:m, j, :], bank(VB[j % 2])[0:m, :], ACT.Copy, scale=1.0 / WSCALE)\
                               .then_inc(v_hi, 1)
                    if j >= LAG:
                        n = j - LAG
                        act.wait_ge(turn_ps, at(i, NORMED, n + 1))
                        src = bank(TB[n % 2])
                        if n < ET:
                            act.copy(kT[0][:, :, n * P:n * P + rows[n]],
                                     src.rearrange("p (g e) -> p g e", g=NKV)[:, :, 0:rows[n]]).then_inc(turned_hi, 1)
                        else:
                            act.activation(qT[0][:, n - ET, :], src, ACT.Copy, scale=qk_w[:]).then_inc(turned_hi, 1)

                def exp(n, part):
                    if part == 0:
                        act.wait_ge(nmx_ready, at(i, HEADS, n + 1))
                    piece = sc[n % 3][:, 0:CUT] if part == 0 else sc[n % 3][:, CUT:E]
                    ins = act.activation(piece, piece, ACT.Exp, bias=nmx[:, n % 3:n % 3 + 1],
                                         accum_out=sums[:, n, part:part + 1])
                    if part == 1:
                        ins.then_inc(exp_done, 1)

                def spread_copy(m):
                    if m >= 2:
                        act.wait_ge(oT_ready, at(i, PAIRS, m - 1))
                    act.wait_ge(t_ps, at(i, T_PS, r_count(m)))
                    act.copy(rbc[m % 2][:], t_bank(t_index["r", m])[:, 0:2 * P]).then_inc(t_act, 1)

                exp(0, 0)
                exp(0, 1)
                for n in range(HEADS):
                    m = n // 2
                    if n % 2 == 0 and m >= 2:
                        act.wait_ge(pv_ps, at(i, PAIRS, m - 1))
                    for j in range(SLOTS):
                        r, ne = slot_rows(j), slot_tiles(j)
                        act.wait_ge(t_ps, at(i, T_PS, t_count(n, j)))
                        act.copy(pT[m % 2][0][0:r, G * j:G * j + ne, n % 2, :],
                                 t_bank(t_index[n, j])[0:r, 0:ne * P].rearrange("p (e s) -> p e s", e=ne))\
                           .then_inc(t_act, 1)
                        if n % 2 == 0 and m and j == 2:
                            spread_copy(m - 1)
                        if j in (0, 2) and n + 1 < HEADS:
                            exp(n + 1, j // 2)
                spread_copy(PAIRS - 1)

        @block.vector
        def _(dve):
            s.credits(dve)
            dve.sem_inc(mixed, 1)
            dve.wait_ge(w_loaded, W_ALL)
            dve.wait_ge(const_ready, 1)
            dve.tensor_copy(bv_b, bv_c[:].unsqueeze(2).to_broadcast([P, NKV, P])).then_inc(const_ready, 1)
            dve.wait_ge(const_ready, 2)
            dve.nop().then_inc(const_ready, 1)
            dve.scalar_tensor_tensor(qk_w[:], nw[:, 0:1], float(HD) ** -0.5, nw[:, 1:2], ALU.mult, ALU.mult)\
               .then_inc(const_ready, 1)
            for n, (t_, cs, dc, a, w) in enumerate(w_in):
                dve.wait_ge(w_hi, n + 1)
                dve.scalar_tensor_tensor(t_[1][:, cs, :], w.rearrange("p (c n) -> p c n", c=cs.stop - cs.start), WSCALE,
                                         t_[0][:, cs, :], ALU.mult, ALU.subtract).then_inc(w_ready, 1)
            dve.wait_ge(bias_ps, 1)
            dve.tensor_copy(vbias[:], bank(YB)[:, 0:D]).then_inc(w_ready, 1)
            dve.wait_ge(w_ready, len(w_in) + 1)

            def sequence(i, before):
                own = Chain(dve, dve_own, HEADS + 2 * PAIRS, i)

                def context_lo(c):
                    e0, w = chunks[c]
                    dve.wait_ge(ctx_hi, at(i, NC, c + 1))
                    dve.tensor_tensor(ctx_p[1][:, :, e0:e0 + w], ctxT[:, :, e0:e0 + w], ctx_p[0][:, :, e0:e0 + w],
                                      ALU.subtract).then_inc(ctx_ready, 1)

                context_lo(0)
                for j in range(NORMED + LAG + 1):
                    if j < NORMED:
                        key = j < ET
                        m = rows[j] if key else P
                        bias = bk_s[:] if key else bq_s[:, (j - ET) % NKV * 512:((j - ET) % NKV + 1) * 512]
                        dve.wait_ge(kq_ps, at(i, NORMED, j + 1))
                        if j >= 3:
                            dve.wait_ge(sq_ready, at(i, NORMED, j - 2))
                            dve.wait_ge(nrm_ready, at(i, NORMED, j - 2))
                        dve.scalar_tensor_tensor(raw[j % 3][0:m, :], bank(KQ[j % 2])[0:m, :], 1.0 / WSCALE, bias[0:m, :],
                                                 ALU.mult, ALU.add).then_inc(raw_ready, 1)
                    if j == 1:
                        s.norm_before(dve, before)
                    if j % G == 1 and j // G + 1 < NC:
                        context_lo(j // G + 1)
                    if j == XJ:
                        dve.wait_ge(xT_hi, at(i, 1, 1))
                        dve.tensor_tensor(xT_p[1].rearrange("p c s -> p (c s)"), bank(YB),
                                          xT_p[0].rearrange("p c s -> p (c s)"), ALU.subtract)\
                           .then_inc(s.xT_ready, 1)
                    if j > LAG:
                        n = j - LAG - 1
                        dve.wait_ge(turned_hi, at(i, NORMED, n + 1))
                        src = bank(TB[n % 2])
                        if n < ET:
                            hi, lo = (t_[:, :, n * P:n * P + rows[n]] for t_ in kT)
                            dve.tensor_tensor(lo, src.rearrange("p (g e) -> p g e", g=NKV)[:, :, 0:rows[n]], hi,
                                              ALU.subtract).then_inc(turned, 1)
                        else:
                            dve.scalar_tensor_tensor(qT[1][:, n - ET, :], src, qk_w[:], qT[0][:, n - ET, :],
                                                     ALU.mult, ALU.subtract).then_inc(turned, 1)
                    if j < NORMED:
                        dve.wait_ge(sq_ready, at(i, NORMED, j + 1))
                        dve.tensor_scalar(msq[0:m, j % 2, :], msq[0:m, j % 2, :], 1.0 / HD, RMS_EPS,
                                          ALU.mult, ALU.add).then_inc(ms_ready, 1)
                    if j < ET:
                        dve.wait_ge(v_hi, at(i, ET, j + 1))
                        dve.scalar_tensor_tensor(v[1][0:m, j, :], bank(VB[j % 2])[0:m, :], 1.0 / WSCALE,
                                                 v[0][0:m, j, :], ALU.mult, ALU.subtract).then_inc(v_ready, 1)

                def maxima(n, c):
                    st = n // G // NKV
                    e0, w = chunks[c]
                    x = NC * n + c
                    if n >= 3 and c == 0:
                        dve.wait_ge(t_ps, at(i, T_PS, t_count(n - 3, SLOTS - 1)))
                    dve.wait_ge(sc_ps, at(i, NC * HEADS, NC * n + c + 1))
                    s.carry(dve)
                    dve.tensor_tensor_reduce(sc[n % 3][:, e0:e0 + w], bank(SB[x % 3])[:, 0:w], mask[:, st, e0:e0 + w],
                                             1.0, -3.0e38, ALU.add, ALU.max, mx[:, n % 3, c:c + 1])\
                       .then_inc(sc_read, 1)
                    if c == NC - 1:
                        dve.wait_ge(sc_read, at(i, NC * HEADS, NC * n + NC))
                        own(dve.tensor_reduce(nmx[:, n % 3:n % 3 + 1], mx[:, n % 3, :], AX_X, ALU.max, negate=True))
                        dve.tensor_scalar(nmx[:, n % 3:n % 3 + 1], nmx[:, n % 3:n % 3 + 1], PSCALE, None, ALU.add)\
                           .then_inc(nmx_ready, 1)

                def low_part(n, j):
                    r, ne = slot_rows(j), slot_tiles(j)
                    dve.wait_ge(t_act, at(i, T_PS, t_count(n, j)))
                    hi, lo = (t_[0:r, G * j:G * j + ne, n % 2, :] for t_ in pT[n // 2 % 2])
                    dve.tensor_tensor(lo, t_bank(t_index[n, j])[0:r, 0:ne * P].rearrange("p (e s) -> p e s", e=ne),
                                      hi, ALU.subtract).then_inc(t_dve, 1)

                def reciprocals(m):
                    dve.wait_ge(exp_done, at(i, HEADS, 2 * m + 2))
                    if m >= 1:
                        dve.wait_ge(t_act, at(i, T_PS, r_count(m - 1)))
                    own(dve.tensor_tensor(rsum[:], sums[:, 2 * m:2 * m + 2, 0], sums[:, 2 * m:2 * m + 2, 1], ALU.add))
                    own(dve.reciprocal(rsum[:], rsum[:]))
                    dve.tensor_tensor(diag.rearrange("p (h s) -> p h s", h=2),
                                      ident[:].unsqueeze(1).to_broadcast([P, 2, P]),
                                      rsum[:].unsqueeze(2).to_broadcast([P, 2, P]), ALU.mult)\
                       .then_inc(diag_ready, 1)

                def divide(m):
                    dve.wait_ge(t_act, at(i, T_PS, r_count(m)))
                    dve.wait_ge(pv_ps, at(i, PAIRS, m + 1))
                    if m >= 2:
                        dve.wait_ge(y_ps, at(i, PAIRS, m - 1))
                    dve.tensor_tensor(oT[m % 2][:], bank(OB[m % 2])[:, 0:2 * P], rbc[m % 2][:], ALU.mult)\
                       .then_inc(oT_ready, 1)

                for n in range(2):
                    for c in range(NC):
                        maxima(n, c)
                for n in range(HEADS):
                    m = n // 2
                    for j in range(SLOTS):
                        low_part(n, j)
                        if n % 2 == 0 and j == 0 and m >= 1:
                            reciprocals(m - 1)
                        if n % 2 == 0 and j == 1 and m >= 2:
                            divide(m - 2)
                        if n + 2 < HEADS:
                            maxima(n + 2, j)
                reciprocals(PAIRS - 1)
                divide(PAIRS - 2)
                divide(PAIRS - 1)
                dve.wait_ge(s.x_kept, at(i, 1, 1))
                dve.wait_ge(y_ps, at(i, PAIRS, PAIRS))
                dve.tensor_tensor(s.z[:].rearrange("p s d -> p (s d)"), bank(YB),
                                  s.xr[:].rearrange("p s d -> p (s d)"), ALU.add).then_inc(s.z_made, 1)

            s.each_sequence(dve, sequence)
    s.close()


def experts_stage(k, x_in, x_out, gate_w, gate_up, down, merge, dominant):
    nc, ps, ident = k.nc, k.ps, k.ident
    E, I = down.shape[0], down.shape[1]
    GR = dominant.shape[1]
    s = Stage(k, "experts", x_in, x_out)
    gw = s.sb("gw", [P, DC, E])
    gu = s.sb("gu", [P, DC, GR * 2 * I])
    dn = s.sb("dn", [I, GR, D])
    dom = s.sb("dom", [1, GR], I32)
    mg, mgf = s.sb("mg", [E, 1], I32), s.sb("mgf", [E, 1])
    gi, gf = s.sb("gi", [E, GR], I32), s.sb("gf", [E, GR])
    group = s.sb("group", [E, GR])
    nmx, e, top, left, sel = (s.sb("nmx", [P, ST]), s.sb("e", [P, ST, E]), s.sb("top", [P, ST, 8]),
                              s.sb("left", [P, ST, E]), s.sb("sel", [P, ST, E]))
    tsum, rts, selT, wt = s.sb("tsum", [P, ST]), s.sb("rts", [P, ST]), s.sb("selT", [E, S]), s.sb("wt", [P, ST, GR])
    g = [s.sb(f"g{n}", [P, GR, I]) for n in range(ST)]
    a = [s.sb(f"a{n}", [P, GR, I]) for n in range(ST)]
    aT = [s.sb(f"aT{n}", [I, GR, P]) for n in range(ST)]
    (w_loaded, dom_loaded, const_ready, lg_ps, nmx_ready, e_ready, sel_ready, selT_ps, selT_ready, w_ps, wt_ready,
     h_ps, silu_ready, a_half, a_ready, t_ps, t_ev, y_ps, dve_own) = (s.sem(n) for n in (
        "w_loaded", "dom_loaded", "const_ready", "lg_ps", "nmx_ready", "e_ready", "sel_ready", "selT_ps",
        "selT_ready", "w_ps", "wt_ready", "h_ps", "silu_ready", "a_half", "a_ready", "t_ps", "t_ev", "y_ps",
        "dve_own"))
    HB = range(0, 4)
    TB, YB, MB, XB = (4, 5), 6, 7, 4
    W2 = 2 * 2 * I
    hid = ps[:, 0:4, 0:W2].rearrange("p b (g o) -> p b g o", g=2)
    v4 = lambda t_: t_[:].rearrange("p (b g) i -> p b g i", g=2)
    misc = ps[:, MB, :]
    LG, WP, TP = misc[:, 0:ST * E], misc[:, 64:64 + ST * GR], misc[0:E, 128:128 + S]

    with nc.Block() as block:
        @block.sync
        def _(sp):
            sp.dma_start(dom[:], dominant).then_inc(dom_loaded, 16)
            sp.dma_start(gw[:], gate_w.rearrange("(c p) n -> p c n", p=P)).then_inc(w_loaded, 16)
            sp.dma_start(mg[:], merge).then_inc(w_loaded, 16)
            sp.wait_ge(dom_loaded, 16)
            for n in range(GR):
                x = sp.value_load(dom[0:1, n:n + 1], min_val=0, max_val=E - 1)
                sp.dma_start(gu[:, :, n * 2 * I:(n + 1) * 2 * I],
                             one(gate_up, x).rearrange("(c p) o -> p c o", p=P)).then_inc(w_loaded, 16)
                sp.dma_start(dn[:, n, :], one(down, x)).then_inc(w_loaded, 16)
            s.rows_dma(sp)

        @block.gpsimd
        def _(pool):
            pool.iota(gi[:], [[1, GR]], base=0, channel_multiplier=0).then_inc(const_ready, 1)
            with pool.Fori(0, B) as i:
                s.keep_x(pool, i)
                s.norm_pool(pool, i)

        @block.tensor
        def _(pe):
            pe.wait_ge(w_loaded, 16 * (2 + 2 * GR))
            pe.wait_ge(const_ready, 2)
            with pe.Fori(0, B) as i:
                def hidden(st):
                    if st >= 1:
                        pe.wait_ge(a_half, at(i, ST, st))
                    for q in HB:
                        for dc in range(DC):
                            last = pe.matmul(ps[:, q, 0:W2], s.xT[:, dc, st * P:(st + 1) * P],
                                             gu[:, dc, q * W2:(q + 1) * W2], start=dc == 0, stop=dc == DC - 1)
                    last.then_inc(h_ps, 1)

                def down_product(st):
                    pe.wait_ge(a_ready, at(i, ST, st + 1))
                    if st >= 1:
                        pe.wait_ge(t_ev, at(i, 2 * ST, 2 * st))
                    for n in range(GR):
                        last = pe.transpose(ps[0:I, TB[n // 4], (n % 4) * P:(n % 4 + 1) * P], a[st][:, n, :], ident[:])
                        if n % 4 == 3:
                            last.then_inc(t_ps, 1)
                    pe.wait_ge(t_ev, at(i, 2 * ST, 2 * st + 2))
                    if st == 0:
                        pe.wait_ge(s.z_made, at(i, 1, 1))
                    for n in range(GR):
                        last = pe.matmul(ps[:, YB, st * D:(st + 1) * D], aT[st][:, n, :], dn[:, n, :],
                                         start=n == 0, stop=n == GR - 1)
                    last.then_inc(y_ps, 1)

                s.transpose_x(pe, i, ps[:, XB, :])
                pe.wait_ge(s.xT_ready, at(i, 1, 1))
                for st in range(ST):
                    for dc in range(DC):
                        last = pe.matmul(LG[:, st * E:(st + 1) * E], s.xT[:, dc, st * P:(st + 1) * P], gw[:, dc, :],
                                         start=dc == 0, stop=dc == DC - 1)
                last.then_inc(lg_ps, 1)
                hidden(0)
                pe.wait_ge(sel_ready, at(i, 1, 1))
                for st in range(ST):
                    last = pe.transpose(TP[:, st * P:(st + 1) * P], sel[:, st, :], ident[:])
                last.then_inc(selT_ps, 1)
                pe.wait_ge(selT_ready, at(i, 1, 1))
                for st in range(ST):
                    last = pe.matmul(WP[:, st * GR:(st + 1) * GR], selT[:, st * P:(st + 1) * P], group[:],
                                     start=True, stop=True)
                last.then_inc(w_ps, 1)
                hidden(1)
                down_product(0)
                down_product(1)

        @block.scalar
        def _(act):
            with act.Fori(0, B) as i:
                s.copy_xT(act, i, ps[:, XB, :])
                act.wait_ge(nmx_ready, at(i, 1, 1))
                for st in range(ST):
                    last = act.activation(e[:, st, :], LG[:, st * E:(st + 1) * E], ACT.Exp, bias=nmx[:, st:st + 1])
                last.then_inc(e_ready, 1)
                for st in range(ST):
                    act.wait_ge(h_ps, at(i, ST, st + 1))
                    act.activation(v4(g[st]), hid[:, :, :, 0:I], ACT.Silu).then_inc(silu_ready, 1)
                for st in range(ST):
                    for q in range(2):
                        act.wait_ge(t_ps, at(i, 2 * ST, 2 * st + q + 1))
                        act.copy(aT[st][:, 4 * q:4 * q + 4, :].rearrange("p g s -> p (g s)"),
                                 ps[0:I, TB[q], :]).then_inc(t_ev, 1)

        @block.vector
        def _(dve):
            s.credits(dve)
            dve.wait_ge(w_loaded, 16 * (2 + 2 * GR))
            dve.wait_ge(const_ready, 1)
            first = Chain(dve, dve_own)
            dve.tensor_copy(mgf[:], mg[:])
            first(dve.tensor_copy(gf[:], gi[:]))
            dve.tensor_scalar(group[:], gf[:], mgf[:], None, ALU.is_equal).then_inc(const_ready, 1)

            def sequence(i, before):
                own = Chain(dve, a_half, ST, i)
                fence = Chain(dve, s.own2, 3, i)
                dve.wait_ge(lg_ps, at(i, 1, 1))
                dve.tensor_reduce(nmx[:], LG.rearrange("p (s e) -> p s e", s=ST), AX_X, ALU.max, negate=True)\
                   .then_inc(nmx_ready, 1)
                dve.wait_ge(e_ready, at(i, 1, 1))
                s.carry(dve)
                for st in range(ST):
                    last = dve.max(top[:, st, :], e[:, st, :])
                fence(last)
                s.carry(dve)
                for st in range(ST):
                    last = dve.match_replace(left[:, st, :], top[:, st, :], e[:, st, :], -1.0)
                fence(last)
                for st in range(ST):
                    last = dve.scalar_tensor_tensor(sel[:, st, :], left[:, st, :], 0.0, e[:, st, :], ALU.is_lt,
                                                    ALU.mult, accum_out=tsum[:, st:st + 1])
                fence(last)
                dve.sem_inc(sel_ready, 1)
                dve.reciprocal(rts[:], tsum[:])
                s.norm_before(dve, before)
                dve.wait_ge(selT_ps, at(i, 1, 1))
                dve.tensor_copy(selT[:], TP).then_inc(selT_ready, 1)
                dve.wait_ge(w_ps, at(i, 1, 1))
                dve.tensor_tensor(wt[:], WP.rearrange("p (s g) -> p s g", s=ST),
                                  rts[:].unsqueeze(2).to_broadcast([P, ST, GR]), ALU.mult).then_inc(wt_ready, 1)
                for st in range(ST):
                    dve.wait_ge(silu_ready, at(i, ST, st + 1))
                    own(dve.tensor_tensor(v4(a[st]), hid[:, :, :, I:2 * I], v4(g[st]), ALU.mult))
                    if st == 0:
                        dve.wait_ge(wt_ready, at(i, 1, 1))
                    dve.tensor_tensor(a[st][:], a[st][:], wt[:, st, :].unsqueeze(2).to_broadcast([P, GR, I]),
                                      ALU.mult).then_inc(a_ready, 1)
                own.end()
                dve.wait_ge(s.x_kept, at(i, 1, 1))
                dve.wait_ge(y_ps, at(i, ST, ST))
                dve.tensor_tensor(s.z[:].rearrange("p s d -> p (s d)"), ps[:, YB, :],
                                  s.xr[:].rearrange("p s d -> p (s d)"), ALU.add).then_inc(s.z_made, 1)

            s.each_sequence(dve, sequence)
    s.close()


def memory_stage(k, x_in, x_out, ctxT_in, ctx_in, mask_in):
    nc, ps, ident = k.nc, k.ps, k.ident
    E = ctxT_in.shape[2]
    ET = (E + P - 1) // P
    FULL = E // P
    rows = [min(P, E - e * P) for e in range(ET)]
    chunks = [(c, min(BANK, E - c)) for c in range(0, E, BANK)]
    NC = len(chunks)
    SCALE = float(D) ** -0.5
    G = BANK // P
    SLOTS = (ET + G - 1) // G
    NT = ST * SLOTS
    s = Stage(k, "memory", x_in, x_out)
    ctxT, ctx = s.sb("ctxT", [P, DC, E]), s.sb("ctx", [P, ET, D])
    m8 = s.sb("m8", [P, E], U8)
    am = s.sb("am", [P, E])
    any_ = s.sb("any", [P, 1])
    sc = [s.sb(f"sc{n}", [P, E]) for n in range(ST)]
    pT = [s.sb(f"pT{n}", [P, ET, P]) for n in range(ST)]
    mx, nmx, sums, rs = s.sb("mx", [P, ST, NC]), s.sb("nmx", [P, ST]), s.sb("sums", [P, ST]), s.sb("rs", [P, ST])
    (ctxT_loaded, ctx_loaded, m_loaded, am_ready, any_ready, sc_ps, sc_read, nmx_ready, exp_done, t_ps, t_ev, o_ps, dve_own) = (
        s.sem(n) for n in ("ctxT_loaded", "ctx_loaded", "m_loaded", "am_ready", "any_ready", "sc_ps", "sc_read", "nmx_ready",
                           "exp_done", "t_ps", "t_ev", "o_ps", "dve_own"))
    TB, OB, XB = (4, 5), 6, 7

    with nc.Block() as block:
        @block.sync
        def _(sp):
            def context(i):
                later = not isinstance(i, int)
                if later:
                    sp.wait_ge(am_ready, at(i, 1, 0))
                    sp.wait_ge(any_ready, at(i, 1, 0))
                    s.carry(sp)
                sp.dma_start(m8[:], one(mask_in, i).partition_broadcast(P)).then_inc(m_loaded, 16)
                if later:
                    sp.wait_ge(sc_ps, at(i, NC * ST, 0))
                    s.carry(sp)
                sp.dma_start(ctxT[:], one(ctxT_in, i).rearrange("(c p) e -> p c e", p=P)).then_inc(ctxT_loaded, 16)
                if later:
                    sp.wait_ge(o_ps, at(i, ST, 0))
                    s.carry(sp)
                c = one(ctx_in, i)
                sp.dma_start(ctx[:, 0:FULL, :], c[0:FULL * P, :].rearrange("(e p) d -> p e d", p=P))\
                  .then_inc(ctx_loaded, 16)
                sp.dma_start(ctx[0:rows[-1], FULL, :], c[FULL * P:E, :]).then_inc(ctx_loaded, 16)

            s.rows_dma(sp, context)

        @block.gpsimd
        def _(pool):
            def slots(i):
                pool.wait_ge(m_loaded, at(i, 16, 16))
                s.carry(pool)
                pool.tensor_scalar(am[:], m8[:], 1.0, 1e30 / SCALE, ALU.subtract, ALU.mult).then_inc(am_ready, 1)

            slots(0)
            with pool.Fori(0, B - 1) as i:
                s.keep_x(pool, i)
                pool.wait_ge(sc_read, at(i, NC * ST, NC * ST))
                slots(i + 1)
                s.norm_pool(pool, i)
            s.keep_x(pool, B - 1)
            s.norm_pool(pool, B - 1)

        @block.tensor
        def _(pe):
            with pe.Fori(0, B) as i:
                def scores(st):
                    for c, (e0, w) in enumerate(chunks):
                        if st >= 1:
                            pe.wait_ge(sc_read, at(i, NC * ST, NC * (st - 1) + c + 1))
                        for dc in range(DC):
                            last = pe.matmul(ps[:, c, 0:w], s.xT[:, dc, st * P:(st + 1) * P], ctxT[:, dc, e0:e0 + w],
                                             start=dc == 0, stop=dc == DC - 1)
                        last.then_inc(sc_ps, 1)

                def turn_probs(st):
                    pe.wait_ge(exp_done, at(i, ST, st + 1))
                    for j in range(SLOTS):
                        n = SLOTS * st + j
                        if n >= 2:
                            pe.wait_ge(t_ev, at(i, NT, n - 1))
                        for e in range(G * j, min(G * j + G, ET)):
                            last = pe.transpose(ps[0:rows[e], TB[n % 2], (e % G) * P:(e % G + 1) * P],
                                                sc[st][:, e * P:e * P + rows[e]], ident[:])
                        last.then_inc(t_ps, 1)

                def mix(st):
                    pe.wait_ge(t_ev, at(i, NT, SLOTS * (st + 1)))
                    if st == 0:
                        pe.wait_ge(s.z_made, at(i, 1, 1))
                    for e in range(ET):
                        last = pe.matmul(ps[:, OB, st * D:(st + 1) * D], pT[st][0:rows[e], e, :], ctx[0:rows[e], e, :],
                                         start=e == 0, stop=e == ET - 1)
                    last.then_inc(o_ps, 1)

                s.transpose_x(pe, i, ps[:, XB, :])
                pe.wait_ge(s.xT_ready, at(i, 1, 1))
                pe.wait_ge(ctxT_loaded, at(i, 16, 16))
                scores(0)
                scores(1)
                turn_probs(0)
                pe.wait_ge(ctx_loaded, at(i, 32, 32))
                mix(0)
                turn_probs(1)
                mix(1)

        @block.scalar
        def _(act):
            with act.Fori(0, B) as i:
                s.copy_xT(act, i, ps[:, XB, :])
                for st in range(ST):
                    act.wait_ge(nmx_ready, at(i, ST, st + 1))
                    act.activation(sc[st][:], sc[st][:], ACT.Exp, bias=nmx[:, st:st + 1], scale=SCALE,
                                   accum_out=sums[:, st:st + 1]).then_inc(exp_done, 1)
                    for j in range(SLOTS):
                        n = SLOTS * st + j
                        act.wait_ge(t_ps, at(i, NT, n + 1))
                        ne = min(G, ET - G * j)
                        m = P if ne == G else rows[-1]
                        act.copy(pT[st][0:m, G * j:G * j + ne, :].rearrange("p e s -> p (e s)"),
                                 ps[0:m, TB[n % 2], 0:ne * P]).then_inc(t_ev, 1)

        @block.vector
        def _(dve):
            s.credits(dve)

            def sequence(i, before):
                own = Chain(dve, dve_own, ST + 2, i)
                dve.wait_ge(am_ready, at(i, 1, 1))
                for st in range(ST):
                    for c, (e0, w) in enumerate(chunks):
                        dve.wait_ge(sc_ps, at(i, NC * ST, NC * st + c + 1))
                        s.carry(dve)
                        dve.tensor_tensor_reduce(sc[st][:, e0:e0 + w], ps[:, c, 0:w], am[:, e0:e0 + w], 1.0, -3.0e38,
                                                 ALU.add, ALU.max, mx[:, st, c:c + 1]).then_inc(sc_read, 1)
                    dve.wait_ge(sc_read, at(i, NC * ST, NC * st + NC))
                    own(dve.tensor_reduce(nmx[:, st:st + 1], mx[:, st, :], AX_X, ALU.max, negate=True))
                    dve.tensor_scalar(nmx[:, st:st + 1], nmx[:, st:st + 1], SCALE, None, ALU.mult)\
                       .then_inc(nmx_ready, 1)
                    if st == 0:
                        s.norm_before(dve, before)
                dve.wait_ge(m_loaded, at(i, 16, 16))
                dve.tensor_reduce(any_[:], m8[:], AX_X, ALU.max).then_inc(any_ready, 1)
                dve.wait_ge(any_ready, at(i, 1, 1))
                dve.wait_ge(exp_done, at(i, ST, ST))
                own(dve.reciprocal(rs[:], sums[:]))
                own(dve.tensor_scalar(rs[:], rs[:], any_[:], None, ALU.mult))
                own.end()
                dve.wait_ge(s.x_kept, at(i, 1, 1))
                dve.wait_ge(o_ps, at(i, ST, ST))
                for st in range(ST):
                    last = dve.scalar_tensor_tensor(s.z[:, st, :], ps[:, OB, st * D:(st + 1) * D], rs[:, st:st + 1],
                                                    s.xr[:, st, :], ALU.mult, ALU.add)
                last.then_inc(s.z_made, 1)

            s.each_sequence(dve, sequence)
    s.close()


def rotary_stage(k, x_in, x_out, wq, bq, wk, bk, wv, bv, wo, bo, key_w, cos_in, sin_in):
    nc, ps, ident = k.nc, k.ps, k.ident
    NH, NKV, HD = 32, 8, 64
    HALF = HD // 2
    QUARTERS = NH // NKV
    G = NH // NKV
    OT = NH * HD // P
    OW = NH * HD
    W3 = 3 * P
    SCALE = float(HD) ** -0.5
    SPLITS = 6
    WSCALE = 64.0
    PSCALE = 15 * float(np.log(2.0))
    PASSES = ((0, 0), (0, 1), (1, 0))
    s = Stage(k, "rotary", x_in, x_out)
    wq_p, wk_p, wv_p, wo_p = ([s.sb(f"{name}_{part}", [P, c, n], F16) for part in ("hi", "lo")]
                              for name, c, n in (("wq", DC, OW), ("wk", DC, NKV * HD), ("wv", DC, NKV * HD),
                                                 ("wo", OT, D)))
    bq_s, bk_s, bv_s, bo_s = s.sb("bq", [P, OW]), s.sb("bk", [P, 512]), s.sb("bv", [P, 512]), s.sb("bo", [P, D])
    kw = s.sb("kw", [P, NH])
    ident16 = s.sb("ident16", [P, P], F16)
    cos, sin = s.sb("cos", [P, ST, HALF]), s.sb("sin", [P, ST, HALF])
    nsin = s.sb("nsin", [P, ST, HALF])
    cm = s.sb("cm", [P, W3])
    raw = [s.sb(f"raw{n}", [P, 512]) for n in range(2)]
    byc = [s.sb(f"byc{n}", [P, 512]) for n in range(2)]
    rot = [s.sb(f"rot{n}", [P, 512]) for n in range(2)]
    bys = s.sb("bys", [P, 512])
    split = [s.sb(f"split{n}", [P, NKV, 2, HD], F16) for n in range(SPLITS)]
    kT = [s.sb(f"kT_{part}", [P, NKV, S], F16) for part in ("hi", "lo")]
    v_f = [s.sb(f"v_f{n}", [P, NKV * HD]) for n in range(ST)]
    v = [s.sb(f"v_{part}", [P, ST, NKV * HD], F16) for part in ("hi", "lo")]
    qT = s.sb("qT", [P, ST, NH, P], F16)
    sc = [s.sb(f"sc{n}", [P, W3]) for n in range(4)]
    pT = [[s.sb(f"pT{n}_{part}", [P, W3], F16) for part in ("hi", "lo")] for n in range(4)]
    mx, nmx, sums, rs = (s.sb("mx", [P, 4, ST]), s.sb("nmx", [P, 4, ST]), s.sb("sums", [P, NH, ST]),
                         s.sb("rs", [P, G * ST]))
    o = s.sb("o", [P, ST, OW])
    oT = [s.sb(f"oT_{part}", [P, ST, OT, P], F16) for part in ("hi", "lo")]
    xT_p = [s.xT[:].rearrange("p c s -> p (c s)").bitcast(F16)[:, n * DC * S:(n + 1) * DC * S]
            .rearrange("p (c s) -> p c s", c=DC) for n in range(2)]
    w_in = [(wk_p, wk, raw[0][:], raw[1][:]), (wv_p, wv, byc[0][:], byc[1][:])]
    wq_in = qT[:].rearrange("p s n q -> p (s n q)").bitcast(F32)
    wo_in = o[:].rearrange("p s n -> p (s n)")
    (w_loaded, const_ready, w_hi, w_ready, xT_hi, pr_ps, raw_ready, byc_ready, bys_ready, rot_ready, split_hi,
     k_split, q_split, turn_ps, turned, v_ps, v_sum, v_hi, v_ready) = (s.sem(n) for n in (
            "w_loaded", "const_ready", "w_hi", "w_ready", "xT_hi", "pr_ps", "raw_ready", "byc_ready", "bys_ready",
            "rot_ready", "split_hi", "k_split", "q_split", "turn_ps", "turned", "v_ps", "v_sum", "v_hi", "v_ready"))
    (sc_ps, sc_read, nmx_ready, exp_done, t_ps, pT_hi, pT_ready, o_ps, o_ready, oT_ps, oT_hi, oT_ready, y_ps,
     dve_own) = (s.sem(n) for n in (
            "sc_ps", "sc_read", "nmx_ready", "exp_done", "t_ps", "pT_hi", "pT_ready", "o_ps", "o_ready", "oT_ps",
            "oT_hi", "oT_ready", "y_ps", "dve_own"))
    tiles = [("k", st, 0) for st in range(ST)] + [("q", st, a) for st in range(ST) for a in range(QUARTERS)]
    NT = len(tiles)
    turns = [(j, part) for j in range(ST) for part in range(2)] + [(j, 0) for j in range(ST, NT)]
    NTURN = len(turns)
    first_turn = lambda j: 2 * j if j < ST else j + ST
    LAG = 3
    TB, OB, XB = (4, 5), (6, 7), 7
    half = lambda n: ps[:, TB[n % 2], :].bitcast(F16)
    GROUPS = NH // G
    OTT = ST * OT // 4

    with nc.Block() as block:
        @block.sync
        def _(sp):
            def w(t_, a):
                sp.dma_start(t_, a).then_inc(w_loaded, 16)

            for parts, a, in0, in1 in w_in:
                w(in0, a[0:P, :])
                w(in1, a[P:2 * P, :])
            w(wq_in.rearrange("p (c n) -> p c n", c=DC), wq.rearrange("(c p) n -> p c n", p=P))
            for t_, a in ((bk_s, bk), (bv_s, bv), (bq_s, bq), (bo_s, bo), (kw, key_w)):
                w(t_[:], a.partition_broadcast(P))
            w(cos[:], cos_in.rearrange("(s p) e -> p s e", p=P))
            w(sin[:], sin_in.rearrange("(s p) e -> p s e", p=P))
            w(wo_in.rearrange("p (q n) -> p q n", q=OT), wo.rearrange("(q p) n -> p q n", p=P))
            s.rows_dma(sp)

        W_ALL = 16 * (4 + 1 + 5 + 2 + 1)
        W_SPLITS = 4 + 1 + 1

        @block.gpsimd
        def _(pool):
            own = Chain(pool, s.pool_own)
            own(pool.memset(cm[:], 0.0))
            for a in (0, 2 * P):
                last = pool.affine_select(out=cm[:, a:a + P], in_=cm[:, a:a + P], compare_op=ALU.is_ge, fill=-1e30,
                                          base=0, pattern=[[-1, P]], channel_multiplier=1)
            last.then_inc(const_ready, 1)
            pool.wait_ge(w_ready, W_SPLITS)
            with pool.Fori(0, B) as i:
                s.keep_x(pool, i, bo_s[:])
                def low_part(j):
                    f = first_turn(j) % SPLITS
                    pool.wait_ge(split_hi, at(i, NT, j + 1))
                    pool.tensor_tensor(split[f][:, :, 1, :], rot[j % 2][:].rearrange("p (h e) -> p h e", e=HD),
                                       split[f][:, :, 0, :], ALU.subtract).then_inc(q_split, 1)

                for j, (kind, st, a) in enumerate(tiles):
                    pool.wait_ge(raw_ready, at(i, NT, j + 1))
                    if j >= 2:
                        pool.wait_ge(rot_ready, at(i, NT, j - 1))
                    pool.tensor_tensor(byc[j % 2][:].rearrange("p (h e) -> p h e", e=HALF),
                                       raw[j % 2][:].rearrange("p (h e) -> p h e", e=HALF),
                                       cos[:, st, :].unsqueeze(1).to_broadcast([P, 16, HALF]), ALU.mult)\
                        .then_inc(byc_ready, 1)
                    if j > ST:
                        low_part(j - 1)
                low_part(NT - 1)
                for n in range(NH):
                    pool.wait_ge(sc_read, at(i, NH * ST, ST * n + ST))
                    s.carry(pool)
                    pool.tensor_scalar(nmx[:, n % 4, :], mx[:, n % 4, :], -SCALE, PSCALE, ALU.mult, ALU.add)\
                        .then_inc(nmx_ready, 1)
                s.norm_pool(pool, i)

        @block.tensor
        def _(pe):
            pe.wait_ge(w_ready, W_SPLITS)
            with pe.Fori(0, B) as i:
                def product(out, st, right, n0, n1):
                    for dc in range(DC):
                        for lp, rp in PASSES:
                            last = pe.matmul(out, xT_p[lp][:, dc, st * P:(st + 1) * P], right[rp][:, dc, n0:n1],
                                             start=dc + lp + rp == 0, stop=dc == DC - 1 and lp == 1)
                    return last

                def project(j):
                    kind, st, a = tiles[j]
                    if j >= 2:
                        pe.wait_ge(raw_ready, at(i, NT, j - 1))
                    if kind == "k":
                        product(ps[:, j % 2, :], st, wk_p, 0, 512).then_inc(pr_ps, 1)
                        product(ps[:, 2 + st, :], st, wv_p, 0, 512).then_inc(v_ps, 1)
                    else:
                        product(ps[:, j % 2, :], st, wq_p, a * 512, (a + 1) * 512).then_inc(pr_ps, 1)

                def turn(x):
                    j, part = turns[x]
                    if j < ST and part == 0:
                        pe.wait_ge(split_hi, at(i, NT, j + 1))
                    elif j < ST:
                        pe.wait_ge(k_split, at(i, ST, j + 1))
                    else:
                        pe.wait_ge(q_split, at(i, NT - ST, j - ST + 1))
                    if x >= 2:
                        pe.wait_ge(turned, at(i, NTURN, x - 1))
                    for h in range(NKV):
                        last = pe.transpose(half(x)[:, h * P:(h + 1) * P],
                                            split[x % SPLITS][:, h, :, :].rearrange("p t e -> p (t e)"), ident16[:])
                    last.then_inc(turn_ps, 1)

                def scores(n):
                    if n >= 4:
                        pe.wait_ge(sc_read, at(i, NH * ST, ST * (n - 3)))
                    for st in range(ST):
                        for part in range(2):
                            last = pe.matmul(ps[:, n % 4, st * P:st * P + (st + 1) * P], qT[:, st, n, :],
                                             kT[part][:, n // G, 0:(st + 1) * P], start=part == 0, stop=part == 1)
                    last.then_inc(sc_ps, 1)

                def turn_probs(n):
                    pe.wait_ge(exp_done, at(i, NH, n + 1))
                    if n >= 2:
                        pe.wait_ge(pT_ready, at(i, NH, n - 1))
                    for q in range(3):
                        last = pe.transpose(ps[:, TB[n % 2], q * P:(q + 1) * P], sc[n % 4][:, q * P:(q + 1) * P],
                                            ident[:])
                    last.then_inc(t_ps, 1)

                def mix(n):
                    kv = n // G
                    out = lambda st: ps[:, OB[n // G % 2], (n % G * ST + st) * HD:(n % G * ST + st + 1) * HD]
                    pe.wait_ge(pT_ready, at(i, NH, n + 1))
                    if n % G == 0 and n >= 2 * G:
                        pe.wait_ge(o_ready, at(i, GROUPS, n // G - 1))
                    for q, st, kt in ((0, 0, 0), (1, 1, 0), (2, 1, 1)):
                        for pp, vv in PASSES:
                            last = pe.matmul(out(st), pT[n % 4][pp][:, q * P:(q + 1) * P],
                                             v[vv][:, kt, kv * HD:(kv + 1) * HD], start=kt + pp + vv == 0,
                                             stop=kt == st and pp == 1)
                    last.then_inc(o_ps, 1)

                s.transpose_x(pe, i, ps[:, XB, :])
                pe.wait_ge(s.z_made, at(i, 1, 1))
                pe.wait_ge(s.xT_ready, at(i, 1, 1))
                x = 0
                for j in range(NT + LAG):
                    if j < NT:
                        project(j)
                    while j >= LAG and x < NTURN and turns[x][0] <= j - LAG:
                        turn(x)
                        x += 1
                pe.wait_ge(turned, at(i, NTURN, NTURN))
                pe.wait_ge(v_ready, at(i, ST, ST))
                for n in range(-3, NH):
                    if n + 3 < NH:
                        scores(n + 3)
                    if n >= 0:
                        turn_probs(n)
                    if n >= 2:
                        mix(n - 2)
                mix(NH - 2)
                mix(NH - 1)
                pe.wait_ge(o_ready, at(i, GROUPS, GROUPS))
                for t in range(OTT):
                    st, p0 = divmod(4 * t, OT)
                    if t >= 2:
                        pe.wait_ge(oT_ready, at(i, OTT, t - 1))
                    for q in range(4):
                        last = pe.transpose(ps[:, TB[t % 2], q * P:(q + 1) * P],
                                            o[:, st, (p0 + q) * P:(p0 + q + 1) * P], ident[:])
                    last.then_inc(oT_ps, 1)
                    for u in ([t - 2] if t >= 2 else []) + ([OTT - 2, OTT - 1] if t == OTT - 1 else []):
                        pe.wait_ge(oT_ready, at(i, OTT, u + 1))
                        ut, u0 = divmod(4 * u, OT)
                        for p in range(u0, u0 + 4):
                            for lp, rp in PASSES:
                                last = pe.matmul(ps[:, ut, 0:D], oT[lp][:, ut, p, :], wo_p[rp][:, p, :],
                                                 start=p + lp + rp == 0, stop=p == OT - 1 and lp == 1)
                last.then_inc(y_ps, 1)

        @block.scalar
        def _(act):
            act.wait_ge(w_loaded, W_ALL)
            x = 0
            for parts, a, in0, in1 in w_in:
                for dc, w in enumerate((in0, in1)):
                    act.activation(parts[0][:, dc, :], w, ACT.Copy, scale=WSCALE).then_inc(w_hi, 1)
            act.activation(wo_p[0][:].rearrange("p q n -> p (q n)"), wo_in, ACT.Copy, scale=WSCALE).then_inc(w_hi, 1)
            act.wait_ge(const_ready, 2)
            act.copy(wq_p[0][:].rearrange("p c n -> p (c n)"), wq_in).then_inc(w_hi, 1)
            act.wait_ge(w_ready, W_SPLITS)
            with act.Fori(0, B) as i:
                act.wait_ge(s.xT_ps, at(i, 1, 1))
                act.copy(xT_p[0].rearrange("p c s -> p (c s)"), ps[:, XB, :]).then_inc(xT_hi, 1)

                def high_part(j):
                    kind, st, a = tiles[j]
                    f = first_turn(j)
                    x = rot[j % 2][:].rearrange("p (h e) -> p h e", e=HD)
                    act.wait_ge(rot_ready, at(i, NT, j + 1))
                    if f >= SPLITS:
                        act.wait_ge(turn_ps, at(i, NTURN, f - SPLITS + 1))
                    if kind == "k":
                        act.copy(split[f][:], x.unsqueeze(2).to_broadcast([P, NKV, 2, HD])).then_inc(split_hi, 1)
                        act.wait_ge(v_sum, at(i, ST, st + 1))
                        act.copy(v[0][:, st, :], v_f[st][:]).then_inc(v_hi, 1)
                    else:
                        act.copy(split[f % SPLITS][:, :, 0, :], x).then_inc(split_hi, 1)

                def turned_copy(x):
                    j, part = turns[x]
                    kind, st, a = tiles[j]
                    act.wait_ge(turn_ps, at(i, NTURN, x + 1))
                    if kind == "k":
                        act.copy(kT[part][:, :, st * P:(st + 1) * P], half(x).rearrange("p (g e) -> p g e", g=NKV))\
                           .then_inc(turned, 1)
                    else:
                        act.copy(qT[:, st, NKV * a:NKV * (a + 1), :].rearrange("p n q -> p (n q)"), half(x))\
                           .then_inc(turned, 1)

                x = 0
                for j in range(NT + LAG):
                    while j >= LAG and x < NTURN and turns[x][0] <= j - LAG:
                        turned_copy(x)
                        x += 1
                    if j < NT:
                        high_part(j)

                def exp(n):
                    act.wait_ge(nmx_ready, at(i, NH, n + 1))
                    for st in range(ST):
                        part = sc[n % 4][:, st * P:st * P + (st + 1) * P]
                        last = act.activation(part, part, ACT.Exp, bias=nmx[:, n % 4, st:st + 1], scale=SCALE,
                                              accum_out=sums[:, n, st:st + 1])
                    last.then_inc(exp_done, 1)

                exp(0)
                for n in range(NH):
                    if n + 1 < NH:
                        exp(n + 1)
                    if n >= 4:
                        act.wait_ge(o_ps, at(i, NH, n - 3))
                    act.wait_ge(t_ps, at(i, NH, n + 1))
                    act.copy(pT[n % 4][0][:], ps[:, TB[n % 2], 0:W3]).then_inc(pT_hi, 1)
                for t in range(OTT):
                    st, p0 = divmod(4 * t, OT)
                    act.wait_ge(oT_ps, at(i, OTT, t + 1))
                    act.copy(oT[0][:, st, p0:p0 + 4, :].rearrange("p q s -> p (q s)"), ps[:, TB[t % 2], :])\
                       .then_inc(oT_hi, 1)

        @block.vector
        def _(dve):
            s.credits(dve)
            dve.wait_ge(w_loaded, W_ALL)
            dve.wait_ge(const_ready, 1)
            own0 = Chain(dve, s.own2)
            for dc in range(DC):
                w = wq_in[:, dc * OW:(dc + 1) * OW].rearrange("p (n e) -> p n e", n=NH)
                dve.scalar_tensor_tensor(w, w, WSCALE, kw[:].unsqueeze(2).to_broadcast([P, NH, HD]), ALU.mult, ALU.mult)
            dve.tensor_tensor(bq_s[:].rearrange("p (n e) -> p n e", e=HD), bq_s[:].rearrange("p (n e) -> p n e", e=HD),
                              kw[:].unsqueeze(2).to_broadcast([P, NH, HD]), ALU.mult)
            dve.tensor_copy(ident16[:], ident[:])
            own0(dve.tensor_scalar(nsin[:], sin[:], -1.0, None, ALU.mult))
            dve.sem_inc(const_ready, 1)
            x = 0
            for parts, a, in0, in1 in w_in:
                for dc, w in enumerate((in0, in1)):
                    x += 1
                    dve.wait_ge(w_hi, x)
                    dve.scalar_tensor_tensor(parts[1][:, dc, :], w, WSCALE, parts[0][:, dc, :], ALU.mult, ALU.subtract)\
                       .then_inc(w_ready, 1)
            dve.wait_ge(w_hi, x + 1)
            dve.scalar_tensor_tensor(wo_p[1][:].rearrange("p q n -> p (q n)"), wo_in, WSCALE,
                                     wo_p[0][:].rearrange("p q n -> p (q n)"), ALU.mult, ALU.subtract)\
               .then_inc(w_ready, 1)
            dve.wait_ge(w_hi, x + 2)
            dve.tensor_tensor(wq_p[1][:].rearrange("p c n -> p (c n)"), wq_in,
                              wq_p[0][:].rearrange("p c n -> p (c n)"), ALU.subtract).then_inc(w_ready, 1)
            dve.wait_ge(w_ready, W_SPLITS)

            def sequence(i, before):
                own = Chain(dve, dve_own, NH // G, i)

                def biased(j):
                    kind, st, a = tiles[j]
                    dve.wait_ge(pr_ps, at(i, NT, j + 1))
                    if j >= 2:
                        dve.wait_ge(byc_ready, at(i, NT, j - 1))
                    dve.scalar_tensor_tensor(raw[j % 2][:], ps[:, j % 2, :], 1.0 / WSCALE,
                                             bk_s[:] if kind == "k" else bq_s[:, a * 512:(a + 1) * 512], ALU.mult,
                                             ALU.add).then_inc(raw_ready, 1)
                    if kind == "k":
                        dve.wait_ge(v_ps, at(i, ST, st + 1))
                        dve.scalar_tensor_tensor(v_f[st][:], ps[:, 2 + st, :], 1.0 / WSCALE, bv_s[:], ALU.mult,
                                                 ALU.add).then_inc(v_sum, 1)

                def rotate(j):
                    kind, st, a = tiles[j]
                    x = raw[j % 2][:].rearrange("p (h t e) -> p h t e", t=2, e=HALF)
                    y = bys[:].rearrange("p (h t e) -> p h t e", t=2, e=HALF)
                    dve.wait_ge(raw_ready, at(i, NT, j + 1))
                    if j >= 1:
                        dve.wait_ge(rot_ready, at(i, NT, j))
                    for half_, table in ((0, nsin), (1, sin)):
                        last = dve.tensor_tensor(y[:, :, half_, :], x[:, :, 1 - half_, :],
                                                 table[:, st, :].unsqueeze(1).to_broadcast([P, 8, HALF]), ALU.mult)
                    last.then_inc(bys_ready, 1)
                    dve.wait_ge(bys_ready, at(i, NT, j + 1))
                    dve.wait_ge(byc_ready, at(i, NT, j + 1))
                    if j >= 2:
                        n = j - 1
                        dve.wait_ge(*((k_split, at(i, ST, n)) if n <= ST else (q_split, at(i, NT - ST, n - ST))))
                    dve.tensor_tensor(rot[j % 2][:], byc[j % 2][:], bys[:], ALU.add).then_inc(rot_ready, 1)

                dve.wait_ge(xT_hi, at(i, 1, 1))
                dve.tensor_tensor(xT_p[1].rearrange("p c s -> p (c s)"), ps[:, XB, :],
                                  xT_p[0].rearrange("p c s -> p (c s)"), ALU.subtract).then_inc(s.xT_ready, 1)
                s.norm_before(dve, before)
                biased(0)
                for j in range(NT):
                    if j + 1 < NT:
                        biased(j + 1)
                    rotate(j)
                    if 1 <= j <= ST:
                        f = first_turn(j - 1)
                        dve.wait_ge(split_hi, at(i, NT, j))
                        dve.tensor_tensor(split[f + 1][:], rot[j - 1][:].rearrange("p (h e) -> p h e", e=HD)
                                          .unsqueeze(2).to_broadcast([P, NKV, 2, HD]), split[f][:], ALU.subtract)\
                           .then_inc(k_split, 1)
                        dve.wait_ge(v_hi, at(i, ST, j))
                        dve.tensor_tensor(v[1][:, j - 1, :], v_f[j - 1][:], v[0][:, j - 1, :], ALU.subtract)\
                           .then_inc(v_ready, 1)

                def maxima(n):
                    dve.wait_ge(sc_ps, at(i, NH, n + 1))
                    if n >= 4:
                        dve.wait_ge(t_ps, at(i, NH, n - 3))
                    for st in range(ST):
                        a, b = st * P, st * P + (st + 1) * P
                        s.carry(dve)
                        dve.tensor_tensor_reduce(sc[n % 4][:, a:b], ps[:, n % 4, a:b], cm[:, a:b], 1.0, -3.0e38,
                                                 ALU.add, ALU.max, mx[:, n % 4, st:st + 1]).then_inc(sc_read, 1)

                def low_part(n):
                    dve.wait_ge(pT_hi, at(i, NH, n + 1))
                    dve.tensor_tensor(pT[n % 4][1][:], ps[:, TB[n % 2], 0:W3], pT[n % 4][0][:], ALU.subtract)\
                       .then_inc(pT_ready, 1)

                def outputs(g):
                    dve.wait_ge(exp_done, at(i, NH, G * g + G))
                    if g >= 1:
                        dve.wait_ge(o_ready, at(i, GROUPS, g))
                    own(dve.reciprocal(rs[:], sums[:, G * g:G * g + G, :].rearrange("p n s -> p (n s)")))
                    dve.wait_ge(o_ps, at(i, NH, G * g + G))
                    dve.tensor_tensor(
                        o[:, :, G * g * HD:(G * g + G) * HD].rearrange("p s (n d) -> p n s d", n=G),
                        ps[:, OB[g % 2], :].rearrange("p (n s d) -> p n s d", n=G, s=ST),
                        rs[:].rearrange("p (n s) -> p n s", n=G).unsqueeze(3).to_broadcast([P, G, ST, HD]),
                        ALU.mult).then_inc(o_ready, 1)

                for n in range(-3, NH + 3):
                    if 0 <= n + 3 < NH:
                        maxima(n + 3)
                    if 0 <= n < NH:
                        low_part(n)
                    if n >= G and n % G == 2:
                        outputs(n // G - 1)
                for t in range(OTT):
                    st, p0 = divmod(4 * t, OT)
                    dve.wait_ge(oT_hi, at(i, OTT, t + 1))
                    hi, lo = (t_[:, st, p0:p0 + 4, :].rearrange("p q s -> p (q s)") for t_ in oT)
                    dve.tensor_tensor(lo, ps[:, TB[t % 2], :], hi, ALU.subtract).then_inc(oT_ready, 1)
                dve.wait_ge(s.x_kept, at(i, 1, 1))
                dve.wait_ge(y_ps, at(i, 1, 1))
                for st in range(ST):
                    last = dve.scalar_tensor_tensor(s.z[:, st, :], ps[:, st, 0:D], 1.0 / WSCALE, s.xr[:, st, :],
                                                    ALU.mult, ALU.add)
                last.then_inc(s.z_made, 1)

            s.each_sequence(dve, sequence)
    s.close()


def routed_stage(k, x_in, x_out, router, w1, b1, w2, b2):
    nc, ps, ident = k.nc, k.ps, k.ident
    E, CAP, K = router.shape[1], 64, 2
    F = w1.shape[1]
    FC = F // P
    NT = B * ST
    s = Stage(k, "route", x_in, x_out)
    rw, w1_s, w2_s = s.sb("rw", [P, DC, E]), s.sb("w1", [P, DC, F]), s.sb("w2", [P, FC, D])
    b1_s, b2_s = s.sb("b1", [P, FC]), s.sb("b2", [P, D])
    hT = s.sb("hT", [P, FC, S])
    y = s.sb("y", [P, ST, D])
    lg = s.sb("lg", [P, ST, E])
    lgs = s.sb("lgs", [P, NT, E])
    pref = s.sb("pref", [P, E])
    prefi = s.sb("prefi", [P, E], I32)
    upto, ones = s.sb("upto", [P, P]), s.sb("ones", [P, P])
    reset = s.sb("reset", [P, E, K * NT])
    pick = s.sb("pick", [P, K, NT, E])
    rank = s.sb("rank", [P, K * NT, E])
    total, before = s.sb("total", [P, E, K * NT]), s.sb("before", [P, E, K * NT])
    tmp, pw = s.sb("tmp", [P, NT, E]), s.sb("pw", [P, NT, E])
    m1, m2, den, w = s.sb("m1", [P, NT]), s.sb("m2", [P, NT]), s.sb("den", [P, NT]), s.sb("w", [P, NT])
    wb = s.sb("wb", [P, ST])
    (w_loaded, const_ready, h_ps, hT_ready, y_ps, y_ready, y_stored, lg_ps, lg_ready, lg_moved, ch, ex, rank_ps,
     w_ready, wb_loaded, y_loaded) = (s.sem(n) for n in (
        "w_loaded", "const_ready", "h_ps", "hT_ready", "y_ps", "y_ready", "y_stored", "lg_ps", "lg_ready",
        "lg_moved", "ch", "ex", "rank_ps", "w_ready", "wb_loaded", "y_loaded"))
    y_dram = nc.dram_tensor("mlp_rows", [B, P, ST * D], F32, kind="Internal").ap()
    XB, YB, LB = 5, 6, 7

    with nc.Block() as block:
        @block.sync
        def _(sp):
            sp.dma_start(rw[:], router.rearrange("(c p) n -> p c n", p=P)).then_inc(w_loaded, 16)
            sp.dma_start(w1_s[:], w1.rearrange("(c p) n -> p c n", p=P)).then_inc(w_loaded, 16)
            sp.dma_start(w2_s[:], w2.rearrange("(c p) n -> p c n", p=P)).then_inc(w_loaded, 16)
            sp.dma_start(b1_s[:], b1).then_inc(w_loaded, 16)
            sp.dma_start(b2_s[:], b2.partition_broadcast(P)).then_inc(w_loaded, 16)

            def keep(i):
                sp.wait_ge(lg_ready, at(i, 1, 1))
                s.carry(sp)
                sp.dma_start(lgs[:, bass.ds(i * ST, ST), :], lg[:]).then_inc(lg_moved, 16)
                sp.wait_ge(y_ready, at(i, 1, 1))
                sp.dma_start(one(y_dram, i), y[:].rearrange("p s d -> p (s d)")).then_inc(y_stored, 16)

            s.load_x(sp, 0, False)
            with sp.Fori(0, B - 1) as i:
                s.load_x(sp, i + 1, False)
                keep(i)
            keep(B - 1)
            sp.wait_ge(y_stored, 16 * (B + 1))

        @block.gpsimd
        def _(pool):
            own = Chain(pool, s.pool_own)
            pool.memset(ones[:], 1.0)
            pool.memset(upto[:], 1.0)
            pool.memset(reset[:], 1.0)
            own(pool.iota(prefi[:], [[-1, E]], base=E, channel_multiplier=0))
            pool.affine_select(out=upto[:], in_=upto[:], compare_op=ALU.is_ge, fill=0.0, base=0, pattern=[[1, P]],
                               channel_multiplier=-1)
            own(pool.memset(reset[:, :, 0:1], 0.0))
            pool.sem_inc(const_ready, 1)

        @block.tensor
        def _(pe):
            pe.wait_ge(w_loaded, 16 * 5)
            pe.wait_ge(const_ready, 1)
            with pe.Fori(0, B) as i:
                s.transpose_x(pe, i, ps[:, XB, :])
                pe.wait_ge(s.z_made, at(i, 1, 1))
                pe.wait_ge(s.xT_ready, at(i, 1, 1))
                for st in range(ST):
                    for dc in range(DC):
                        last = pe.matmul(ps[:, LB, st * E:(st + 1) * E], s.xT[:, dc, st * P:(st + 1) * P],
                                         rw[:, dc, :], start=dc == 0, stop=dc == DC - 1)
                last.then_inc(lg_ps, 1)
                for f in range(FC):
                    if f >= 4:
                        pe.wait_ge(hT_ready, at(i, FC, f - 3))
                    for dc in range(DC):
                        last = pe.matmul(ps[:, f % 4, 0:S], w1_s[:, dc, f * P:(f + 1) * P], s.xT[:, dc, :],
                                         start=dc == 0, stop=dc == DC - 1)
                    last.then_inc(h_ps, 1)
                for st in range(ST):
                    for f in range(FC):
                        if st == 0:
                            pe.wait_ge(hT_ready, at(i, FC, f + 1))
                        last = pe.matmul(ps[:, YB, st * D:(st + 1) * D], hT[:, f, st * P:(st + 1) * P], w2_s[:, f, :],
                                         start=f == 0, stop=f == FC - 1)
                last.then_inc(y_ps, 1)

        @block.scalar
        def _(act):
            act.wait_ge(w_loaded, 16 * 5)
            with act.Fori(0, B) as i:
                s.copy_xT(act, i, ps[:, XB, :])
                for f in range(FC):
                    act.wait_ge(h_ps, at(i, FC, f + 1))
                    act.activation(hT[:, f, :], ps[:, f % 4, 0:S], ACT.Gelu, bias=b1_s[:, f:f + 1]).then_inc(hT_ready, 1)

        @block.vector
        def _(dve):
            dve.sem_inc(s.z_made, 1)
            dve.sem_inc(lg_moved, 16)
            dve.sem_inc(y_stored, 16)
            dve.wait_ge(w_loaded, 16 * 5)
            dve.wait_ge(const_ready, 1)
            dve.tensor_copy(pref[:], prefi[:])
            with dve.Fori(0, B) as i:
                dve.wait_ge(lg_ps, at(i, 1, 1))
                dve.wait_ge(lg_moved, at(i, 16, 16))
                dve.tensor_copy(lg[:].rearrange("p s e -> p (s e)"), ps[:, LB, 0:ST * E]).then_inc(lg_ready, 1)
                dve.wait_ge(y_ps, at(i, 1, 1))
                dve.wait_ge(y_stored, at(i, 16, 16))
                dve.tensor_tensor(y[:], ps[:, YB, :].rearrange("p (s d) -> p s d", s=ST),
                                  b2_s[:].unsqueeze(1).to_broadcast([P, ST, D]), ALU.add).then_inc(y_ready, 1)
                dve.wait_ge(y_ready, at(i, 1, 1))
                dve.sem_inc(s.z_made, 1)

    all_e = lambda t_: t_[:].unsqueeze(2).to_broadcast([P, NT, E])
    with nc.Block() as block:
        @block.tensor
        def _(pe):
            pe.wait_ge(w_ready, 1)
            picks = pick[:].rearrange("p k t e -> p (k t e)")
            pe.matmul(ps[:, 0, 0:K * NT * E], upto[:], picks, start=True, stop=True)
            pe.matmul(ps[:, 1, 0:K * NT * E], ones[:], picks, start=True, stop=True).then_inc(rank_ps, 1)

        @block.scalar
        def _(act):
            act.wait_ge(ex, 1)
            act.activation(lgs[:], lgs[:], ACT.Exp).then_inc(ex, 1)

        @block.vector
        def _(dve):
            own = Chain(dve, ch)
            own(dve.tensor_reduce(m1[:], lgs[:], AX_X, ALU.max))
            own(dve.tensor_tensor(lgs[:], lgs[:], all_e(m1), ALU.subtract))
            dve.sem_inc(ex, 1)
            dve.wait_ge(ex, 2)
            own(dve.tensor_reduce(den[:], lgs[:], AX_X, ALU.add))
            own(dve.reciprocal(den[:], den[:]))
            own(dve.tensor_tensor(lgs[:], lgs[:], all_e(den), ALU.mult))
            own(dve.tensor_copy(pw[:], lgs[:]))
            for c in range(K):
                own(dve.tensor_reduce(m1[:], pw[:], AX_X, ALU.max))
                own(dve.tensor_tensor(tmp[:], pw[:], all_e(m1), ALU.is_equal))
                own(dve.tensor_tensor(tmp[:], tmp[:], pref[:].unsqueeze(1).to_broadcast([P, NT, E]), ALU.mult))
                own(dve.tensor_reduce(m2[:], tmp[:], AX_X, ALU.max))
                own(dve.tensor_tensor(pick[:, c], tmp[:], all_e(m2), ALU.is_equal))
                own(dve.scalar_tensor_tensor(pw[:], pick[:, c], -4.0, pw[:], ALU.mult, ALU.add))
            dve.sem_inc(w_ready, 1)
            dve.wait_ge(rank_ps, 1)
            own(dve.tensor_copy(total[:], ps[:, 1, 0:K * NT * E].rearrange("p (t e) -> p e t", e=E)))
            own(dve.tensor_tensor_scan(before[:].rearrange("p e t -> p (e t)"), reset[:].rearrange("p e t -> p (e t)"),
                                       total[:].rearrange("p e t -> p (e t)"), 0.0, ALU.mult, ALU.add))
            own(dve.tensor_tensor(before[:], before[:], total[:], ALU.subtract))
            own(dve.tensor_tensor(rank[:], ps[:, 0, 0:K * NT * E].rearrange("p (t e) -> p t e", e=E),
                                  before[:].rearrange("p e t -> p t e"), ALU.add))
            own(dve.scalar_tensor_tensor(rank[:].rearrange("p t e -> p (t e)"), rank[:].rearrange("p t e -> p (t e)"),
                                         CAP + 0.5, pick[:].rearrange("p k t e -> p (k t e)"), ALU.is_lt, ALU.mult))
            kept = rank[:].rearrange("p (k t) e -> p k t e", k=K)
            own(dve.tensor_tensor(tmp[:], kept[:, 0], kept[:, 1], ALU.add))
            own(dve.tensor_tensor(tmp[:], tmp[:], lgs[:], ALU.mult))
            own(dve.tensor_reduce(w[:], tmp[:], AX_X, ALU.add))

    x2, y2 = s.sb("x2", [P, ST, D]), s.sb("y2", [P, ST, D])
    in2, free2 = s.sem("in2"), s.sem("free2")
    with nc.Block() as block:
        @block.sync
        def _(sp):
            def rows(i):
                sp.wait_ge(free2, at(i, 1, 1))
                s.carry(sp)
                sp.dma_start(x2[:], one(s.x_in, i)).then_inc(in2, 16)
                sp.dma_start(y2[:].rearrange("p s d -> p (s d)"), one(y_dram, i)).then_inc(in2, 16)
                sp.dma_start(wb[:], w[:, bass.ds(i * ST, ST)]).then_inc(in2, 16)

            rows(0)
            with sp.Fori(0, B - 1) as i:
                rows(i + 1)
                s.store_x(sp, i)
            s.store_x(sp, B - 1)
            sp.wait_ge(s.xo_stored, 16 * (B + 1))

        @block.gpsimd
        def _(pool):
            with pool.Fori(0, B) as i:
                s.norm_pool(pool, i)

        @block.vector
        def _(dve):
            dve.sem_inc(free2, 1)
            dve.sem_inc(s.xo_stored, 16)
            with dve.Fori(0, B) as i:
                own = Chain(dve, s.own2, 1, i)
                dve.wait_ge(in2, at(i, 48, 48))
                for st in range(ST):
                    last = dve.scalar_tensor_tensor(s.z[:, st, :], y2[:, st, :], wb[:, st:st + 1], x2[:, st, :],
                                                    ALU.mult, ALU.add)
                own(last)
                dve.sem_inc(free2, 1)
                s.norm_dve(dve, i, wait=False)
    s.close()


class Kernel:

    def __init__(self, nc, ctx):
        self.nc = nc
        self.ps = ctx.enter_context(nc.psum_tensor("ps", [P, 8, BANK], F32))
        self.ident = ctx.enter_context(nc.sbuf_tensor("ident", [P, P], F32))
        self.neg_half = ctx.enter_context(nc.sbuf_tensor("neg_half", [P, 64], F32))
        const = ctx.enter_context(nc.semaphore("common_consts"))
        with nc.Block() as block:
            @block.gpsimd
            def _(pool):
                own = Chain(pool, const)
                pool.memset(self.neg_half[:], -0.5)
                own(pool.memset(self.ident[:], 0.0))
                own(pool.affine_select(out=self.ident[:], in_=self.ident[:], compare_op=ALU.not_equal, fill=1.0,
                                       base=0, pattern=[[-1, P]], channel_multiplier=1))


STAGES = [
    (gla_stage, ["gla_wq", "gla_wk", "gla_wv", "gla_wo", "gla_nw"]),
    (cross_stage, ["ctxT", "mask", "x_wq", "x_bq", "x_wk", "x_bk", "x_wv", "x_bv", "x_wo", "x_qn", "x_kn"]),
    (experts_stage, ["e_gate", "e_gu", "e_dn", "e_merge", "e_dom"]),
    (rotary_stage, ["r_wq", "r_bq", "r_wk", "r_bk", "r_wv", "r_bv", "r_wo", "r_bo", "r_kw", "r_cos", "r_sin"]),
    (memory_stage, ["ctxT", "ctx", "kept"]),
    (routed_stage, ["m_router", "m_w1", "m_b1", "m_w2", "m_b2"]),
]


def layout(**a):
    c = np.ascontiguousarray
    T = lambda w: c(np.asarray(w).T)

    inv = (1.0 / np.power(np.float32(10000.0), np.arange(0, 64, 2, dtype=np.float32) / np.float32(64))).astype(np.float32)
    angle = (np.arange(S, dtype=np.float32)[:, None] * inv[None, :]).astype(np.float32)
    return {
        "x": c(a["x"]).reshape(B * S, D),
        "gla_wq": T(a["L0_attn_Wq"]), "gla_wk": T(a["L0_attn_Wk"]), "gla_wv": T(a["L0_attn_Wv"]),
        "gla_wo": T(a["L0_attn_Wo"]), "gla_nw": c(np.asarray(a["L0_attn_norm_w"]).reshape(2, P).T),
        "ctx": c(a["ctx_2048"]), "ctxT": c(np.asarray(a["ctx_2048"]).transpose(0, 2, 1)),
        "mask": c(a["mask_1xSxS2_ff0"])[0],
        "x_wq": c(a["L0_xattn_Wq"]), "x_bq": c(a["L0_xattn_bq"]), "x_wk": c(a["L0_xattn_Wk"]),
        "x_bk": c(a["L0_xattn_bk"]), "x_wv": c(a["L0_xattn_Wv"]), "x_bv": c(np.asarray(a["L0_xattn_bv"]).reshape(-1, P).T),
        "x_wo": c(a["L0_xattn_Wo"]), "x_qn": c(a["L0_xattn_qn_w"]).reshape(P, 1),
        "x_kn": c(a["L0_xattn_kn_w"]).reshape(P, 1),
        "e_gate": T(a["L0_ffn_gate_weight"]), "e_gu": c(np.asarray(a["L0_ffn_gate_up_proj"]).transpose(0, 2, 1)),
        "e_dn": c(np.asarray(a["L0_ffn_down_proj"]).transpose(0, 2, 1)),
        "e_merge": c(a["L0_ffn_merge_groups"]).reshape(-1, 1), "e_dom": c(a["L0_ffn_dominant_experts"]).reshape(1, -1),
        "r_wq": T(a["L1_attn_Wq"]), "r_bq": c(a["L1_attn_bq"]), "r_wk": T(a["L1_attn_Wk"]),
        "r_bk": c(a["L1_attn_bk"]), "r_wv": T(a["L1_attn_Wv"]), "r_bv": c(a["L1_attn_bv"]),
        "r_wo": T(a["L1_attn_Wo"]), "r_bo": c(a["L1_attn_bo"]), "r_kw": c(a["L1_attn_key_weights"]),
        "r_cos": np.cos(angle), "r_sin": np.sin(angle),
        "m_router": T(a["L1_ffn_router_w"]), "m_w1": T(a["L1_ffn_w1"]),
        "m_b1": c(np.asarray(a["L1_ffn_b1"]).reshape(-1, P).T), "m_w2": T(a["L1_ffn_w2"]), "m_b2": c(a["L1_ffn_b2"]),
        "kept": c(a["mask_BxS2_bk0"]),
    }


_OUT = "out"


def build(nc, ap):
    with ExitStack() as ctx:
        k = Kernel(nc, ctx)
        rows = ap["x"]
        for n, (stage, names) in enumerate(STAGES):
            after = ap[_OUT] if n == len(STAGES) - 1 else \
                nc.dram_tensor(f"rows_{n + 1}", [B * S, D], F32, kind="Internal").ap()
            stage(k, rows, after, *[ap[name] for name in names])
            rows = after


def kernel(**inputs):
    import concourse.bacc as bacc
    from concourse.bass_utils import run_bass_kernel_spmd

    nc = bacc.Bacc("TRN2", target_bir_lowering=False, num_devices=1)
    arrays = layout(**inputs)
    ap = {name: nc.dram_tensor(name, a.shape, mybir.dt.from_np(a.dtype), kind="ExternalInput").ap()
          for name, a in arrays.items()}
    ap[_OUT] = nc.dram_tensor(_OUT, [B * S, D], F32, kind="ExternalOutput").ap()
    build(nc, ap)
    result = run_bass_kernel_spmd(nc, [arrays], core_ids=[0])
    return result.results[0][_OUT].reshape(B, S, D)
```

```python
from contextlib import ExitStack

import numpy as np

import concourse.bass as bass
from concourse import mybir

F32 = mybir.dt.float32
F16 = mybir.dt.float16
I32 = mybir.dt.int32
U8 = mybir.dt.uint8
ALU = mybir.AluOpType
ACT = mybir.ActivationFunctionType
AX_X = mybir.AxisListType.X

P = 128
B = 8
S = 256
D = 256
ST = S // P
DC = D // P
BANK = 512
LN_EPS = 1e-5
RMS_EPS = 1e-6


def at(i, per_iteration, k):
    return i * per_iteration + k


def one(ap, i):
    return ap[bass.ds(i, 1)].squeeze(0)


class Chain:

    def __init__(self, eng, sem, per=0, i=None):
        self.eng, self.sem, self.per, self.i, self.k = eng, sem, per, i, 0

    def __call__(self, ins):
        self.k += 1
        ins.then_inc(self.sem, 1)
        self.eng.wait_ge(self.sem, self.k if self.i is None else at(self.i, self.per, self.k))

    def end(self):
        assert self.i is None or self.k == self.per, self.k


class Stage:

    def __init__(self, k, name, x_in, x_out):
        self.k, self.nc, self.name = k, k.nc, name
        self.ctx, self.sems = ExitStack(), []
        self.x_in = x_in.rearrange("(b s p) d -> b p s d", s=ST, p=P)
        self.x_out = x_out.rearrange("(b s p) d -> b p s d", s=ST, p=P)
        self.xb = self.sb("xb", [P, ST, D])
        self.xr = self.sb("xr", [P, ST, D])
        self.xT = self.sb("xT", [P, DC, S])
        self.z = self.sb("z", [P, ST, D])
        self.xo = self.sb("xo", [P, ST, D])
        self.bn = self.sb("bn", [P, ST, 6])
        self.mv = self.sb("mv", [P, ST, 2])
        self.ve = self.sb("ve", [P, ST])
        self.rstd = self.sb("rstd", [P, ST])
        self.x_loaded = self.sem("x_loaded")
        self.x_kept = self.sem("x_kept")
        self.z_made = self.sem("z_made")
        self.xT_ps = self.sem("xT_ps")
        self.xT_ready = self.sem("xT_ready")
        self.var_ready = self.sem("var_ready")
        self.rstd_ready = self.sem("rstd_ready")
        self.xo_ready = self.sem("xo_ready")
        self.xo_stored = self.sem("xo_stored")
        self.pool_own = self.sem("pool_own")
        self.ln_own = self.sem("ln_own")
        self.fence = self.sem("fence")
        self.own2 = self.sem("own2")

    def sb(self, name, shape, dt=F32):
        return self.ctx.enter_context(self.nc.sbuf_tensor(f"{self.name}_{name}_sb", shape, dt))

    def sem(self, name):
        self.sems.append(self.nc.alloc_semaphore(name=f"{self.name}_{name}"))
        return self.sems[-1]

    def close(self):
        self.nc.clear_and_free_semaphores(self.sems)
        self.nc.all_engine_barrier()
        self.ctx.close()

    def carry(self, dve):
        dve.sem_inc(self.fence, 1)

    def load_x(self, sp, i, keeps=True):
        if not isinstance(i, int):
            sp.wait_ge(self.xT_ps, at(i, 1, 0))
            if keeps:
                sp.wait_ge(self.x_kept, at(i, 1, 0))
        sp.dma_start(self.xb[:], one(self.x_in, i)).then_inc(self.x_loaded, 16)

    def store_x(self, sp, i):
        sp.wait_ge(self.xo_ready, at(i, 1, 1))
        sp.dma_start(one(self.x_out, i), self.xo[:]).then_inc(self.xo_stored, 16)

    def rows_dma(self, sp, more=None):
        if more:
            more(0)
        self.load_x(sp, 0)
        with sp.Fori(0, B - 1) as i:
            self.load_x(sp, i + 1)
            if more:
                more(i + 1)
            self.store_x(sp, i)
        self.store_x(sp, B - 1)
        sp.wait_ge(self.xo_stored, 16 * (B + 1))

    def keep_x(self, pool, i, bias=None):
        pool.wait_ge(self.x_loaded, at(i, 16, 16))
        pool.wait_ge(self.z_made, at(i, 1, 1))
        if bias is None:
            self.carry(pool)
            pool.tensor_copy(self.xr[:], self.xb[:]).then_inc(self.x_kept, 1)
        else:
            pool.tensor_tensor(self.xr[:], self.xb[:], bias.unsqueeze(1).to_broadcast([P, ST, D]), ALU.add)\
                .then_inc(self.x_kept, 1)

    def transpose_x(self, pe, i, ps):
        pe.wait_ge(self.x_loaded, at(i, 16, 16))
        for dc in range(DC):
            for st in range(ST):
                last = pe.transpose(ps[:, dc * S + st * P:dc * S + (st + 1) * P],
                                    self.xb[:, st, dc * P:(dc + 1) * P], self.k.ident[:])
        last.then_inc(self.xT_ps, 1)

    def copy_xT(self, act, i, ps):
        act.wait_ge(self.xT_ps, at(i, 1, 1))
        act.copy(self.xT[:].rearrange("p c s -> p (c s)"), ps).then_inc(self.xT_ready, 1)

    def credits(self, dve):
        dve.sem_inc(self.z_made, 1)
        dve.sem_inc(self.xo_stored, 16)

    def each_sequence(self, dve, sequence):
        sequence(0, None)
        with dve.Fori(0, B - 1) as i:
            sequence(i + 1, i)
        self.norm_dve(dve, B - 1)

    def norm_before(self, dve, before):
        if before is not None:
            self.norm_dve(dve, before)

    def norm_dve(self, dve, i, wait=True):
        if wait:
            dve.wait_ge(self.z_made, at(i, 1, 2))
        own = Chain(dve, self.ln_own, 3, i)
        for st in range(ST - 1):
            dve.bn_stats(self.bn[:, st, :], self.z[:, st, :])
        own(dve.bn_stats(self.bn[:, ST - 1, :], self.z[:, ST - 1, :]))
        self.carry(dve)
        for st in range(ST - 1):
            dve.bn_aggr(self.mv[:, st, :], self.bn[:, st, :])
        own(dve.bn_aggr(self.mv[:, ST - 1, :], self.bn[:, ST - 1, :]))
        dve.tensor_scalar(self.ve[:], self.mv[:, :, 1], LN_EPS, None, ALU.add).then_inc(self.var_ready, 1)
        dve.wait_ge(self.rstd_ready, at(i, 1, 1))
        dve.wait_ge(self.xo_stored, at(i, 16, 16))
        for st in range(ST):
            last = dve.tensor_scalar(self.xo[:, st, :], self.z[:, st, :], self.mv[:, st, 0:1],
                                     self.rstd[:, st:st + 1], ALU.subtract, ALU.mult)
        own(last)
        own.end()
        dve.nop().then_inc(self.xo_ready, 1)

    def norm_pool(self, pool, i):
        pool.wait_ge(self.var_ready, at(i, 1, 1))
        pool.tensor_tensor(self.rstd[:], self.ve[:], self.k.neg_half[:, 0:ST], ALU.pow).then_inc(self.rstd_ready, 1)


def gla_stage(k, x_in, x_out, wq, wk, wv, wo, norm_w):
    nc, ps, ident = k.nc, k.ps, k.ident
    H, CH = 2, 64
    NCH = S // CH
    s = Stage(k, "gla", x_in, x_out)
    W = {n: s.sb(n, [P, DC, D]) for n in ("wq", "wk", "wv", "wo")}
    nw = s.sb("nw", [P, H])
    keep = s.sb("keep", [P, P])
    reset = s.sb("reset", [P, H * S])
    ones = s.sb("ones", [P, 1])
    t = {n: s.sb(n, [P, H * S]) for n in ("qs", "f", "g", "lf", "c", "kk", "dec", "grow", "qd", "kd",
                                          "kr", "ow", "sq")}
    v = s.sb("v", [P, ST, D])
    krn = s.sb("krn", [P, H * ST, P])
    scm = s.sb("scm", [P, H * ST, P])
    state = s.sb("state", [P, H, NCH - 1, P])
    ss = s.sb("ss", [P, ST])
    r = s.sb("r", [P, ST])
    w_loaded, const_ready = s.sem("w_loaded"), s.sem("const_ready")
    proj_ps, exps, cums, decays, decayed = (s.sem(n) for n in (
        "proj_ps", "exps", "cums", "decays", "decayed"))
    v_ready, sc_ps, sc_ready, kr_ps, kr_ready, st_ps, st_ready = (s.sem(n) for n in (
        "v_ready", "sc_ps", "sc_ready", "kr_ps", "kr_ready", "st_ps", "st_ready"))
    o_ps, o_ready, sq_ready, ss_ps, ss_ready, r_ready, y_ps, dve_own, act_own = (s.sem(n) for n in (
        "o_ps", "o_ready", "sq_ready", "ss_ps", "ss_ready", "r_ready", "y_ps", "dve_own", "act_own"))
    qps, fps, vps, scps, krps, ops, stps0, stps1 = (ps[:, n, :] for n in range(8))
    update = lambda h, c: (stps0, stps1)[c % 2][:, (c // 2 * H + h) * P:(c // 2 * H + h + 1) * P]
    xps, yps, ssps = vps, qps, fps

    with nc.Block() as block:
        @block.sync
        def _(sp):
            for n, w in (("wq", wq), ("wk", wk), ("wv", wv), ("wo", wo)):
                sp.dma_start(W[n][:], w.rearrange("(c p) n -> p c n", p=P)).then_inc(w_loaded, 16)
            sp.dma_start(nw[:], norm_w).then_inc(w_loaded, 16)
            s.rows_dma(sp)

        @block.gpsimd
        def _(pool):
            own = Chain(pool, s.pool_own)
            own(pool.memset(keep[:], 1.0))
            own(pool.affine_select(out=keep[:], in_=keep[:], compare_op=ALU.is_ge, fill=0.0, base=0,
                                   pattern=[[1, P]], channel_multiplier=-1))
            own(pool.memset(keep[0:CH, CH:P], 0.0))
            pool.memset(ones[:], 1.0)
            own(pool.memset(reset[:], 1.0))
            pool.memset(reset[:].rearrange("p (c n) -> p c n", n=CH)[:, :, 0:1], 0.0).then_inc(const_ready, 1)
            with pool.Fori(0, B) as i:
                s.keep_x(pool, i)
                pool.wait_ge(ss_ready, at(i, 1, 1))
                pool.tensor_tensor(r[:], ss[:], k.neg_half[:, 0:ST], ALU.pow).then_inc(r_ready, 1)
                s.norm_pool(pool, i)

        @block.tensor
        def _(pe):
            pe.wait_ge(w_loaded, 16 * 5)
            pe.wait_ge(const_ready, 1)
            with pe.Fori(0, B) as i:
                s.transpose_x(pe, i, xps)
                pe.wait_ge(s.z_made, at(i, 1, 1))
                pe.wait_ge(s.xT_ready, at(i, 1, 1))
                for out, w in ((qps, "wq"), (fps, "wk")):
                    for h in range(H):
                        for dc in range(DC):
                            last = pe.matmul(out[:, h * S:(h + 1) * S], W[w][:, dc, h * P:(h + 1) * P],
                                             s.xT[:, dc, :], start=dc == 0, stop=dc == DC - 1)
                    last.then_inc(proj_ps, 1)
                for st in range(ST):
                    for dc in range(DC):
                        last = pe.matmul(vps[:, st * D:(st + 1) * D], s.xT[:, dc, st * P:(st + 1) * P],
                                         W["wv"][:, dc, :], start=dc == 0, stop=dc == DC - 1)
                last.then_inc(proj_ps, 1)
                pe.wait_ge(decayed, at(i, 2, 1))
                for h in range(H):
                    for st in range(ST):
                        a = h * S + st * P
                        last = pe.matmul(scps[:, (h * ST + st) * P:(h * ST + st + 1) * P], t["kd"][:, a:a + P],
                                         t["qd"][:, a:a + P], start=True, stop=True)
                last.then_inc(sc_ps, 1)
                pe.wait_ge(decayed, at(i, 2, 2))
                for n in range(H * ST):
                    last = pe.transpose(krps[:, n * P:(n + 1) * P], t["kr"][:, n * P:(n + 1) * P], ident[:])
                last.then_inc(kr_ps, 1)
                pe.wait_ge(kr_ready, at(i, 1, 1))
                pe.wait_ge(v_ready, at(i, 1, 1))
                for c in range(NCH - 1):
                    for h in range(H):
                        a = (c % 2) * CH
                        last = pe.matmul(update(h, c), krn[a:a + CH, h * ST + c // 2, :],
                                         v[a:a + CH, c // 2, h * P:(h + 1) * P], start=True, stop=True)
                last.then_inc(st_ps, 1)
                pe.wait_ge(sc_ready, at(i, 1, 1))
                for h in range(H):
                    for st in range(ST):
                        n = h * ST + st
                        pe.matmul(ops[:, n * P:(n + 1) * P], v[:, st, h * P:(h + 1) * P], scm[:, n, :],
                                  start=n == 0, stop=False, skip_group_check=True)
                for c in range(1, NCH):
                    pe.wait_ge(st_ready, at(i, NCH - 1, c))
                    for h in range(H):
                        a = h * S + c * CH
                        last = pe.matmul(ops[:, a:a + CH], state[:, h, c - 1, :], t["qd"][:, a:a + CH],
                                         start=False, stop=True, skip_group_check=True)
                last.then_inc(o_ps, 1)
                pe.wait_ge(sq_ready, at(i, 1, 1))
                for st in range(ST):
                    for h in range(H):
                        last = pe.matmul(ssps[:, st:st + 1], t["sq"][:, h * S + st * P:h * S + (st + 1) * P],
                                         ones[:], start=h == 0, stop=h == H - 1)
                last.then_inc(ss_ps, 1)
                pe.wait_ge(o_ready, at(i, 1, 1))
                for st in range(ST):
                    for h in range(H):
                        last = pe.matmul(yps[:, st * D:(st + 1) * D], t["ow"][:, h * S + st * P:h * S + (st + 1) * P],
                                         W["wo"][:, h, :], start=h == 0, stop=h == H - 1)
                last.then_inc(y_ps, 1)

        @block.scalar
        def _(act):
            with act.Fori(0, B) as i:
                own = Chain(act, act_own, 3, i)
                s.copy_xT(act, i, xps)
                act.wait_ge(proj_ps, at(i, 3, 1))
                act.activation(t["qs"][:], qps, ACT.Sigmoid).then_inc(exps, 1)
                act.wait_ge(proj_ps, at(i, 3, 2))
                own(act.activation(t["f"][:], fps, ACT.Sigmoid))
                own(act.activation(t["g"][:], t["f"][:], ACT.Sigmoid))
                act.activation(t["kk"][:], t["f"][:], ACT.Sigmoid, scale=-1.0).then_inc(exps, 1)
                act.activation(t["lf"][:], t["g"][:], ACT.Ln).then_inc(exps, 1)
                act.wait_ge(proj_ps, at(i, 3, 3))
                act.copy(v[:].rearrange("p s d -> p (s d)"), vps).then_inc(v_ready, 1)
                act.wait_ge(cums, at(i, 1, 1))
                act.activation(t["dec"][:], t["c"][:], ACT.Exp).then_inc(decays, 1)
                act.activation(t["grow"][:], t["c"][:], ACT.Exp, scale=-1.0).then_inc(decays, 1)
                act.wait_ge(kr_ps, at(i, 1, 1))
                act.copy(krn[:].rearrange("p n q -> p (n q)"), krps).then_inc(kr_ready, 1)
                act.wait_ge(o_ps, at(i, 1, 1))
                own(act.activation(t["sq"][:], ops, ACT.Square))
                act.nop().then_inc(sq_ready, 1)
                own.end()

        @block.vector
        def _(dve):
            s.credits(dve)
            dve.wait_ge(w_loaded, 16 * 5)
            dve.wait_ge(const_ready, 1)

            def sequence(i, before):
                own = Chain(dve, dve_own, 4, i)
                dve.wait_ge(exps, at(i, 3, 1))
                own(dve.tensor_tensor(t["qs"][:], qps, t["qs"][:], ALU.mult))
                s.norm_before(dve, before)
                dve.wait_ge(exps, at(i, 3, 3))
                dve.tensor_tensor_scan(t["c"][:], reset[:], t["lf"][:], 0.0, ALU.mult, ALU.add).then_inc(cums, 1)
                dve.wait_ge(decays, at(i, 2, 1))
                dve.tensor_tensor(t["qd"][:], t["qs"][:], t["dec"][:], ALU.mult)
                dve.wait_ge(decays, at(i, 2, 2))
                own(dve.tensor_tensor(t["kd"][:], t["kk"][:], t["grow"][:], ALU.mult))
                dve.nop().then_inc(decayed, 1)
                to_end = t["dec"][:].rearrange("p (c n) -> p c n", n=CH)[:, :, CH - 1:CH]
                dve.tensor_tensor(t["kr"][:].rearrange("p (c n) -> p c n", n=CH),
                                  t["kd"][:].rearrange("p (c n) -> p c n", n=CH),
                                  to_end.to_broadcast([P, H * NCH, CH]), ALU.mult).then_inc(decayed, 1)
                dve.wait_ge(sc_ps, at(i, 1, 1))
                dve.tensor_tensor(scm[:], scps.rearrange("p (n q) -> p n q", q=P),
                                  keep[:].unsqueeze(1).to_broadcast([P, H * ST, P]), ALU.mult).then_inc(sc_ready, 1)
                dve.wait_ge(st_ps, at(i, 1, 1))
                for c in range(NCH - 1):
                    for h in range(H):
                        new, u = state[:, h, c, :], update(h, c)
                        e = h * S + (c + 1) * CH - 1
                        if c == 0:
                            last = dve.tensor_copy(new, u)
                        else:
                            last = dve.scalar_tensor_tensor(new, state[:, h, c - 1, :], t["dec"][:, e:e + 1], u,
                                                            ALU.mult, ALU.add)
                    last.then_inc(st_ready, 1)
                    dve.wait_ge(st_ready, at(i, NCH - 1, c + 1))
                dve.wait_ge(sq_ready, at(i, 1, 1))
                for h in range(H):
                    last = dve.tensor_scalar(t["ow"][:, h * S:(h + 1) * S], ops[:, h * S:(h + 1) * S],
                                             nw[:, h:h + 1], None, ALU.mult)
                own(last)
                dve.nop().then_inc(o_ready, 1)
                dve.wait_ge(ss_ps, at(i, 1, 1))
                dve.tensor_scalar(ss[:], ssps[:, 0:ST], 1.0 / D, RMS_EPS, ALU.mult, ALU.add).then_inc(ss_ready, 1)
                dve.wait_ge(y_ps, at(i, 1, 1))
                dve.wait_ge(r_ready, at(i, 1, 1))
                dve.wait_ge(s.x_kept, at(i, 1, 1))
                for st in range(ST):
                    last = dve.scalar_tensor_tensor(s.z[:, st, :], yps[:, st * D:(st + 1) * D], r[:, st:st + 1],
                                                    s.xr[:, st, :], ALU.mult, ALU.add)
                own(last)
                own.end()
                dve.nop().then_inc(s.z_made, 1)

            s.each_sequence(dve, sequence)
    s.close()


def cross_stage(k, x_in, x_out, ctxT_in, mask_in, wq, bq, wk, bk, wv, bv, wo, qn, kn):
    nc, ps, ident = k.nc, k.ps, k.ident
    NH, NKV, HD = 16, 4, 128
    G = NH // NKV
    E = ctxT_in.shape[2]
    ET = (E + P - 1) // P
    rows = [min(P, E - e * P) for e in range(ET)]
    chunks = [(c, min(BANK, E - c)) for c in range(0, E, BANK)]
    NC = len(chunks)
    UNITS = ST * NKV
    HEADS = UNITS * G
    NORMED = ET + UNITS
    LAG = 3
    XJ = ET - 4
    s = Stage(k, "cross", x_in, x_out)
    wq_p, wk_p, wv_p = ([s.sb(f"{name}_{part}", [P, DC, n], F16) for part in ("hi", "lo")]
                        for name, n in (("wq", NH * HD), ("wk", NKV * HD), ("wv", NKV * HD)))
    wo_p = [s.sb(f"wo_{part}", [P, NH, D], F16) for part in ("hi", "lo")]
    bq_s, bk_s, bv_c = s.sb("bq", [P, NH * HD]), s.sb("bk", [P, NKV * HD]), s.sb("bv", [P, NKV])
    vbias = s.sb("vbias", [P, D])
    nw = s.sb("nw", [P, 2])
    qk_w = s.sb("qk_w", [P, 1])
    mask = s.sb("mask", [P, ST, E])
    ctxT = s.sb("ctxT", [P, DC, E])
    kT_flat = [s.sb(f"kT_{part}", [P, NKV * E], F16) for part in ("hi", "lo")]
    kT = [t_[:].rearrange("p (g e) -> p g e", g=NKV) for t_ in kT_flat]
    v = [s.sb(f"v_{part}", [P, ET, NKV * HD], F16) for part in ("hi", "lo")]
    qT = [s.sb(f"qT_{part}", [P, UNITS, G * P], F16) for part in ("hi", "lo")]
    pT = [[s.sb(f"pT{n}_{part}", [P, ET, 2, P], F16) for part in ("hi", "lo")] for n in range(2)]
    sc = [s.sb(f"sc{n}", [P, E]) for n in range(3)]
    raw = [s.sb(f"raw{n}", [P, NKV * HD]) for n in range(3)]
    nrm, sq = [sc[2][:, 0:512], sc[2][:, 512:1024]], sc[2][:, 1024:1536]
    ctx_p = [t_[:].rearrange("p e g s -> p (e g s)")[:, 0:DC * E].rearrange("p (c e) -> p c e", c=DC)
             for t_ in pT[0]]
    xT_p = [s.xT[:].rearrange("p c s -> p (c s)").bitcast(F16)[:, n * DC * S:(n + 1) * DC * S]
            .rearrange("p (c s) -> p c s", c=DC) for n in range(2)]
    as_f32 = lambda t_: t_[:].rearrange("p g e -> p (g e)").bitcast(F32)
    w_in = [(wk_p, slice(0, DC), 0, wk, sc[0][:, 0:DC * NKV * HD]), (wv_p, slice(0, DC), 0, wv, sc[1][:, 0:DC * NKV * HD])] + \
           [(wq_p, slice(dc, dc + 1), dc, wq, as_f32(v[dc])[:, 0:NH * HD]) for dc in range(DC)]
    wo_in = [kT_flat[x][:, 0:NH * D].bitcast(F32) for x in range(2)]
    w_in += [(wo_p, slice(NH // 2 * x, NH // 2 * (x + 1)), x, wo, wo_in[x]) for x in range(2)]
    bv_b = raw[0][:].rearrange("p (g s) -> p g s", g=NKV)
    msq, rr = s.sb("msq", [P, 2, NKV]), s.sb("rr", [P, 3, NKV])
    mx, nmx, sums, rsum = s.sb("mx", [P, 3, NC]), s.sb("nmx", [P, 3]), s.sb("sums", [P, HEADS, 2]), s.sb("rsum", [P, 2])
    parts16 = lambda t_, n: [t_[:, n + x:n + x + P].bitcast(F16) for x in (0, P)]
    diag, diag_p = raw[0][:, 0:2 * P], parts16(raw[0], 2 * P)
    rbc = [raw[1][:, 2 * P * n:2 * P * (n + 1)] for n in range(2)]
    oT_p = [parts16(raw[2], 2 * P * n) for n in range(2)]
    oT = s.sb("oT", [P, 2 * P])
    ident_r, ones16 = s.sb("ident_r", [P, P]), s.sb("ones16", [P, P], F16)
    (w_loaded, const_ready, ctx_loaded, kq_ps, v_ps, raw_ready, sq_ready, v_ready, ms_ready, rr_ready,
     nrm_ready, turn_ps, turned, turned_hi, v_hi) = (s.sem(n) for n in (
        "w_loaded", "const_ready", "ctx_loaded", "kq_ps", "v_ps", "raw_ready", "sq_ready", "v_ready",
        "ms_ready", "rr_ready", "nrm_ready", "turn_ps", "turned", "turned_hi", "v_hi"))
    (diag_made, diag_hi, of_ready, oT_hi) = (s.sem(n) for n in ("diag_made", "diag_hi", "of_ready", "oT_hi"))
    (w_hi, w_ready, bias_ps, ctx_hi, ctx_ready, xT_hi, mixed, mask_loaded) = (s.sem(n) for n in (
        "w_hi", "w_ready", "bias_ps", "ctx_hi", "ctx_ready", "xT_hi", "mixed", "mask_loaded"))
    (sc_ps, sc_read, nmx_ready, exp_done, t_ps, t_act, t_dve, pv_ps, diag_ready, oT_ready, y_ps, dve_own) = (
        s.sem(n) for n in ("sc_ps", "sc_read", "nmx_ready", "exp_done", "t_ps", "t_act", "t_dve", "pv_ps",
                           "diag_ready", "oT_ready", "y_ps", "dve_own"))
    bank = lambda n: ps[:, n, :]
    KQ, VB, SB, TB, OB, YB = (0, 1), (2, 5), (0, 1, 2), (3, 4), (5, 6), 7
    SLOTS = (ET + G - 1) // G
    PAIRS = HEADS // 2
    slot_tiles = lambda j: min(G, ET - G * j)
    slot_rows = lambda j: P if slot_tiles(j) == G else rows[-1]
    order = []
    for n in range(HEADS):
        for j in range(SLOTS):
            order.append((n, j))
            if n % 2 == 1 and n > 1 and j == 0:
                order.append(("r", n // 2 - 1))
    order.append(("r", PAIRS - 1))
    T_PS = len(order)
    t_index = {what: x for x, what in enumerate(order)}
    t_count = lambda n, j: t_index[n, j] + 1
    r_count = lambda m: t_index["r", m] + 1
    d_count = lambda n, j: SLOTS * n + j + 1
    t_bank = lambda x: ps[:, TB[x % 2], :]
    PSCALE, RSCALE = 2.0 ** 15, 2.0 ** 9
    WSCALE = 64.0
    PASSES = ((0, 0), (0, 1), (1, 0))
    CUT = 768
    early = [(n, c) for n in range(2) for c in range(NC)]
    parts = [range(ET * x // (2 * SLOTS), ET * (x + 1) // (2 * SLOTS)) for x in range(2 * SLOTS)]

    W_ALL = 16 * (len(w_in) + 2 + 1 + 2)

    with nc.Block() as block:
        @block.sync
        def _(sp):
            for _, cs, dc, a, t_ in w_in:
                sp.dma_start(t_.rearrange("p (c n) -> p c n", c=cs.stop - cs.start),
                             a.rearrange("(c p) n -> p c n", p=P)[:, cs, :]).then_inc(w_loaded, 16)
            for t_, a in ((bk_s, bk), (bq_s, bq)):
                sp.dma_start(t_[:], a.partition_broadcast(P)).then_inc(w_loaded, 16)
            sp.dma_start(bv_c[:], bv).then_inc(w_loaded, 16)
            sp.dma_start(nw[:, 0:1], qn).then_inc(w_loaded, 16)
            sp.dma_start(nw[:, 1:2], kn).then_inc(w_loaded, 16)
            def context(i):
                if not isinstance(i, int):
                    sp.wait_ge(ctx_ready, at(i, NC, 0))
                sp.dma_start(ctxT[:], one(ctxT_in, i).rearrange("(c p) e -> p c e", p=P)).then_inc(ctx_loaded, 16)
                if isinstance(i, int):
                    sp.dma_start(mask[:], mask_in.rearrange("(s p) e -> p s e", p=P)).then_inc(mask_loaded, 16)

            s.rows_dma(sp, context)

        @block.gpsimd
        def _(pool):
            pool.memset(ones16[:], 1.0).then_inc(const_ready, 1)
            pool.wait_ge(w_ready, len(w_in) + 1)
            with pool.Fori(0, B) as i:
                s.keep_x(pool, i, vbias[:])
                for j in range(NORMED):
                    m = rows[j] if j < ET else P
                    pool.wait_ge(ms_ready, at(i, NORMED, j + 1))
                    pool.tensor_tensor(rr[:, j % 3, :], msq[:, j % 2, :], k.neg_half[:, 0:NKV], ALU.pow)\
                        .then_inc(rr_ready, 1)
                    pool.wait_ge(rr_ready, at(i, NORMED, j + 1))
                    if j >= 2:
                        pool.wait_ge(turn_ps, at(i, NORMED, j - 1))
                    pool.tensor_tensor(nrm[j % 2][0:m, :].rearrange("p (g d) -> p g d", g=NKV),
                                       raw[j % 3][0:m, :].rearrange("p (g d) -> p g d", g=NKV),
                                       rr[0:m, j % 3, :].unsqueeze(2).to_broadcast([m, NKV, HD]), ALU.mult)\
                        .then_inc(nrm_ready, 1)
                s.norm_pool(pool, i)

        @block.tensor
        def _(pe):
            pe.wait_ge(w_loaded, W_ALL)
            pe.wait_ge(const_ready, 3)
            for h in range(NH):
                last = pe.matmul(bank(YB)[:, 0:D], bv_b[:, h // G, :],
                                 wo_in[h * 2 // NH][:, h % (NH // 2) * D:(h % (NH // 2) + 1) * D], start=h == 0, stop=h == NH - 1)
            last.then_inc(bias_ps, 1)
            pe.wait_ge(w_ready, len(w_in) + 1)
            with pe.Fori(0, B) as i:
                def project(j):
                    key = j < ET
                    m = rows[j] if key else P
                    if j >= 2:
                        pe.wait_ge(raw_ready, at(i, NORMED, j - 1))
                    def product(out, left, right, n0, n1, e0):
                        for dc in range(DC):
                            for lp, rp in PASSES:
                                last = pe.matmul(out[0:m, :], left[lp][:, dc, e0:e0 + m], right[rp][:, dc, n0:n1],
                                                 start=dc + lp + rp == 0, stop=dc == DC - 1 and lp == 1)
                        return last

                    if key:
                        last = product(bank(KQ[j % 2]), ctx_p, wk_p, 0, NKV * HD, j * P)
                    else:
                        st, g = divmod(j - ET, NKV)
                        last = product(bank(KQ[j % 2]), xT_p, wq_p, g * G * HD, (g + 1) * G * HD, st * P)
                    last.then_inc(kq_ps, 1)
                    if key:
                        if j >= 2:
                            pe.wait_ge(v_ready, at(i, ET, j - 1))
                        product(bank(VB[j % 2]), ctx_p, wv_p, 0, NKV * HD, j * P).then_inc(v_ps, 1)

                def turn(j):
                    m = rows[j] if j < ET else P
                    pe.wait_ge(nrm_ready, at(i, NORMED, j + 1))
                    if j >= 2:
                        pe.wait_ge(turned, at(i, NORMED, j - 1))
                    for g in range(NKV):
                        last = pe.transpose(bank(TB[j % 2])[:, g * P:g * P + m], nrm[j % 2][0:m, g * P:(g + 1) * P],
                                            ident[0:m, 0:m])
                    last.then_inc(turn_ps, 1)

                def scores(n, c):
                    u = n // G
                    g = u % NKV
                    e0, w = chunks[c]
                    x = NC * n + c
                    if x >= 3:
                        pe.wait_ge(sc_read, at(i, NC * HEADS, x - 2))
                    for q, kk in ((0, 0), (0, 1), (1, 0)):
                        last = pe.matmul(bank(SB[x % 3])[:, 0:w], qT[q][:, u, (n % G) * P:(n % G + 1) * P],
                                         kT[kk][:, g, e0:e0 + w], start=q + kk == 0, stop=q == 1)
                    last.then_inc(sc_ps, 1)

                def bank_read(x):
                    if x >= 2:
                        n, j = order[x - 2]
                        if n == "r":
                            pe.wait_ge(t_act, at(i, T_PS, r_count(j)))
                        else:
                            pe.wait_ge(t_dve, at(i, SLOTS * HEADS, d_count(n, j)))

                def turn_probs(n, j):
                    if j == 0:
                        pe.wait_ge(exp_done, at(i, HEADS, n + 1))
                    x = t_index[n, j]
                    bank_read(x)
                    for e in range(G * j, min(G * j + G, ET)):
                        last = pe.transpose(t_bank(x)[0:rows[e], (e % G) * P:(e % G + 1) * P],
                                            sc[n % 3][:, e * P:e * P + rows[e]], ident[:])
                    last.then_inc(t_ps, 1)

                def spread(m):
                    pe.wait_ge(diag_ready, at(i, PAIRS, m + 1))
                    x = t_index["r", m]
                    bank_read(x)
                    for part in range(2):
                        last = pe.matmul(t_bank(x)[:, 0:2 * P], ones16[:], diag_p[part], start=part == 0, stop=part == 1)
                    last.then_inc(t_ps, 1)

                def mix(m, part):
                    if part == 0:
                        pe.wait_ge(t_dve, at(i, SLOTS * HEADS, d_count(2 * m + 1, SLOTS - 1)))
                        if m >= 2:
                            pe.wait_ge(of_ready, at(i, PAIRS, m - 1))
                    g = m // 2 % NKV
                    for e in parts[part]:
                        for vv, pp in ((0, 0), (0, 1), (1, 0)):
                            last = pe.matmul(bank(OB[m % 2])[:, 0:2 * P], v[vv][0:rows[e], e, g * HD:(g + 1) * HD],
                                             pT[m % 2][pp][0:rows[e], e, :, :].rearrange("p g s -> p (g s)"),
                                             start=e == 0 and vv + pp == 0, stop=e == ET - 1 and vv == 1)
                    if part == 2 * SLOTS - 1:
                        last.then_inc(pv_ps, 1)

                def output(m):
                    st, g = divmod(m // 2, NKV)
                    pe.wait_ge(oT_ready, at(i, PAIRS, m + 1))
                    for h in range(2):
                        for lp, rp in PASSES:
                            last = pe.matmul(bank(YB)[:, st * D:(st + 1) * D], oT_p[m % 2][lp][:, h * P:(h + 1) * P],
                                             wo_p[rp][:, g * G + m % 2 * 2 + h, :],
                                             start=g == 0 and m % 2 + h + lp + rp == 0,
                                             stop=g == NKV - 1 and m % 2 == 1 and h == 1 and lp == 1)
                    last.then_inc(y_ps, 1)

                for j in range(NORMED + LAG):
                    if j == XJ:
                        pe.wait_ge(s.z_made, at(i, 1, 1))
                        s.transpose_x(pe, i, bank(YB))
                    if j < ET and (j * P) % BANK == 0:
                        pe.wait_ge(ctx_ready, at(i, NC, j * P // BANK + 1))
                    if j == ET:
                        pe.wait_ge(s.xT_ready, at(i, 1, 1))
                    if j < NORMED:
                        project(j)
                    if j >= LAG:
                        turn(j - LAG)
                    if j == NORMED + 1:
                        pe.wait_ge(turned, at(i, NORMED, ET + 1))
                        pe.wait_ge(raw_ready, at(i, NORMED, NORMED))
                        pe.wait_ge(v_ready, at(i, ET, ET))
                    if j > NORMED:
                        scores(*early[j - NORMED - 1])
                for n, c in early[LAG - 1:]:
                    scores(n, c)
                pe.wait_ge(turned, at(i, NORMED, NORMED))
                for n in range(HEADS):
                    m, odd = divmod(n, 2)
                    for j in range(SLOTS):
                        turn_probs(n, j)
                        if m >= 1:
                            mix(m - 1, SLOTS * odd + j)
                            if n % 2 == 1 and j == 0:
                                spread(m - 1)
                        if n + 2 < HEADS:
                            scores(n + 2, j)
                        if m >= 3 and odd == 0 and j == 1:
                            output(m - 3)
                for part in range(2 * SLOTS):
                    mix(PAIRS - 1, part)
                spread(PAIRS - 1)
                output(PAIRS - 3)
                output(PAIRS - 2)
                output(PAIRS - 1)
                pe.wait_ge(pv_ps, at(i, PAIRS, PAIRS))
                pe.sem_inc(mixed, 1)

        @block.scalar
        def _(act):
            act.wait_ge(w_loaded, W_ALL)
            act.wait_ge(const_ready, 4)
            for n, (t_, cs, dc, a, w) in enumerate(w_in):
                act.activation(t_[0][:, cs, :], w.rearrange("p (c n) -> p c n", c=cs.stop - cs.start), ACT.Copy,
                               scale=WSCALE).then_inc(w_hi, 1)
            act.wait_ge(w_ready, len(w_in) + 1)
            with act.Fori(0, B) as i:
                def context_hi(c):
                    e0, w = chunks[c]
                    act.copy(ctx_p[0][:, :, e0:e0 + w], ctxT[:, :, e0:e0 + w]).then_inc(ctx_hi, 1)

                act.wait_ge(mixed, at(i, 1, 1))
                act.wait_ge(ctx_loaded, at(i, 16, 16))
                context_hi(0)
                for j in range(NORMED + LAG):
                    if j % G == 1 and j // G + 1 < NC:
                        context_hi(j // G + 1)
                    if j == XJ:
                        act.wait_ge(s.xT_ps, at(i, 1, 1))
                        act.copy(xT_p[0].rearrange("p c s -> p (c s)"), bank(YB)).then_inc(xT_hi, 1)
                    if j < NORMED:
                        m = rows[j] if j < ET else P
                        act.wait_ge(raw_ready, at(i, NORMED, j + 1))
                        if j >= 1:
                            act.wait_ge(sq_ready, at(i, NORMED, j))
                        if j >= 2:
                            act.wait_ge(rr_ready, at(i, NORMED, j - 1))
                        for g in range(NKV):
                            last = act.activation(sq[0:m, g * HD:(g + 1) * HD], raw[j % 3][0:m, g * HD:(g + 1) * HD],
                                                  ACT.Square, accum_out=msq[0:m, j % 2, g:g + 1])
                        last.then_inc(sq_ready, 1)
                        if j < ET:
                            act.wait_ge(v_ps, at(i, ET, j + 1))
                            act.activation(v[0][0:m, j, :], bank(VB[j % 2])[0:m, :], ACT.Copy, scale=1.0 / WSCALE)\
                               .then_inc(v_hi, 1)
                    if j >= LAG:
                        n = j - LAG
                        act.wait_ge(turn_ps, at(i, NORMED, n + 1))
                        src = bank(TB[n % 2])
                        if n < ET:
                            act.copy(kT[0][:, :, n * P:n * P + rows[n]],
                                     src.rearrange("p (g e) -> p g e", g=NKV)[:, :, 0:rows[n]]).then_inc(turned_hi, 1)
                        else:
                            act.activation(qT[0][:, n - ET, :], src, ACT.Copy, scale=qk_w[:]).then_inc(turned_hi, 1)

                def exp(n, part):
                    if part == 0:
                        act.wait_ge(nmx_ready, at(i, HEADS, n + 1))
                    piece = sc[n % 3][:, 0:CUT] if part == 0 else sc[n % 3][:, CUT:E]
                    ins = act.activation(piece, piece, ACT.Exp, bias=nmx[:, n % 3:n % 3 + 1],
                                         accum_out=sums[:, n, part:part + 1])
                    if part == 1:
                        ins.then_inc(exp_done, 1)

                def spread_copy(m):
                    if m >= 2:
                        act.wait_ge(of_ready, at(i, PAIRS, m - 1))
                    act.wait_ge(t_ps, at(i, T_PS, r_count(m)))
                    act.activation(rbc[m % 2], t_bank(t_index["r", m])[:, 0:2 * P], ACT.Copy,
                                   scale=1.0 / PSCALE / RSCALE).then_inc(t_act, 1)

                def spread_hi(m):
                    if m >= 1:
                        act.wait_ge(t_ps, at(i, T_PS, r_count(m - 1)))
                    act.wait_ge(diag_made, at(i, PAIRS, m + 1))
                    act.copy(diag_p[0], diag).then_inc(diag_hi, 1)

                def output_hi(m):
                    if m >= 2:
                        act.wait_ge(y_ps, at(i, PAIRS, m - 1))
                    act.wait_ge(of_ready, at(i, PAIRS, m + 1))
                    act.copy(oT_p[m % 2][0], oT[:]).then_inc(oT_hi, 1)

                exp(0, 0)
                exp(0, 1)
                for n in range(HEADS):
                    m = n // 2
                    if n % 2 == 0 and m >= 2:
                        act.wait_ge(pv_ps, at(i, PAIRS, m - 1))
                    for j in range(SLOTS):
                        r, ne = slot_rows(j), slot_tiles(j)
                        act.wait_ge(t_ps, at(i, T_PS, t_count(n, j)))
                        act.activation(pT[m % 2][0][0:r, G * j:G * j + ne, n % 2, :],
                                       t_bank(t_index[n, j])[0:r, 0:ne * P].rearrange("p (e s) -> p e s", e=ne),
                                       ACT.Copy, scale=PSCALE).then_inc(t_act, 1)
                        if n % 2 == 0 and m and j == 1:
                            spread_hi(m - 1)
                        if n % 2 == 1 and m and j == 0:
                            spread_copy(m - 1)
                        if n % 2 == 1 and m >= 2 and j == 2:
                            output_hi(m - 2)
                        if j in (0, 2) and n + 1 < HEADS:
                            exp(n + 1, j // 2)
                spread_hi(PAIRS - 1)
                output_hi(PAIRS - 2)
                spread_copy(PAIRS - 1)
                output_hi(PAIRS - 1)

        @block.vector
        def _(dve):
            s.credits(dve)
            dve.sem_inc(mixed, 1)
            dve.wait_ge(w_loaded, W_ALL)
            dve.wait_ge(const_ready, 1)
            dve.tensor_copy(bv_b, bv_c[:].unsqueeze(2).to_broadcast([P, NKV, P])).then_inc(const_ready, 1)
            dve.wait_ge(const_ready, 2)
            dve.nop().then_inc(const_ready, 1)
            dve.tensor_scalar(ident_r[:], ident[:], RSCALE, None, ALU.mult)
            dve.scalar_tensor_tensor(qk_w[:], nw[:, 0:1], float(HD) ** -0.5, nw[:, 1:2], ALU.mult, ALU.mult)\
               .then_inc(const_ready, 1)
            for n, (t_, cs, dc, a, w) in enumerate(w_in):
                dve.wait_ge(w_hi, n + 1)
                dve.scalar_tensor_tensor(t_[1][:, cs, :], w.rearrange("p (c n) -> p c n", c=cs.stop - cs.start), WSCALE,
                                         t_[0][:, cs, :], ALU.mult, ALU.subtract).then_inc(w_ready, 1)
            dve.wait_ge(bias_ps, 1)
            dve.tensor_copy(vbias[:], bank(YB)[:, 0:D]).then_inc(w_ready, 1)
            dve.wait_ge(w_ready, len(w_in) + 1)

            def sequence(i, before):
                own = Chain(dve, dve_own, 2 * PAIRS, i)

                def context_lo(c):
                    e0, w = chunks[c]
                    dve.wait_ge(ctx_hi, at(i, NC, c + 1))
                    dve.tensor_tensor(ctx_p[1][:, :, e0:e0 + w], ctxT[:, :, e0:e0 + w], ctx_p[0][:, :, e0:e0 + w],
                                      ALU.subtract).then_inc(ctx_ready, 1)

                def maxima(n, c):
                    st = n // G // NKV
                    e0, w = chunks[c]
                    x = NC * n + c
                    if n >= 3 and c == 0:
                        dve.wait_ge(t_ps, at(i, T_PS, t_count(n - 3, SLOTS - 1)))
                    dve.wait_ge(sc_ps, at(i, NC * HEADS, NC * n + c + 1))
                    s.carry(dve)
                    dve.tensor_tensor_reduce(sc[n % 3][:, e0:e0 + w], bank(SB[x % 3])[:, 0:w], mask[:, st, e0:e0 + w],
                                             1.0, -3.0e38, ALU.add, ALU.max, mx[:, n % 3, c:c + 1])\
                       .then_inc(sc_read, 1)
                    if c == NC - 1:
                        dve.wait_ge(sc_read, at(i, NC * HEADS, NC * n + NC))
                        dve.tensor_reduce(nmx[:, n % 3:n % 3 + 1], mx[:, n % 3, :], AX_X, ALU.max, negate=True)\
                           .then_inc(nmx_ready, 1)

                context_lo(0)
                for j in range(NORMED + LAG + 1):
                    if j < NORMED:
                        key = j < ET
                        m = rows[j] if key else P
                        bias = bk_s[:] if key else bq_s[:, (j - ET) % NKV * 512:((j - ET) % NKV + 1) * 512]
                        dve.wait_ge(kq_ps, at(i, NORMED, j + 1))
                        if j >= 3:
                            dve.wait_ge(sq_ready, at(i, NORMED, j - 2))
                            dve.wait_ge(nrm_ready, at(i, NORMED, j - 2))
                        dve.scalar_tensor_tensor(raw[j % 3][0:m, :], bank(KQ[j % 2])[0:m, :], 1.0 / WSCALE, bias[0:m, :],
                                                 ALU.mult, ALU.add).then_inc(raw_ready, 1)
                    if j == 1:
                        s.norm_before(dve, before)
                    if j % G == 1 and j // G + 1 < NC:
                        context_lo(j // G + 1)
                    if j == XJ:
                        dve.wait_ge(xT_hi, at(i, 1, 1))
                        dve.tensor_tensor(xT_p[1].rearrange("p c s -> p (c s)"), bank(YB),
                                          xT_p[0].rearrange("p c s -> p (c s)"), ALU.subtract)\
                           .then_inc(s.xT_ready, 1)
                    if j > LAG:
                        n = j - LAG - 1
                        dve.wait_ge(turned_hi, at(i, NORMED, n + 1))
                        src = bank(TB[n % 2])
                        if n < ET:
                            hi, lo = (t_[:, :, n * P:n * P + rows[n]] for t_ in kT)
                            dve.tensor_tensor(lo, src.rearrange("p (g e) -> p g e", g=NKV)[:, :, 0:rows[n]], hi,
                                              ALU.subtract).then_inc(turned, 1)
                        else:
                            dve.scalar_tensor_tensor(qT[1][:, n - ET, :], src, qk_w[:], qT[0][:, n - ET, :],
                                                     ALU.mult, ALU.subtract).then_inc(turned, 1)
                    if j < NORMED:
                        dve.wait_ge(sq_ready, at(i, NORMED, j + 1))
                        dve.tensor_scalar(msq[0:m, j % 2, :], msq[0:m, j % 2, :], 1.0 / HD, RMS_EPS,
                                          ALU.mult, ALU.add).then_inc(ms_ready, 1)
                    if j < ET:
                        dve.wait_ge(v_hi, at(i, ET, j + 1))
                        dve.scalar_tensor_tensor(v[1][0:m, j, :], bank(VB[j % 2])[0:m, :], 1.0 / WSCALE,
                                                 v[0][0:m, j, :], ALU.mult, ALU.subtract).then_inc(v_ready, 1)
                    if j == NORMED + 2:
                        dve.wait_ge(mask_loaded, 16)
                    if j > NORMED + 1:
                        maxima(*early[j - NORMED - 2])

                def low_part(n, j):
                    r, ne = slot_rows(j), slot_tiles(j)
                    dve.wait_ge(t_act, at(i, T_PS, t_count(n, j)))
                    hi, lo = (t_[0:r, G * j:G * j + ne, n % 2, :] for t_ in pT[n // 2 % 2])
                    dve.scalar_tensor_tensor(lo, t_bank(t_index[n, j])[0:r, 0:ne * P]
                                             .rearrange("p (e s) -> p e s", e=ne), PSCALE, hi, ALU.mult,
                                             ALU.subtract).then_inc(t_dve, 1)

                def reciprocals(m):
                    dve.wait_ge(exp_done, at(i, HEADS, 2 * m + 2))
                    if m >= 1:
                        dve.wait_ge(diag_ready, at(i, PAIRS, m))
                    own(dve.tensor_tensor(rsum[:], sums[:, 2 * m:2 * m + 2, 0], sums[:, 2 * m:2 * m + 2, 1], ALU.add))
                    own(dve.reciprocal(rsum[:], rsum[:]))
                    dve.tensor_tensor(diag.rearrange("p (h s) -> p h s", h=2),
                                      ident_r[:].unsqueeze(1).to_broadcast([P, 2, P]),
                                      rsum[:].unsqueeze(2).to_broadcast([P, 2, P]), ALU.mult)\
                       .then_inc(diag_made, 1)

                def spread_lo(m):
                    dve.wait_ge(diag_hi, at(i, PAIRS, m + 1))
                    dve.tensor_tensor(diag_p[1], diag, diag_p[0], ALU.subtract).then_inc(diag_ready, 1)

                def divide(m):
                    dve.wait_ge(t_act, at(i, T_PS, r_count(m)))
                    dve.wait_ge(pv_ps, at(i, PAIRS, m + 1))
                    if m >= 1:
                        dve.wait_ge(oT_ready, at(i, PAIRS, m))
                    dve.tensor_tensor(oT[:], bank(OB[m % 2])[:, 0:2 * P], rbc[m % 2], ALU.mult).then_inc(of_ready, 1)

                def output_lo(m):
                    dve.wait_ge(oT_hi, at(i, PAIRS, m + 1))
                    dve.tensor_tensor(oT_p[m % 2][1], oT[:], oT_p[m % 2][0], ALU.subtract).then_inc(oT_ready, 1)

                for n, c in early[LAG - 1:]:
                    maxima(n, c)
                for n in range(HEADS):
                    m = n // 2
                    for j in range(SLOTS):
                        low_part(n, j)
                        if n % 2 == 0 and j == 0 and m >= 1:
                            reciprocals(m - 1)
                        if n % 2 == 0 and j == 2 and m >= 1:
                            spread_lo(m - 1)
                        if n % 2 == 1 and j == 1 and m >= 2:
                            divide(m - 2)
                        if n % 2 == 1 and j == 3 and m >= 2:
                            output_lo(m - 2)
                        if n + 2 < HEADS:
                            maxima(n + 2, j)
                reciprocals(PAIRS - 1)
                divide(PAIRS - 2)
                spread_lo(PAIRS - 1)
                output_lo(PAIRS - 2)
                divide(PAIRS - 1)
                output_lo(PAIRS - 1)
                dve.wait_ge(s.x_kept, at(i, 1, 1))
                dve.wait_ge(y_ps, at(i, PAIRS, PAIRS))
                dve.scalar_tensor_tensor(s.z[:].rearrange("p s d -> p (s d)"), bank(YB), 1.0 / WSCALE,
                                         s.xr[:].rearrange("p s d -> p (s d)"), ALU.mult, ALU.add)\
                   .then_inc(s.z_made, 1)

            s.each_sequence(dve, sequence)
    s.close()


def experts_stage(k, x_in, x_out, gate_w, gate_up, down, merge, dominant):
    nc, ps, ident = k.nc, k.ps, k.ident
    E, I = down.shape[0], down.shape[1]
    GR = dominant.shape[1]
    s = Stage(k, "experts", x_in, x_out)
    gw = s.sb("gw", [P, DC, E])
    gu = s.sb("gu", [P, DC, GR * 2 * I])
    dn = s.sb("dn", [I, GR, D])
    dom = s.sb("dom", [1, GR], I32)
    mg, mgf = s.sb("mg", [E, 1], I32), s.sb("mgf", [E, 1])
    gi, gf = s.sb("gi", [E, GR], I32), s.sb("gf", [E, GR])
    group = s.sb("group", [E, GR])
    nmx, e, top, left, sel = (s.sb("nmx", [P, ST]), s.sb("e", [P, ST, E]), s.sb("top", [P, ST, 8]),
                              s.sb("left", [P, ST, E]), s.sb("sel", [P, ST, E]))
    tsum, rts, selT, wt = s.sb("tsum", [P, ST]), s.sb("rts", [P, ST]), s.sb("selT", [E, S]), s.sb("wt", [P, ST, GR])
    g = [s.sb(f"g{n}", [P, GR, I]) for n in range(ST)]
    a = [s.sb(f"a{n}", [P, GR, I]) for n in range(ST)]
    aT = [s.sb(f"aT{n}", [I, GR, P]) for n in range(ST)]
    (w_loaded, dom_loaded, const_ready, lg_ps, nmx_ready, e_ready, sel_ready, selT_ps, selT_ready, w_ps, wt_ready,
     h_ps, silu_ready, a_half, a_ready, t_ps, t_ev, y_ps, dve_own) = (s.sem(n) for n in (
        "w_loaded", "dom_loaded", "const_ready", "lg_ps", "nmx_ready", "e_ready", "sel_ready", "selT_ps",
        "selT_ready", "w_ps", "wt_ready", "h_ps", "silu_ready", "a_half", "a_ready", "t_ps", "t_ev", "y_ps",
        "dve_own"))
    HB = range(0, 4)
    TB, YB, MB, XB = (4, 5), 6, 7, 4
    W2 = 2 * 2 * I
    hid = ps[:, 0:4, 0:W2].rearrange("p b (g o) -> p b g o", g=2)
    v4 = lambda t_: t_[:].rearrange("p (b g) i -> p b g i", g=2)
    misc = ps[:, MB, :]
    LG, WP, TP = misc[:, 0:ST * E], misc[:, 64:64 + ST * GR], misc[0:E, 128:128 + S]

    with nc.Block() as block:
        @block.sync
        def _(sp):
            sp.dma_start(dom[:], dominant).then_inc(dom_loaded, 16)
            sp.dma_start(gw[:], gate_w.rearrange("(c p) n -> p c n", p=P)).then_inc(w_loaded, 16)
            sp.dma_start(mg[:], merge).then_inc(w_loaded, 16)
            sp.wait_ge(dom_loaded, 16)
            for n in range(GR):
                x = sp.value_load(dom[0:1, n:n + 1], min_val=0, max_val=E - 1)
                sp.dma_start(gu[:, :, n * 2 * I:(n + 1) * 2 * I],
                             one(gate_up, x).rearrange("(c p) o -> p c o", p=P)).then_inc(w_loaded, 16)
                sp.dma_start(dn[:, n, :], one(down, x)).then_inc(w_loaded, 16)
            s.rows_dma(sp)

        @block.gpsimd
        def _(pool):
            pool.iota(gi[:], [[1, GR]], base=0, channel_multiplier=0).then_inc(const_ready, 1)
            with pool.Fori(0, B) as i:
                s.keep_x(pool, i)
                s.norm_pool(pool, i)

        @block.tensor
        def _(pe):
            pe.wait_ge(w_loaded, 16 * (2 + 2 * GR))
            pe.wait_ge(const_ready, 2)
            with pe.Fori(0, B) as i:
                def hidden(st):
                    if st >= 1:
                        pe.wait_ge(a_half, at(i, ST, st))
                    for q in HB:
                        for dc in range(DC):
                            last = pe.matmul(ps[:, q, 0:W2], s.xT[:, dc, st * P:(st + 1) * P],
                                             gu[:, dc, q * W2:(q + 1) * W2], start=dc == 0, stop=dc == DC - 1)
                    last.then_inc(h_ps, 1)

                def down_product(st):
                    pe.wait_ge(a_ready, at(i, ST, st + 1))
                    if st >= 1:
                        pe.wait_ge(t_ev, at(i, 2 * ST, 2 * st))
                    for n in range(GR):
                        last = pe.transpose(ps[0:I, TB[n // 4], (n % 4) * P:(n % 4 + 1) * P], a[st][:, n, :], ident[:])
                        if n % 4 == 3:
                            last.then_inc(t_ps, 1)
                    pe.wait_ge(t_ev, at(i, 2 * ST, 2 * st + 2))
                    if st == 0:
                        pe.wait_ge(s.z_made, at(i, 1, 1))
                    for n in range(GR):
                        last = pe.matmul(ps[:, YB, st * D:(st + 1) * D], aT[st][:, n, :], dn[:, n, :],
                                         start=n == 0, stop=n == GR - 1)
                    last.then_inc(y_ps, 1)

                s.transpose_x(pe, i, ps[:, XB, :])
                pe.wait_ge(s.xT_ready, at(i, 1, 1))
                for st in range(ST):
                    for dc in range(DC):
                        last = pe.matmul(LG[:, st * E:(st + 1) * E], s.xT[:, dc, st * P:(st + 1) * P], gw[:, dc, :],
                                         start=dc == 0, stop=dc == DC - 1)
                last.then_inc(lg_ps, 1)
                hidden(0)
                pe.wait_ge(sel_ready, at(i, 1, 1))
                for st in range(ST):
                    last = pe.transpose(TP[:, st * P:(st + 1) * P], sel[:, st, :], ident[:])
                last.then_inc(selT_ps, 1)
                pe.wait_ge(selT_ready, at(i, 1, 1))
                for st in range(ST):
                    last = pe.matmul(WP[:, st * GR:(st + 1) * GR], selT[:, st * P:(st + 1) * P], group[:],
                                     start=True, stop=True)
                last.then_inc(w_ps, 1)
                hidden(1)
                down_product(0)
                down_product(1)

        @block.scalar
        def _(act):
            with act.Fori(0, B) as i:
                s.copy_xT(act, i, ps[:, XB, :])
                act.wait_ge(nmx_ready, at(i, 1, 1))
                for st in range(ST):
                    last = act.activation(e[:, st, :], LG[:, st * E:(st + 1) * E], ACT.Exp, bias=nmx[:, st:st + 1])
                last.then_inc(e_ready, 1)
                for st in range(ST):
                    act.wait_ge(h_ps, at(i, ST, st + 1))
                    act.activation(v4(g[st]), hid[:, :, :, 0:I], ACT.Silu).then_inc(silu_ready, 1)
                for st in range(ST):
                    for q in range(2):
                        act.wait_ge(t_ps, at(i, 2 * ST, 2 * st + q + 1))
                        act.copy(aT[st][:, 4 * q:4 * q + 4, :].rearrange("p g s -> p (g s)"),
                                 ps[0:I, TB[q], :]).then_inc(t_ev, 1)

        @block.vector
        def _(dve):
            s.credits(dve)
            dve.wait_ge(w_loaded, 16 * (2 + 2 * GR))
            dve.wait_ge(const_ready, 1)
            first = Chain(dve, dve_own)
            dve.tensor_copy(mgf[:], mg[:])
            first(dve.tensor_copy(gf[:], gi[:]))
            dve.tensor_scalar(group[:], gf[:], mgf[:], None, ALU.is_equal).then_inc(const_ready, 1)

            def sequence(i, before):
                own = Chain(dve, a_half, ST, i)
                fence = Chain(dve, s.own2, 3, i)
                dve.wait_ge(lg_ps, at(i, 1, 1))
                dve.tensor_reduce(nmx[:], LG.rearrange("p (s e) -> p s e", s=ST), AX_X, ALU.max, negate=True)\
                   .then_inc(nmx_ready, 1)
                dve.wait_ge(e_ready, at(i, 1, 1))
                s.carry(dve)
                for st in range(ST):
                    last = dve.max(top[:, st, :], e[:, st, :])
                fence(last)
                s.carry(dve)
                for st in range(ST):
                    last = dve.match_replace(left[:, st, :], top[:, st, :], e[:, st, :], -1.0)
                fence(last)
                for st in range(ST):
                    last = dve.scalar_tensor_tensor(sel[:, st, :], left[:, st, :], 0.0, e[:, st, :], ALU.is_lt,
                                                    ALU.mult, accum_out=tsum[:, st:st + 1])
                fence(last)
                dve.sem_inc(sel_ready, 1)
                dve.reciprocal(rts[:], tsum[:])
                s.norm_before(dve, before)
                dve.wait_ge(selT_ps, at(i, 1, 1))
                dve.tensor_copy(selT[:], TP).then_inc(selT_ready, 1)
                dve.wait_ge(w_ps, at(i, 1, 1))
                dve.tensor_tensor(wt[:], WP.rearrange("p (s g) -> p s g", s=ST),
                                  rts[:].unsqueeze(2).to_broadcast([P, ST, GR]), ALU.mult).then_inc(wt_ready, 1)
                for st in range(ST):
                    dve.wait_ge(silu_ready, at(i, ST, st + 1))
                    own(dve.tensor_tensor(v4(a[st]), hid[:, :, :, I:2 * I], v4(g[st]), ALU.mult))
                    if st == 0:
                        dve.wait_ge(wt_ready, at(i, 1, 1))
                    dve.tensor_tensor(a[st][:], a[st][:], wt[:, st, :].unsqueeze(2).to_broadcast([P, GR, I]),
                                      ALU.mult).then_inc(a_ready, 1)
                own.end()
                dve.wait_ge(s.x_kept, at(i, 1, 1))
                dve.wait_ge(y_ps, at(i, ST, ST))
                dve.tensor_tensor(s.z[:].rearrange("p s d -> p (s d)"), ps[:, YB, :],
                                  s.xr[:].rearrange("p s d -> p (s d)"), ALU.add).then_inc(s.z_made, 1)

            s.each_sequence(dve, sequence)
    s.close()


def memory_stage(k, x_in, x_out, ctxT_in, ctx_in, mask_in):
    nc, ps, ident = k.nc, k.ps, k.ident
    E = ctxT_in.shape[2]
    ET = (E + P - 1) // P
    FULL = E // P
    rows = [min(P, E - e * P) for e in range(ET)]
    chunks = [(c, min(BANK, E - c)) for c in range(0, E, BANK)]
    NC = len(chunks)
    SCALE = float(D) ** -0.5
    G = BANK // P
    SLOTS = (ET + G - 1) // G
    NT = ST * SLOTS
    s = Stage(k, "memory", x_in, x_out)
    ctxT, ctx = s.sb("ctxT", [P, DC, E]), s.sb("ctx", [P, ET, D])
    m8 = s.sb("m8", [P, E], U8)
    am = s.sb("am", [P, E])
    any_ = s.sb("any", [P, 1])
    sc = [s.sb(f"sc{n}", [P, E]) for n in range(ST)]
    pT = [s.sb(f"pT{n}", [P, ET, P]) for n in range(ST)]
    mx, nmx, sums, rs = s.sb("mx", [P, ST, NC]), s.sb("nmx", [P, ST]), s.sb("sums", [P, ST]), s.sb("rs", [P, ST])
    (ctxT_loaded, ctx_loaded, m_loaded, am_ready, any_ready, sc_ps, sc_read, nmx_ready, exp_done, t_ps, t_ev, o_ps, dve_own) = (
        s.sem(n) for n in ("ctxT_loaded", "ctx_loaded", "m_loaded", "am_ready", "any_ready", "sc_ps", "sc_read", "nmx_ready",
                           "exp_done", "t_ps", "t_ev", "o_ps", "dve_own"))
    TB, OB, XB = (4, 5), 6, 7

    with nc.Block() as block:
        @block.sync
        def _(sp):
            def context(i):
                later = not isinstance(i, int)
                if later:
                    sp.wait_ge(am_ready, at(i, 1, 0))
                    sp.wait_ge(any_ready, at(i, 1, 0))
                    s.carry(sp)
                sp.dma_start(m8[:], one(mask_in, i).partition_broadcast(P)).then_inc(m_loaded, 16)
                if later:
                    sp.wait_ge(sc_ps, at(i, NC * ST, 0))
                    s.carry(sp)
                sp.dma_start(ctxT[:], one(ctxT_in, i).rearrange("(c p) e -> p c e", p=P)).then_inc(ctxT_loaded, 16)
                if later:
                    sp.wait_ge(o_ps, at(i, ST, 0))
                    s.carry(sp)
                c = one(ctx_in, i)
                sp.dma_start(ctx[:, 0:FULL, :], c[0:FULL * P, :].rearrange("(e p) d -> p e d", p=P))\
                  .then_inc(ctx_loaded, 16)
                sp.dma_start(ctx[0:rows[-1], FULL, :], c[FULL * P:E, :]).then_inc(ctx_loaded, 16)

            s.rows_dma(sp, context)

        @block.gpsimd
        def _(pool):
            def slots(i):
                pool.wait_ge(m_loaded, at(i, 16, 16))
                s.carry(pool)
                pool.tensor_scalar(am[:], m8[:], 1.0, 1e30 / SCALE, ALU.subtract, ALU.mult).then_inc(am_ready, 1)

            slots(0)
            with pool.Fori(0, B - 1) as i:
                s.keep_x(pool, i)
                pool.wait_ge(sc_read, at(i, NC * ST, NC * ST))
                slots(i + 1)
                s.norm_pool(pool, i)
            s.keep_x(pool, B - 1)
            s.norm_pool(pool, B - 1)

        @block.tensor
        def _(pe):
            with pe.Fori(0, B) as i:
                def scores(st):
                    for c, (e0, w) in enumerate(chunks):
                        if st >= 1:
                            pe.wait_ge(sc_read, at(i, NC * ST, NC * (st - 1) + c + 1))
                        for dc in range(DC):
                            last = pe.matmul(ps[:, c, 0:w], s.xT[:, dc, st * P:(st + 1) * P], ctxT[:, dc, e0:e0 + w],
                                             start=dc == 0, stop=dc == DC - 1)
                        last.then_inc(sc_ps, 1)

                def turn_probs(st):
                    pe.wait_ge(exp_done, at(i, ST, st + 1))
                    for j in range(SLOTS):
                        n = SLOTS * st + j
                        if n >= 2:
                            pe.wait_ge(t_ev, at(i, NT, n - 1))
                        for e in range(G * j, min(G * j + G, ET)):
                            last = pe.transpose(ps[0:rows[e], TB[n % 2], (e % G) * P:(e % G + 1) * P],
                                                sc[st][:, e * P:e * P + rows[e]], ident[:])
                        last.then_inc(t_ps, 1)

                def mix(st):
                    pe.wait_ge(t_ev, at(i, NT, SLOTS * (st + 1)))
                    if st == 0:
                        pe.wait_ge(s.z_made, at(i, 1, 1))
                    for e in range(ET):
                        last = pe.matmul(ps[:, OB, st * D:(st + 1) * D], pT[st][0:rows[e], e, :], ctx[0:rows[e], e, :],
                                         start=e == 0, stop=e == ET - 1)
                    last.then_inc(o_ps, 1)

                s.transpose_x(pe, i, ps[:, XB, :])
                pe.wait_ge(s.xT_ready, at(i, 1, 1))
                pe.wait_ge(ctxT_loaded, at(i, 16, 16))
                scores(0)
                scores(1)
                turn_probs(0)
                pe.wait_ge(ctx_loaded, at(i, 32, 32))
                mix(0)
                turn_probs(1)
                mix(1)

        @block.scalar
        def _(act):
            with act.Fori(0, B) as i:
                s.copy_xT(act, i, ps[:, XB, :])
                for st in range(ST):
                    act.wait_ge(nmx_ready, at(i, ST, st + 1))
                    act.activation(sc[st][:], sc[st][:], ACT.Exp, bias=nmx[:, st:st + 1], scale=SCALE,
                                   accum_out=sums[:, st:st + 1]).then_inc(exp_done, 1)
                    for j in range(SLOTS):
                        n = SLOTS * st + j
                        act.wait_ge(t_ps, at(i, NT, n + 1))
                        ne = min(G, ET - G * j)
                        m = P if ne == G else rows[-1]
                        act.copy(pT[st][0:m, G * j:G * j + ne, :].rearrange("p e s -> p (e s)"),
                                 ps[0:m, TB[n % 2], 0:ne * P]).then_inc(t_ev, 1)

        @block.vector
        def _(dve):
            s.credits(dve)

            def sequence(i, before):
                own = Chain(dve, dve_own, ST + 2, i)
                dve.wait_ge(am_ready, at(i, 1, 1))
                for st in range(ST):
                    for c, (e0, w) in enumerate(chunks):
                        dve.wait_ge(sc_ps, at(i, NC * ST, NC * st + c + 1))
                        s.carry(dve)
                        dve.tensor_tensor_reduce(sc[st][:, e0:e0 + w], ps[:, c, 0:w], am[:, e0:e0 + w], 1.0, -3.0e38,
                                                 ALU.add, ALU.max, mx[:, st, c:c + 1]).then_inc(sc_read, 1)
                    dve.wait_ge(sc_read, at(i, NC * ST, NC * st + NC))
                    own(dve.tensor_reduce(nmx[:, st:st + 1], mx[:, st, :], AX_X, ALU.max, negate=True))
                    dve.tensor_scalar(nmx[:, st:st + 1], nmx[:, st:st + 1], SCALE, None, ALU.mult)\
                       .then_inc(nmx_ready, 1)
                    if st == 0:
                        s.norm_before(dve, before)
                dve.wait_ge(m_loaded, at(i, 16, 16))
                dve.tensor_reduce(any_[:], m8[:], AX_X, ALU.max).then_inc(any_ready, 1)
                dve.wait_ge(any_ready, at(i, 1, 1))
                dve.wait_ge(exp_done, at(i, ST, ST))
                own(dve.reciprocal(rs[:], sums[:]))
                own(dve.tensor_scalar(rs[:], rs[:], any_[:], None, ALU.mult))
                own.end()
                dve.wait_ge(s.x_kept, at(i, 1, 1))
                dve.wait_ge(o_ps, at(i, ST, ST))
                for st in range(ST):
                    last = dve.scalar_tensor_tensor(s.z[:, st, :], ps[:, OB, st * D:(st + 1) * D], rs[:, st:st + 1],
                                                    s.xr[:, st, :], ALU.mult, ALU.add)
                last.then_inc(s.z_made, 1)

            s.each_sequence(dve, sequence)
    s.close()


def rotary_stage(k, x_in, x_out, wq, bq, wk, bk, wv, bv, wo, bo, key_w, cos_in, sin_in):
    nc, ps, ident = k.nc, k.ps, k.ident
    NH, NKV, HD = 32, 8, 64
    HALF = HD // 2
    QUARTERS = NH // NKV
    G = NH // NKV
    OT = NH * HD // P
    OW = NH * HD
    GC = G * HD // P
    W3 = 3 * P
    SCALE = float(HD) ** -0.5
    SPLITS = 6
    WSCALE = 64.0
    PSCALE = 15 * float(np.log(2.0))
    PASSES = ((0, 0), (0, 1), (1, 0))
    s = Stage(k, "rotary", x_in, x_out)
    wq_p, wk_p, wv_p, wo_p = ([s.sb(f"{name}_{part}", [P, c, n], F16) for part in ("hi", "lo")]
                              for name, c, n in (("wq", DC, OW), ("wk", DC, NKV * HD), ("wv", DC, NKV * HD),
                                                 ("wo", OT, D)))
    bq_s, bk_s, bv_s, bo_s = s.sb("bq", [P, OW]), s.sb("bk", [P, 512]), s.sb("bv", [P, 512]), s.sb("bo", [P, D])
    kw = s.sb("kw", [P, NH])
    ident16 = s.sb("ident16", [P, P], F16)
    cos, sin = s.sb("cos", [P, ST, HALF]), s.sb("sin", [P, ST, HALF])
    nsin = s.sb("nsin", [P, ST, HALF])
    cm = s.sb("cm", [P, W3])
    raw = [s.sb(f"raw{n}", [P, 512]) for n in range(2)]
    byc = [s.sb(f"byc{n}", [P, 512]) for n in range(2)]
    rot = [s.sb(f"rot{n}", [P, 512]) for n in range(2)]
    bys = s.sb("bys", [P, 512])
    split = [s.sb(f"split{n}", [P, NKV, 2, HD], F16) for n in range(SPLITS)]
    kT = [s.sb(f"kT_{part}", [P, NKV, S], F16) for part in ("hi", "lo")]
    v_f = [s.sb(f"v_f{n}", [P, NKV * HD]) for n in range(ST)]
    v = [s.sb(f"v_{part}", [P, ST, NKV * HD], F16) for part in ("hi", "lo")]
    qT = s.sb("qT", [P, ST, NH, P], F16)
    sc = [s.sb(f"sc{n}", [P, W3]) for n in range(4)]
    pT = [[s.sb(f"pT{n}_{part}", [P, W3], F16) for part in ("hi", "lo")] for n in range(4)]
    mx, nmx, sums, rs = (s.sb("mx", [P, 4, ST]), s.sb("nmx", [P, 4, ST]), s.sb("sums", [P, NH, ST]),
                         s.sb("rs", [P, G * ST]))
    o = s.sb("o", [P, ST, OW])
    oT = [[s.sb(f"oT{n}_{part}", [P, ST, GC, P], F16) for part in ("hi", "lo")] for n in range(2)]
    xT_p = [s.xT[:].rearrange("p c s -> p (c s)").bitcast(F16)[:, n * DC * S:(n + 1) * DC * S]
            .rearrange("p (c s) -> p c s", c=DC) for n in range(2)]
    w_in = [(wk_p, wk, raw[0][:], raw[1][:]), (wv_p, wv, byc[0][:], byc[1][:])]
    wq_in = qT[:].rearrange("p s n q -> p (s n q)").bitcast(F32)
    wo_in = o[:].rearrange("p s n -> p (s n)")
    (kv_loaded, wq_loaded, wo_loaded, const_ready, w_hi, w_ready, xT_hi, pr_ps, raw_ready, byc_ready, bys_ready, rot_ready, split_hi,
     k_split, q_split, turn_ps, turned, v_ps, v_sum, v_hi, v_ready) = (s.sem(n) for n in (
            "kv_loaded", "wq_loaded", "wo_loaded", "const_ready", "w_hi", "w_ready", "xT_hi", "pr_ps", "raw_ready", "byc_ready", "bys_ready",
            "rot_ready", "split_hi", "k_split", "q_split", "turn_ps", "turned", "v_ps", "v_sum", "v_hi", "v_ready"))
    (sc_ps, sc_read, nmx_ready, exp_done, t_ps, t_hi, t_ready, o_ps, o_ready, y_ps,
     dve_own) = (s.sem(n) for n in (
            "sc_ps", "sc_read", "nmx_ready", "exp_done", "t_ps", "t_hi", "t_ready", "o_ps", "o_ready", "y_ps", "dve_own"))
    tiles = [("k", st, 0) for st in range(ST)] + [("q", st, a) for st in range(ST) for a in range(QUARTERS)]
    NT = len(tiles)
    turns = [(j, part) for j in range(ST) for part in range(2)] + [(j, 0) for j in range(ST, NT)]
    NTURN = len(turns)
    first_turn = lambda j: 2 * j if j < ST else j + ST
    LAG = 3
    YB, TB, OB, XB = 3, (4, 5), (6, 7), 7
    half = lambda n: ps[:, TB[n % 2], :].bitcast(F16)
    GROUPS = NH // G
    turned_out = lambda n: n // G - 2 if n % G == 0 and n >= 2 * G else None
    order = []
    for n in range(NH):
        if turned_out(n) is not None:
            order.append(("o", turned_out(n)))
        order.append(n)
    order += [("o", GROUPS - 2), ("o", GROUPS - 1)]
    T_PS = len(order)
    t_index = {what: x for x, what in enumerate(order)}

    with nc.Block() as block:
        @block.sync
        def _(sp):
            def w(t_, a, loaded):
                sp.dma_start(t_, a).then_inc(loaded, 16)

            for parts, a, in0, in1 in w_in:
                w(in0, a[0:P, :], kv_loaded)
                w(in1, a[P:2 * P, :], kv_loaded)
            for t_, a in ((bk_s, bk), (bv_s, bv)):
                w(t_[:], a.partition_broadcast(P), kv_loaded)
            w(cos[:], cos_in.rearrange("(s p) e -> p s e", p=P), kv_loaded)
            w(sin[:], sin_in.rearrange("(s p) e -> p s e", p=P), kv_loaded)
            for t_, a in ((kw, key_w), (bq_s, bq)):
                w(t_[:], a.partition_broadcast(P), wq_loaded)
            w(wq_in.rearrange("p (c n) -> p c n", c=DC), wq.rearrange("(c p) n -> p c n", p=P), wq_loaded)
            w(bo_s[:], bo.partition_broadcast(P), wo_loaded)
            w(wo_in.rearrange("p (q n) -> p q n", q=OT), wo.rearrange("(q p) n -> p q n", p=P), wo_loaded)
            s.rows_dma(sp)

        KV_ALL, WQ_ALL, WO_ALL = 16 * (4 + 2 + 2), 16 * 3, 16 * 2
        W_SPLITS = 4 + 1 + 1

        @block.gpsimd
        def _(pool):
            own = Chain(pool, s.pool_own)
            own(pool.memset(cm[:], 0.0))
            for a in (0, 2 * P):
                last = pool.affine_select(out=cm[:, a:a + P], in_=cm[:, a:a + P], compare_op=ALU.is_ge, fill=-1e30,
                                          base=0, pattern=[[-1, P]], channel_multiplier=1)
            last.then_inc(const_ready, 1)
            pool.wait_ge(w_ready, W_SPLITS)
            with pool.Fori(0, B) as i:
                s.keep_x(pool, i, bo_s[:])
                def low_part(j):
                    f = first_turn(j) % SPLITS
                    pool.wait_ge(split_hi, at(i, NT, j + 1))
                    pool.tensor_tensor(split[f][:, :, 1, :], rot[j % 2][:].rearrange("p (h e) -> p h e", e=HD),
                                       split[f][:, :, 0, :], ALU.subtract).then_inc(q_split, 1)

                for j, (kind, st, a) in enumerate(tiles):
                    pool.wait_ge(raw_ready, at(i, NT, j + 1))
                    if j >= 2:
                        pool.wait_ge(rot_ready, at(i, NT, j - 1))
                    pool.tensor_tensor(byc[j % 2][:].rearrange("p (h e) -> p h e", e=HALF),
                                       raw[j % 2][:].rearrange("p (h e) -> p h e", e=HALF),
                                       cos[:, st, :].unsqueeze(1).to_broadcast([P, 16, HALF]), ALU.mult)\
                        .then_inc(byc_ready, 1)
                    if j > ST:
                        low_part(j - 1)
                low_part(NT - 1)
                for n in range(NH):
                    pool.wait_ge(sc_read, at(i, NH * ST, ST * n + ST))
                    s.carry(pool)
                    pool.tensor_scalar(nmx[:, n % 4, :], mx[:, n % 4, :], -SCALE, PSCALE, ALU.mult, ALU.add)\
                        .then_inc(nmx_ready, 1)
                s.norm_pool(pool, i)

        @block.tensor
        def _(pe):
            pe.wait_ge(w_ready, W_SPLITS)
            with pe.Fori(0, B) as i:
                def product(out, st, right, n0, n1):
                    for dc in range(DC):
                        for lp, rp in PASSES:
                            last = pe.matmul(out, xT_p[lp][:, dc, st * P:(st + 1) * P], right[rp][:, dc, n0:n1],
                                             start=dc + lp + rp == 0, stop=dc == DC - 1 and lp == 1)
                    return last

                def project(j):
                    kind, st, a = tiles[j]
                    if j >= 2:
                        pe.wait_ge(raw_ready, at(i, NT, j - 1))
                    if kind == "k":
                        product(ps[:, j % 2, :], st, wk_p, 0, 512).then_inc(pr_ps, 1)
                        product(ps[:, 2 + st, :], st, wv_p, 0, 512).then_inc(v_ps, 1)
                    else:
                        product(ps[:, j % 2, :], st, wq_p, a * 512, (a + 1) * 512).then_inc(pr_ps, 1)

                def turn(x):
                    j, part = turns[x]
                    if j < ST and part == 0:
                        pe.wait_ge(split_hi, at(i, NT, j + 1))
                    elif j < ST:
                        pe.wait_ge(k_split, at(i, ST, j + 1))
                    else:
                        pe.wait_ge(q_split, at(i, NT - ST, j - ST + 1))
                    if x >= 2:
                        pe.wait_ge(turned, at(i, NTURN, x - 1))
                    for h in range(NKV):
                        last = pe.transpose(half(x)[:, h * P:(h + 1) * P],
                                            split[x % SPLITS][:, h, :, :].rearrange("p t e -> p (t e)"), ident16[:])
                    last.then_inc(turn_ps, 1)

                def scores(n):
                    if n >= 3:
                        pe.wait_ge(sc_read, at(i, NH * ST, ST * (n - 2)))
                    for st in range(ST):
                        for part in range(2):
                            last = pe.matmul(ps[:, n % 3, st * P:st * P + (st + 1) * P], qT[:, st, n, :],
                                             kT[part][:, n // G, 0:(st + 1) * P], start=part == 0, stop=part == 1)
                    last.then_inc(sc_ps, 1)

                def turn_bank(what):
                    x = t_index[what]
                    if x >= 2:
                        pe.wait_ge(t_ready, at(i, T_PS, x - 1))
                    return ps[:, TB[x % 2], :]

                def turn_probs(n):
                    pe.wait_ge(exp_done, at(i, NH, n + 1))
                    out = turn_bank(n)
                    for q in range(3):
                        last = pe.transpose(out[:, q * P:(q + 1) * P], sc[n % 4][:, q * P:(q + 1) * P], ident[:])
                    last.then_inc(t_ps, 1)

                def turn_outputs(g):
                    pe.wait_ge(o_ready, at(i, GROUPS, g + 1))
                    out = turn_bank(("o", g))
                    for st in range(ST):
                        for p in range(GC):
                            last = pe.transpose(out[:, (st * GC + p) * P:(st * GC + p + 1) * P],
                                                o[:, st, (g * GC + p) * P:(g * GC + p + 1) * P], ident[:])
                    last.then_inc(t_ps, 1)

                def output(g, st):
                    if st == 0:
                        pe.wait_ge(t_ready, at(i, T_PS, t_index["o", g] + 1))
                    for p in range(GC):
                        for lp, rp in PASSES:
                            last = pe.matmul(ps[:, YB, st * D:(st + 1) * D], oT[g % 2][lp][:, st, p, :],
                                             wo_p[rp][:, g * GC + p, :], start=g + st + p + lp + rp == 0,
                                             stop=g == GROUPS - 1 and p == GC - 1 and lp == 1,
                                             skip_group_check=True)
                    if st == ST - 1:
                        last.then_inc(y_ps, 1)

                def mix(n):
                    kv = n // G
                    out = lambda st: ps[:, OB[n // G % 2], (n % G * ST + st) * HD:(n % G * ST + st + 1) * HD]
                    pe.wait_ge(t_ready, at(i, T_PS, t_index[n] + 1))
                    if n % G == 0 and n >= 2 * G:
                        pe.wait_ge(o_ready, at(i, GROUPS, n // G - 1))
                    for q, st, kt in ((0, 0, 0), (1, 1, 0), (2, 1, 1)):
                        for pp, vv in PASSES:
                            last = pe.matmul(out(st), pT[n % 4][pp][:, q * P:(q + 1) * P],
                                             v[vv][:, kt, kv * HD:(kv + 1) * HD], start=kt + pp + vv == 0,
                                             stop=kt == st and pp == 1)
                    last.then_inc(o_ps, 1)

                s.transpose_x(pe, i, ps[:, XB, :])
                pe.wait_ge(s.z_made, at(i, 1, 1))
                pe.wait_ge(s.xT_ready, at(i, 1, 1))
                x = 0
                for j in range(NT + LAG):
                    if j < NT:
                        project(j)
                    while j >= LAG and x < NTURN and turns[x][0] <= j - LAG:
                        turn(x)
                        x += 1
                pe.wait_ge(turned, at(i, NTURN, NTURN))
                pe.wait_ge(v_ready, at(i, ST, ST))
                for n in range(-3, NH):
                    if n + 3 < NH:
                        scores(n + 3)
                    if n >= 0:
                        if turned_out(n) is not None:
                            turn_outputs(turned_out(n))
                        turn_probs(n)
                    if n >= 2:
                        mix(n - 2)
                    if n % G >= 2 and n >= 2 * G:
                        output(n // G - 2, n % G - 2)
                turn_outputs(GROUPS - 2)
                mix(NH - 2)
                mix(NH - 1)
                turn_outputs(GROUPS - 1)
                for g in (GROUPS - 2, GROUPS - 1):
                    for st in range(ST):
                        output(g, st)

        @block.scalar
        def _(act):
            act.wait_ge(kv_loaded, KV_ALL)
            for parts, a, in0, in1 in w_in:
                for dc, w in enumerate((in0, in1)):
                    act.activation(parts[0][:, dc, :], w, ACT.Copy, scale=WSCALE).then_inc(w_hi, 1)
            act.wait_ge(const_ready, 2)
            act.copy(wq_p[0][:].rearrange("p c n -> p (c n)"), wq_in).then_inc(w_hi, 1)
            act.wait_ge(wo_loaded, WO_ALL)
            act.activation(wo_p[0][:].rearrange("p q n -> p (q n)"), wo_in, ACT.Copy, scale=WSCALE).then_inc(w_hi, 1)
            act.wait_ge(w_ready, W_SPLITS)
            with act.Fori(0, B) as i:
                act.wait_ge(s.xT_ps, at(i, 1, 1))
                act.copy(xT_p[0].rearrange("p c s -> p (c s)"), ps[:, XB, :]).then_inc(xT_hi, 1)

                def high_part(j):
                    kind, st, a = tiles[j]
                    f = first_turn(j)
                    x = rot[j % 2][:].rearrange("p (h e) -> p h e", e=HD)
                    act.wait_ge(rot_ready, at(i, NT, j + 1))
                    if f >= SPLITS:
                        act.wait_ge(turn_ps, at(i, NTURN, f - SPLITS + 1))
                    if kind == "k":
                        act.copy(split[f][:], x.unsqueeze(2).to_broadcast([P, NKV, 2, HD])).then_inc(split_hi, 1)
                        act.wait_ge(v_sum, at(i, ST, st + 1))
                        act.copy(v[0][:, st, :], v_f[st][:]).then_inc(v_hi, 1)
                    else:
                        act.copy(split[f % SPLITS][:, :, 0, :], x).then_inc(split_hi, 1)

                def turned_copy(x):
                    j, part = turns[x]
                    kind, st, a = tiles[j]
                    act.wait_ge(turn_ps, at(i, NTURN, x + 1))
                    if kind == "k":
                        act.copy(kT[part][:, :, st * P:(st + 1) * P], half(x).rearrange("p (g e) -> p g e", g=NKV))\
                           .then_inc(turned, 1)
                    else:
                        act.copy(qT[:, st, NKV * a:NKV * (a + 1), :].rearrange("p n q -> p (n q)"), half(x))\
                           .then_inc(turned, 1)

                x = 0
                for j in range(NT + LAG):
                    while j >= LAG and x < NTURN and turns[x][0] <= j - LAG:
                        turned_copy(x)
                        x += 1
                    if j < NT:
                        high_part(j)

                def exp(n):
                    act.wait_ge(nmx_ready, at(i, NH, n + 1))
                    for st in range(ST):
                        part = sc[n % 4][:, st * P:st * P + (st + 1) * P]
                        last = act.activation(part, part, ACT.Exp, bias=nmx[:, n % 4, st:st + 1], scale=SCALE,
                                              accum_out=sums[:, n, st:st + 1])
                    last.then_inc(exp_done, 1)

                def outputs_hi(g):
                    x = t_index["o", g]
                    if g >= 2:
                        act.wait_ge(y_ps, at(i, GROUPS, g - 1))
                    act.wait_ge(t_ps, at(i, T_PS, x + 1))
                    act.copy(oT[g % 2][0][:].rearrange("p s c q -> p (s c q)"), ps[:, TB[x % 2], :]).then_inc(t_hi, 1)

                exp(0)
                for n in range(NH):
                    if n + 1 < NH:
                        exp(n + 1)
                    if turned_out(n) is not None:
                        outputs_hi(turned_out(n))
                    if n >= 4:
                        act.wait_ge(o_ps, at(i, NH, n - 3))
                    act.wait_ge(t_ps, at(i, T_PS, t_index[n] + 1))
                    act.copy(pT[n % 4][0][:], ps[:, TB[t_index[n] % 2], 0:W3]).then_inc(t_hi, 1)
                outputs_hi(GROUPS - 2)
                outputs_hi(GROUPS - 1)

        @block.vector
        def _(dve):
            s.credits(dve)
            dve.wait_ge(kv_loaded, KV_ALL)
            dve.tensor_copy(ident16[:], ident[:])
            dve.tensor_scalar(nsin[:], sin[:], -1.0, None, ALU.mult)
            x = 0
            for parts, a, in0, in1 in w_in:
                for dc, w in enumerate((in0, in1)):
                    x += 1
                    dve.wait_ge(w_hi, x)
                    dve.scalar_tensor_tensor(parts[1][:, dc, :], w, WSCALE, parts[0][:, dc, :], ALU.mult, ALU.subtract)\
                       .then_inc(w_ready, 1)
            dve.wait_ge(wq_loaded, WQ_ALL)
            own0 = Chain(dve, s.own2)
            for dc in range(DC):
                w = wq_in[:, dc * OW:(dc + 1) * OW].rearrange("p (n e) -> p n e", n=NH)
                last = dve.scalar_tensor_tensor(w, w, WSCALE, kw[:].unsqueeze(2).to_broadcast([P, NH, HD]), ALU.mult,
                                                ALU.mult)
            own0(last)
            dve.wait_ge(const_ready, 1)
            dve.sem_inc(const_ready, 1)
            dve.tensor_tensor(bq_s[:].rearrange("p (n e) -> p n e", e=HD), bq_s[:].rearrange("p (n e) -> p n e", e=HD),
                              kw[:].unsqueeze(2).to_broadcast([P, NH, HD]), ALU.mult)
            dve.wait_ge(w_hi, x + 1)
            dve.tensor_tensor(wq_p[1][:].rearrange("p c n -> p (c n)"), wq_in,
                              wq_p[0][:].rearrange("p c n -> p (c n)"), ALU.subtract).then_inc(w_ready, 1)
            dve.wait_ge(w_hi, x + 2)
            dve.scalar_tensor_tensor(wo_p[1][:].rearrange("p q n -> p (q n)"), wo_in, WSCALE,
                                     wo_p[0][:].rearrange("p q n -> p (q n)"), ALU.mult, ALU.subtract)\
               .then_inc(w_ready, 1)
            dve.wait_ge(w_ready, W_SPLITS)

            def sequence(i, before):
                own = Chain(dve, dve_own, NH // G, i)

                def biased(j):
                    kind, st, a = tiles[j]
                    dve.wait_ge(pr_ps, at(i, NT, j + 1))
                    if j >= 2:
                        dve.wait_ge(byc_ready, at(i, NT, j - 1))
                    dve.scalar_tensor_tensor(raw[j % 2][:], ps[:, j % 2, :], 1.0 / WSCALE,
                                             bk_s[:] if kind == "k" else bq_s[:, a * 512:(a + 1) * 512], ALU.mult,
                                             ALU.add).then_inc(raw_ready, 1)
                    if kind == "k":
                        dve.wait_ge(v_ps, at(i, ST, st + 1))
                        dve.scalar_tensor_tensor(v_f[st][:], ps[:, 2 + st, :], 1.0 / WSCALE, bv_s[:], ALU.mult,
                                                 ALU.add).then_inc(v_sum, 1)

                def rotate(j):
                    kind, st, a = tiles[j]
                    x = raw[j % 2][:].rearrange("p (h t e) -> p h t e", t=2, e=HALF)
                    y = bys[:].rearrange("p (h t e) -> p h t e", t=2, e=HALF)
                    dve.wait_ge(raw_ready, at(i, NT, j + 1))
                    if j >= 1:
                        dve.wait_ge(rot_ready, at(i, NT, j))
                    for half_, table in ((0, nsin), (1, sin)):
                        last = dve.tensor_tensor(y[:, :, half_, :], x[:, :, 1 - half_, :],
                                                 table[:, st, :].unsqueeze(1).to_broadcast([P, 8, HALF]), ALU.mult)
                    last.then_inc(bys_ready, 1)
                    dve.wait_ge(bys_ready, at(i, NT, j + 1))
                    dve.wait_ge(byc_ready, at(i, NT, j + 1))
                    if j >= 2:
                        n = j - 1
                        dve.wait_ge(*((k_split, at(i, ST, n)) if n <= ST else (q_split, at(i, NT - ST, n - ST))))
                    dve.tensor_tensor(rot[j % 2][:], byc[j % 2][:], bys[:], ALU.add).then_inc(rot_ready, 1)

                dve.wait_ge(xT_hi, at(i, 1, 1))
                dve.tensor_tensor(xT_p[1].rearrange("p c s -> p (c s)"), ps[:, XB, :],
                                  xT_p[0].rearrange("p c s -> p (c s)"), ALU.subtract).then_inc(s.xT_ready, 1)
                s.norm_before(dve, before)
                biased(0)
                for j in range(NT):
                    if j + 1 < NT:
                        biased(j + 1)
                    rotate(j)
                    if 1 <= j <= ST:
                        f = first_turn(j - 1)
                        dve.wait_ge(split_hi, at(i, NT, j))
                        dve.tensor_tensor(split[f + 1][:], rot[j - 1][:].rearrange("p (h e) -> p h e", e=HD)
                                          .unsqueeze(2).to_broadcast([P, NKV, 2, HD]), split[f][:], ALU.subtract)\
                           .then_inc(k_split, 1)
                        dve.wait_ge(v_hi, at(i, ST, j))
                        dve.tensor_tensor(v[1][:, j - 1, :], v_f[j - 1][:], v[0][:, j - 1, :], ALU.subtract)\
                           .then_inc(v_ready, 1)

                def maxima(n):
                    dve.wait_ge(sc_ps, at(i, NH, n + 1))
                    if n >= 4:
                        dve.wait_ge(t_ps, at(i, T_PS, t_index[n - 4] + 1))
                    for st in range(ST):
                        a, b = st * P, st * P + (st + 1) * P
                        s.carry(dve)
                        dve.tensor_tensor_reduce(sc[n % 4][:, a:b], ps[:, n % 3, a:b], cm[:, a:b], 1.0, -3.0e38,
                                                 ALU.add, ALU.max, mx[:, n % 4, st:st + 1]).then_inc(sc_read, 1)

                def low_part(n):
                    x = t_index[n]
                    dve.wait_ge(t_hi, at(i, T_PS, x + 1))
                    dve.tensor_tensor(pT[n % 4][1][:], ps[:, TB[x % 2], 0:W3], pT[n % 4][0][:], ALU.subtract)\
                       .then_inc(t_ready, 1)

                def outputs_lo(g):
                    x = t_index["o", g]
                    dve.wait_ge(t_hi, at(i, T_PS, x + 1))
                    hi, lo = (t_[:].rearrange("p s c q -> p (s c q)") for t_ in oT[g % 2])
                    dve.tensor_tensor(lo, ps[:, TB[x % 2], :], hi, ALU.subtract).then_inc(t_ready, 1)

                def outputs(g):
                    dve.wait_ge(exp_done, at(i, NH, G * g + G))
                    if g >= 1:
                        dve.wait_ge(o_ready, at(i, GROUPS, g))
                    own(dve.reciprocal(rs[:], sums[:, G * g:G * g + G, :].rearrange("p n s -> p (n s)")))
                    dve.wait_ge(o_ps, at(i, NH, G * g + G))
                    dve.tensor_tensor(
                        o[:, :, G * g * HD:(G * g + G) * HD].rearrange("p s (n d) -> p n s d", n=G),
                        ps[:, OB[g % 2], :].rearrange("p (n s d) -> p n s d", n=G, s=ST),
                        rs[:].rearrange("p (n s) -> p n s", n=G).unsqueeze(3).to_broadcast([P, G, ST, HD]),
                        ALU.mult).then_inc(o_ready, 1)

                for n in range(-3, NH):
                    if 0 <= n + 3 < NH:
                        maxima(n + 3)
                    if 0 <= n < NH:
                        if turned_out(n) is not None:
                            outputs_lo(turned_out(n))
                        low_part(n)
                    if n >= G and n % G == 2:
                        outputs(n // G - 1)
                outputs_lo(GROUPS - 2)
                outputs(GROUPS - 1)
                outputs_lo(GROUPS - 1)
                dve.wait_ge(s.x_kept, at(i, 1, 1))
                dve.wait_ge(y_ps, at(i, GROUPS, GROUPS))
                for st in range(ST):
                    last = dve.scalar_tensor_tensor(s.z[:, st, :], ps[:, YB, st * D:(st + 1) * D], 1.0 / WSCALE, s.xr[:, st, :],
                                                    ALU.mult, ALU.add)
                last.then_inc(s.z_made, 1)

            s.each_sequence(dve, sequence)
    s.close()


def routed_stage(k, x_in, x_out, router, w1, b1, w2, b2):
    nc, ps, ident = k.nc, k.ps, k.ident
    E, CAP, K = router.shape[1], 64, 2
    F = w1.shape[1]
    FC = F // P
    NT = B * ST
    s = Stage(k, "route", x_in, x_out)
    rw, w1_s, w2_s = s.sb("rw", [P, DC, E]), s.sb("w1", [P, DC, F]), s.sb("w2", [P, FC, D])
    b1_s, b2_s = s.sb("b1", [P, FC]), s.sb("b2", [P, D])
    hT = s.sb("hT", [P, FC, S])
    y = s.sb("y", [P, ST, D])
    lg = s.sb("lg", [P, ST, E])
    lgs = s.sb("lgs", [P, NT, E])
    pref = s.sb("pref", [P, E])
    prefi = s.sb("prefi", [P, E], I32)
    upto, ones = s.sb("upto", [P, P]), s.sb("ones", [P, P])
    reset = s.sb("reset", [P, E, K * NT])
    pick = s.sb("pick", [P, K, NT, E])
    rank = s.sb("rank", [P, K * NT, E])
    total, before = s.sb("total", [P, E, K * NT]), s.sb("before", [P, E, K * NT])
    tmp, pw = s.sb("tmp", [P, NT, E]), s.sb("pw", [P, NT, E])
    m1, m2, den, w = s.sb("m1", [P, NT]), s.sb("m2", [P, NT]), s.sb("den", [P, NT]), s.sb("w", [P, NT])
    x_all, y_all, z_all = (s.sb(n, [P, NT, D]) for n in ("x_all", "y_all", "z_all"))
    bn, mv = s.sb("bn_all", [P, NT, 6]), s.sb("mv_all", [P, NT, 2])
    ve, nmean, rstd, shift = (s.sb(n, [P, NT]) for n in ("ve_all", "nmean", "rstd_all", "shift"))
    GN = 4
    (w_loaded, const_ready, h_ps, hT_ready, y_ps, y_ready, y_stored, lg_ps, lg_ready, lg_moved, ch, ex, rank_ps,
     w_ready, x_all_loaded, ve_ready, rstds_ready, rows_ready, rows_stored, pool_ch) = (s.sem(n) for n in (
        "w_loaded", "const_ready", "h_ps", "hT_ready", "y_ps", "y_ready", "y_stored", "lg_ps", "lg_ready",
        "lg_moved", "ch", "ex", "rank_ps", "w_ready", "x_all_loaded", "ve_ready", "rstds_ready", "rows_ready", "rows_stored", "pool_ch"))
    XB, YB, LB = 5, 6, 7

    with nc.Block() as block:
        @block.sync
        def _(sp):
            sp.dma_start(rw[:], router.rearrange("(c p) n -> p c n", p=P)).then_inc(w_loaded, 16)
            sp.dma_start(w1_s[:], w1.rearrange("(c p) n -> p c n", p=P)).then_inc(w_loaded, 16)
            sp.dma_start(w2_s[:], w2.rearrange("(c p) n -> p c n", p=P)).then_inc(w_loaded, 16)
            sp.dma_start(b1_s[:], b1).then_inc(w_loaded, 16)
            sp.dma_start(b2_s[:], b2.partition_broadcast(P)).then_inc(w_loaded, 16)

            def keep(i):
                sp.wait_ge(lg_ready, at(i, 1, 1))
                s.carry(sp)
                sp.dma_start(lgs[:, bass.ds(i * ST, ST), :], lg[:]).then_inc(lg_moved, 16)
                sp.wait_ge(y_ready, at(i, 1, 1))
                s.carry(sp)
                sp.dma_start(y_all[:, bass.ds(i * ST, ST), :], y[:]).then_inc(y_stored, 16)

            s.load_x(sp, 0, False)
            sp.dma_start(x_all[:], x_in.rearrange("(t p) d -> p t d", p=P)).then_inc(x_all_loaded, 16)
            with sp.Fori(0, B - 1) as i:
                s.load_x(sp, i + 1, False)
                keep(i)
            keep(B - 1)
            sp.wait_ge(y_stored, 16 * (B + 1))
            sp.wait_ge(x_all_loaded, 16)

        @block.gpsimd
        def _(pool):
            own = Chain(pool, s.pool_own)
            pool.memset(ones[:], 1.0)
            pool.memset(upto[:], 1.0)
            pool.memset(reset[:], 1.0)
            own(pool.iota(prefi[:], [[-1, E]], base=E, channel_multiplier=0))
            pool.affine_select(out=upto[:], in_=upto[:], compare_op=ALU.is_ge, fill=0.0, base=0, pattern=[[1, P]],
                               channel_multiplier=-1)
            own(pool.memset(reset[:, :, 0:1], 0.0))
            pool.sem_inc(const_ready, 1)

        @block.tensor
        def _(pe):
            pe.wait_ge(w_loaded, 16 * 5)
            pe.wait_ge(const_ready, 1)
            with pe.Fori(0, B) as i:
                s.transpose_x(pe, i, ps[:, XB, :])
                pe.wait_ge(s.z_made, at(i, 1, 1))
                pe.wait_ge(s.xT_ready, at(i, 1, 1))
                for st in range(ST):
                    for dc in range(DC):
                        last = pe.matmul(ps[:, LB, st * E:(st + 1) * E], s.xT[:, dc, st * P:(st + 1) * P],
                                         rw[:, dc, :], start=dc == 0, stop=dc == DC - 1)
                last.then_inc(lg_ps, 1)
                for f in range(FC):
                    if f >= 4:
                        pe.wait_ge(hT_ready, at(i, FC, f - 3))
                    for dc in range(DC):
                        last = pe.matmul(ps[:, f % 4, 0:S], w1_s[:, dc, f * P:(f + 1) * P], s.xT[:, dc, :],
                                         start=dc == 0, stop=dc == DC - 1)
                    last.then_inc(h_ps, 1)
                for st in range(ST):
                    for f in range(FC):
                        if st == 0:
                            pe.wait_ge(hT_ready, at(i, FC, f + 1))
                        last = pe.matmul(ps[:, YB, st * D:(st + 1) * D], hT[:, f, st * P:(st + 1) * P], w2_s[:, f, :],
                                         start=f == 0, stop=f == FC - 1)
                last.then_inc(y_ps, 1)

        @block.scalar
        def _(act):
            act.wait_ge(w_loaded, 16 * 5)
            with act.Fori(0, B) as i:
                s.copy_xT(act, i, ps[:, XB, :])
                for f in range(FC):
                    act.wait_ge(h_ps, at(i, FC, f + 1))
                    act.activation(hT[:, f, :], ps[:, f % 4, 0:S], ACT.Gelu, bias=b1_s[:, f:f + 1]).then_inc(hT_ready, 1)

        @block.vector
        def _(dve):
            dve.sem_inc(s.z_made, 1)
            dve.sem_inc(lg_moved, 16)
            dve.sem_inc(y_stored, 16)
            dve.wait_ge(w_loaded, 16 * 5)
            dve.wait_ge(const_ready, 1)
            dve.tensor_copy(pref[:], prefi[:])
            with dve.Fori(0, B) as i:
                dve.wait_ge(lg_ps, at(i, 1, 1))
                dve.wait_ge(lg_moved, at(i, 16, 16))
                dve.tensor_copy(lg[:].rearrange("p s e -> p (s e)"), ps[:, LB, 0:ST * E]).then_inc(lg_ready, 1)
                dve.wait_ge(y_ps, at(i, 1, 1))
                dve.wait_ge(y_stored, at(i, 16, 16))
                dve.tensor_tensor(y[:], ps[:, YB, :].rearrange("p (s d) -> p s d", s=ST),
                                  b2_s[:].unsqueeze(1).to_broadcast([P, ST, D]), ALU.add).then_inc(y_ready, 1)
                dve.wait_ge(y_ready, at(i, 1, 1))
                dve.sem_inc(s.z_made, 1)

    all_e = lambda t_: t_[:].unsqueeze(2).to_broadcast([P, NT, E])
    with nc.Block() as block:
        @block.tensor
        def _(pe):
            pe.wait_ge(w_ready, 1)
            picks = pick[:].rearrange("p k t e -> p (k t e)")
            pe.matmul(ps[:, 0, 0:K * NT * E], upto[:], picks, start=True, stop=True)
            pe.matmul(ps[:, 1, 0:K * NT * E], ones[:], picks, start=True, stop=True).then_inc(rank_ps, 1)

        @block.scalar
        def _(act):
            act.wait_ge(ex, 1)
            act.activation(lgs[:], lgs[:], ACT.Exp).then_inc(ex, 1)
            for t in range(0, NT, GN):
                act.wait_ge(rstds_ready, t // GN + 1)
                for n in range(t, t + GN):
                    last = act.activation(x_all[:, n, :], z_all[:, n, :], ACT.Identity, scale=rstd[:, n:n + 1],
                                          bias=shift[:, n:n + 1])
                last.then_inc(rows_ready, 1)

        @block.gpsimd
        def _(pool):
            own = Chain(pool, pool_ch)
            for t in range(0, NT, GN):
                g = slice(t, t + GN)
                pool.wait_ge(ve_ready, t // GN + 1)
                own(pool.tensor_tensor(rstd[:, g], ve[:, g], k.neg_half[:, 0:GN], ALU.pow))
                pool.tensor_tensor(shift[:, g], nmean[:, g], rstd[:, g], ALU.mult).then_inc(rstds_ready, 1)

        @block.sync
        def _(sp):
            out = x_out.rearrange("(t p) d -> p t d", p=P)
            for t in range(0, NT, GN):
                sp.wait_ge(rows_ready, t // GN + 1)
                sp.dma_start(out[:, t:t + GN, :], x_all[:, t:t + GN, :]).then_inc(rows_stored, 16)
            sp.wait_ge(rows_stored, 16 * (NT // GN))

        @block.vector
        def _(dve):
            own = Chain(dve, ch)
            own(dve.tensor_reduce(m1[:], lgs[:], AX_X, ALU.max))
            own(dve.tensor_tensor(lgs[:], lgs[:], all_e(m1), ALU.subtract))
            dve.sem_inc(ex, 1)
            dve.wait_ge(ex, 2)
            own(dve.tensor_reduce(den[:], lgs[:], AX_X, ALU.add))
            own(dve.reciprocal(den[:], den[:]))
            own(dve.tensor_tensor(lgs[:], lgs[:], all_e(den), ALU.mult))
            own(dve.tensor_copy(pw[:], lgs[:]))
            for c in range(K):
                own(dve.tensor_reduce(m1[:], pw[:], AX_X, ALU.max))
                own(dve.tensor_tensor(tmp[:], pw[:], all_e(m1), ALU.is_equal))
                own(dve.tensor_tensor(tmp[:], tmp[:], pref[:].unsqueeze(1).to_broadcast([P, NT, E]), ALU.mult))
                own(dve.tensor_reduce(m2[:], tmp[:], AX_X, ALU.max))
                own(dve.tensor_tensor(pick[:, c], tmp[:], all_e(m2), ALU.is_equal))
                own(dve.scalar_tensor_tensor(pw[:], pick[:, c], -4.0, pw[:], ALU.mult, ALU.add))
            dve.sem_inc(w_ready, 1)
            dve.wait_ge(rank_ps, 1)
            own(dve.tensor_copy(total[:], ps[:, 1, 0:K * NT * E].rearrange("p (t e) -> p e t", e=E)))
            own(dve.tensor_tensor_scan(before[:].rearrange("p e t -> p (e t)"), reset[:].rearrange("p e t -> p (e t)"),
                                       total[:].rearrange("p e t -> p (e t)"), 0.0, ALU.mult, ALU.add))
            own(dve.tensor_tensor(before[:], before[:], total[:], ALU.subtract))
            own(dve.tensor_tensor(rank[:], ps[:, 0, 0:K * NT * E].rearrange("p (t e) -> p t e", e=E),
                                  before[:].rearrange("p e t -> p t e"), ALU.add))
            own(dve.scalar_tensor_tensor(rank[:].rearrange("p t e -> p (t e)"), rank[:].rearrange("p t e -> p (t e)"),
                                         CAP + 0.5, pick[:].rearrange("p k t e -> p (k t e)"), ALU.is_lt, ALU.mult))
            kept = rank[:].rearrange("p (k t) e -> p k t e", k=K)
            own(dve.tensor_tensor(tmp[:], kept[:, 0], kept[:, 1], ALU.add))
            own(dve.tensor_tensor(tmp[:], tmp[:], lgs[:], ALU.mult))
            own(dve.tensor_reduce(w[:], tmp[:], AX_X, ALU.add))
            for t in range(0, NT, GN):
                tiles, g = range(t, t + GN), slice(t, t + GN)
                for n in tiles:
                    last = dve.scalar_tensor_tensor(z_all[:, n, :], y_all[:, n, :], w[:, n:n + 1], x_all[:, n, :],
                                                    ALU.mult, ALU.add)
                own(last)
                for n in tiles:
                    last = dve.bn_stats(bn[:, n, :], z_all[:, n, :])
                own(last)
                for n in tiles:
                    last = dve.bn_aggr(mv[:, n, :], bn[:, n, :])
                own(last)
                dve.tensor_scalar(nmean[:, g], mv[:, g, 0], -1.0, None, ALU.mult)
                dve.tensor_scalar(ve[:, g], mv[:, g, 1], LN_EPS, None, ALU.add).then_inc(ve_ready, 1)
    s.close()


class Kernel:

    def __init__(self, nc, ctx):
        self.nc = nc
        self.ps = ctx.enter_context(nc.psum_tensor("ps", [P, 8, BANK], F32))
        self.ident = ctx.enter_context(nc.sbuf_tensor("ident", [P, P], F32))
        self.neg_half = ctx.enter_context(nc.sbuf_tensor("neg_half", [P, 64], F32))
        const = ctx.enter_context(nc.semaphore("common_consts"))
        with nc.Block() as block:
            @block.gpsimd
            def _(pool):
                own = Chain(pool, const)
                pool.memset(self.neg_half[:], -0.5)
                own(pool.memset(self.ident[:], 0.0))
                own(pool.affine_select(out=self.ident[:], in_=self.ident[:], compare_op=ALU.not_equal, fill=1.0,
                                       base=0, pattern=[[-1, P]], channel_multiplier=1))


STAGES = [
    (gla_stage, ["gla_wq", "gla_wk", "gla_wv", "gla_wo", "gla_nw"]),
    (cross_stage, ["ctxT", "mask", "x_wq", "x_bq", "x_wk", "x_bk", "x_wv", "x_bv", "x_wo", "x_qn", "x_kn"]),
    (experts_stage, ["e_gate", "e_gu", "e_dn", "e_merge", "e_dom"]),
    (rotary_stage, ["r_wq", "r_bq", "r_wk", "r_bk", "r_wv", "r_bv", "r_wo", "r_bo", "r_kw", "r_cos", "r_sin"]),
    (memory_stage, ["ctxT", "ctx", "kept"]),
    (routed_stage, ["m_router", "m_w1", "m_b1", "m_w2", "m_b2"]),
]


def layout(**a):
    c = np.ascontiguousarray
    T = lambda w: c(np.asarray(w).T)

    inv = (1.0 / np.power(np.float32(10000.0), np.arange(0, 64, 2, dtype=np.float32) / np.float32(64))).astype(np.float32)
    angle = (np.arange(S, dtype=np.float32)[:, None] * inv[None, :]).astype(np.float32)
    return {
        "x": c(a["x"]).reshape(B * S, D),
        "gla_wq": T(a["L0_attn_Wq"]), "gla_wk": T(a["L0_attn_Wk"]), "gla_wv": T(a["L0_attn_Wv"]),
        "gla_wo": T(a["L0_attn_Wo"]), "gla_nw": c(np.asarray(a["L0_attn_norm_w"]).reshape(2, P).T),
        "ctx": c(a["ctx_2048"]), "ctxT": c(np.asarray(a["ctx_2048"]).transpose(0, 2, 1)),
        "mask": c(a["mask_1xSxS2_ff0"])[0],
        "x_wq": c(a["L0_xattn_Wq"]), "x_bq": c(a["L0_xattn_bq"]), "x_wk": c(a["L0_xattn_Wk"]),
        "x_bk": c(a["L0_xattn_bk"]), "x_wv": c(a["L0_xattn_Wv"]), "x_bv": c(np.asarray(a["L0_xattn_bv"]).reshape(-1, P).T),
        "x_wo": c(a["L0_xattn_Wo"]), "x_qn": c(a["L0_xattn_qn_w"]).reshape(P, 1),
        "x_kn": c(a["L0_xattn_kn_w"]).reshape(P, 1),
        "e_gate": T(a["L0_ffn_gate_weight"]), "e_gu": c(np.asarray(a["L0_ffn_gate_up_proj"]).transpose(0, 2, 1)),
        "e_dn": c(np.asarray(a["L0_ffn_down_proj"]).transpose(0, 2, 1)),
        "e_merge": c(a["L0_ffn_merge_groups"]).reshape(-1, 1), "e_dom": c(a["L0_ffn_dominant_experts"]).reshape(1, -1),
        "r_wq": T(a["L1_attn_Wq"]), "r_bq": c(a["L1_attn_bq"]), "r_wk": T(a["L1_attn_Wk"]),
        "r_bk": c(a["L1_attn_bk"]), "r_wv": T(a["L1_attn_Wv"]), "r_bv": c(a["L1_attn_bv"]),
        "r_wo": T(a["L1_attn_Wo"]), "r_bo": c(a["L1_attn_bo"]), "r_kw": c(a["L1_attn_key_weights"]),
        "r_cos": np.cos(angle), "r_sin": np.sin(angle),
        "m_router": T(a["L1_ffn_router_w"]), "m_w1": T(a["L1_ffn_w1"]),
        "m_b1": c(np.asarray(a["L1_ffn_b1"]).reshape(-1, P).T), "m_w2": T(a["L1_ffn_w2"]), "m_b2": c(a["L1_ffn_b2"]),
        "kept": c(a["mask_BxS2_bk0"]),
    }


_OUT = "out"


def build(nc, ap):
    with ExitStack() as ctx:
        k = Kernel(nc, ctx)
        rows = ap["x"]
        for n, (stage, names) in enumerate(STAGES):
            after = ap[_OUT] if n == len(STAGES) - 1 else \
                nc.dram_tensor(f"rows_{n + 1}", [B * S, D], F32, kind="Internal").ap()
            stage(k, rows, after, *[ap[name] for name in names])
            rows = after


def kernel(**inputs):
    import concourse.bacc as bacc
    from concourse.bass_utils import run_bass_kernel_spmd

    nc = bacc.Bacc("TRN2", target_bir_lowering=False, num_devices=1)
    arrays = layout(**inputs)
    ap = {name: nc.dram_tensor(name, a.shape, mybir.dt.from_np(a.dtype), kind="ExternalInput").ap()
          for name, a in arrays.items()}
    ap[_OUT] = nc.dram_tensor(_OUT, [B * S, D], F32, kind="ExternalOutput").ap()
    build(nc, ap)
    result = run_bass_kernel_spmd(nc, [arrays], core_ids=[0])
    return result.results[0][_OUT].reshape(B, S, D)
```
